# Optimizing a Trainium2 kernel written in Bass

```python
import numpy as np
import jax
import jax.numpy as jnp

def _softmax(x, axis=-1):
    return jax.nn.softmax(x, axis=axis)

def _gelu(x):
    return jax.nn.gelu(x, approximate=True)

def _silu(x):
    return jax.nn.silu(x)

def _sigmoid(x):
    return jax.nn.sigmoid(x)

def _layernorm(x, axis=-1, eps=1e-05):
    m = jnp.mean(x, axis=axis, keepdims=True)
    v = jnp.var(x, axis=axis, keepdims=True)
    return (x - m) / jnp.sqrt(v + eps)

def _scatter_add(tgt, idx, src, axis=0):
    return tgt.at[idx].add(src)

def _segment_sum(src, seg, n):
    return jax.ops.segment_sum(src, seg, n)
kernel_name = 'mk_perceiver_d4_seqx_r8_ff05bc'

def setup_inputs(seed: int=0):
    np.random.seed(seed)
    _w = jnp.asarray

    def _rec_inputs():
        import jax
        import jax.numpy as jnp
        _rk = jax.random.key(seed)
        x = -0.0005146 + 1 * jax.random.normal(jax.random.fold_in(_rk, 1), (8, 64, 128), jnp.float32)
        _lenS = 64 - jax.random.randint(jax.random.fold_in(_rk, 7), (8,), 0, max(1, 64 // 4) + 1, jnp.int32)
        _lenS2 = 1601 - jax.random.randint(jax.random.fold_in(_rk, 8), (8,), 0, max(1, 1601 // 4) + 1, jnp.int32)
        _ctx_768P = jax.random.normal(jax.random.fold_in(_rk, 11), (8, 16, 96), jnp.float32)
        _ctx_768c = jax.random.dirichlet(jax.random.fold_in(_rk, 511), 0.3 * jnp.ones((16,), jnp.float32), (8, 1601))
        _ctx_768t = jnp.einsum('bsk,bkd->bsd', _ctx_768c, _ctx_768P)
        _ctx_768t = _ctx_768t * jax.lax.rsqrt(jnp.mean(jnp.square(_ctx_768t)) + 1e-12) * 0.953939
        ctx_768 = -0.00040386 + 0.999972 * (_ctx_768t + 0.3 * jax.random.normal(jax.random.fold_in(_rk, 611), (8, 1601, 96), jnp.float32))
        _validS = jnp.arange(64)[None, :] < _lenS[:, None]
        _validS2 = jnp.arange(1601)[None, :] < _lenS2[:, None]
        _causal = jnp.tril(jnp.ones((64, 64), dtype=bool))
        mask_BxS2_bk0 = jnp.logical_not(jnp.broadcast_to(_validS2[:, :], (8, 1601)))
        mask_BxS_bf1 = jnp.ones((8, 64), dtype=bool)
        mask_BxS2_bf1 = jnp.ones((8, 1601), dtype=bool)
        return (x, ctx_768, mask_BxS2_bk0, mask_BxS_bf1, mask_BxS2_bf1)
    x, ctx_768, mask_BxS2_bk0, mask_BxS_bf1, mask_BxS2_bf1 = _rec_inputs()

    def _L0_xattn_setup():
        import jax, jax.numpy as jnp
        import numpy as np
        DIM_IN, DIM_LAT, DIM_HEAD = (96, 128, 64)
        INNER = max(DIM_LAT, DIM_IN)
        HEADS = INNER // DIM_HEAD
        SCALE = DIM_HEAD ** (-0.5)
        RMS_EPS = 1e-08
        LN_EPS = 1e-05

        def layernorm(x, g, b):
            mu = jnp.mean(x, axis=-1, keepdims=True)
            var = jnp.mean((x - mu) ** 2, axis=-1, keepdims=True)
            return (x - mu) * jax.lax.rsqrt(var + LN_EPS) * g + b

        def rmsnorm(x, gamma):
            norm = jnp.sqrt(jnp.sum(x * x, axis=-1, keepdims=True)) * x.shape[-1] ** (-0.5)
            return x / jnp.maximum(norm, RMS_EPS) * gamma
        key = jax.random.key(seed)
        ks = jax.random.split(key, 12)
        b, n, m = (4, 512, 64)
        x = jax.random.normal(ks[0], (b, n, DIM_IN), jnp.float32)
        latents = jax.random.normal(ks[1], (b, m, DIM_LAT), jnp.float32)
        mask = jax.random.randint(ks[2], (b, n), 0, 2).astype(bool)
        s = lambda k, sh, fan: jax.random.normal(k, sh, jnp.float32) * fan ** (-0.5)
        return {'x': x, 'latents': latents, 'mask': mask, 'ln_x_g': jnp.ones((DIM_IN,), jnp.float32), 'ln_x_b': jnp.zeros((DIM_IN,), jnp.float32), 'ln_l_g': jnp.ones((DIM_LAT,), jnp.float32), 'ln_l_b': jnp.zeros((DIM_LAT,), jnp.float32), 'qn_g': jnp.ones((DIM_HEAD,), jnp.float32), 'kn_g': jnp.ones((DIM_HEAD,), jnp.float32), 'Wq': s(ks[3], (INNER, DIM_LAT), DIM_LAT), 'Wkv': s(ks[4], (2 * INNER, DIM_IN), DIM_IN), 'Wlkv': s(ks[5], (2 * INNER, DIM_LAT), DIM_LAT), 'Wo': s(ks[6], (DIM_LAT, INNER), INNER), 'bo': jnp.zeros((DIM_LAT,), jnp.float32)}
    _L0_xattn_all = _L0_xattn_setup()
    _L0_xattn_in = {k: v for k, v in _L0_xattn_all.items() if k in ('ln_x_g', 'ln_x_b', 'ln_l_g', 'ln_l_b', 'qn_g', 'kn_g', 'Wq', 'Wkv', 'Wlkv', 'Wo', 'bo')}
    del _L0_xattn_all

    def _L0_attn_setup():
        import jax, jax.numpy as jnp
        import numpy as np
        H = 128
        I = 512
        TAU = 9
        LN_EPS = 1e-12

        def _l2_normalize(x):
            n = jnp.sqrt(jnp.sum(x * x, axis=-1, keepdims=True))
            return x / jnp.maximum(n, 1e-12)
        key = jax.random.key(seed)
        k1, k2, k3, k4 = jax.random.split(key, 4)
        return {'hidden_states': jax.random.normal(k1, (4, 256, H), jnp.float32), 'ln_weight': jnp.ones((H,), jnp.float32), 'ln_bias': jnp.zeros((H,), jnp.float32), 'k_weight': 0.02 * jax.random.normal(k2, (I, H), jnp.float32), 'q_weight': 0.02 * jax.random.normal(k3, (I, H), jnp.float32), 'bias': 0.001 * jax.random.normal(k4, (H,), jnp.float32)}
    _L0_attn_all = _L0_attn_setup()
    _L0_attn_in = {k: v for k, v in _L0_attn_all.items() if k in ('ln_weight', 'ln_bias', 'k_weight', 'q_weight', 'bias')}
    del _L0_attn_all

    def _L0_ffn_setup():
        import jax, jax.numpy as jnp
        import numpy as np
        QMAX = 127.0

        def _ste_round(v):
            return v + jax.lax.stop_gradient(jnp.round(v) - v)

        def _act_fake_quant(x, clip_factor):
            scale = jax.nn.sigmoid(clip_factor) * jnp.max(jnp.abs(x)) / QMAX
            return jnp.clip(_ste_round(x / scale), -QMAX - 1.0, QMAX) * scale

        def _weight_fake_quant(w):
            scale = jnp.max(jnp.abs(w), axis=1, keepdims=True) / QMAX
            return jnp.clip(_ste_round(w / scale), -QMAX - 1.0, QMAX) * scale
        key = jax.random.key(seed)
        k1, k2, k3, k4 = jax.random.split(key, 4)
        B, S, H, I = (8, 1024, 128, 352)
        return {'x': jax.random.normal(k1, (B, S, H), dtype=jnp.float32), 'clip_x': jnp.full((1,), 4.0, dtype=jnp.float32), 'clip_down': jnp.full((1,), 4.0, dtype=jnp.float32), 'w_gate': jax.random.normal(k2, (I, H), dtype=jnp.float32) * 0.02, 'w_up': jax.random.normal(k3, (I, H), dtype=jnp.float32) * 0.02, 'w_down': jax.random.normal(k4, (H, I), dtype=jnp.float32) * 0.02}
    _L0_ffn_all = _L0_ffn_setup()
    _L0_ffn_in = {k: v for k, v in _L0_ffn_all.items() if k in ('clip_x', 'clip_down', 'w_gate', 'w_up', 'w_down')}
    del _L0_ffn_all

    def _L1_xattn_setup():
        import jax, jax.numpy as jnp
        import numpy as np
        HEADS = 16
        DIM_HEAD = 64
        SCALE = DIM_HEAD ** (-0.5)
        QUERY_DIM = 128
        CONTEXT_DIM = 96
        INNER_DIM = HEADS * DIM_HEAD
        key = jax.random.key(seed)
        ks = jax.random.split(key, 7)
        B, Nq, Nk = (8, 512, 77)
        x = jax.random.normal(ks[0], (B, Nq, QUERY_DIM), dtype=jnp.float32)
        context = jax.random.normal(ks[1], (B, Nk, CONTEXT_DIM), dtype=jnp.float32)
        Wq = jax.random.normal(ks[2], (QUERY_DIM, INNER_DIM), dtype=jnp.float32) * QUERY_DIM ** (-0.5)
        Wk = jax.random.normal(ks[3], (CONTEXT_DIM, INNER_DIM), dtype=jnp.float32) * CONTEXT_DIM ** (-0.5)
        Wv = jax.random.normal(ks[4], (CONTEXT_DIM, INNER_DIM), dtype=jnp.float32) * CONTEXT_DIM ** (-0.5)
        Wo = jax.random.normal(ks[5], (INNER_DIM, QUERY_DIM), dtype=jnp.float32) * INNER_DIM ** (-0.5)
        bo = jnp.zeros((QUERY_DIM,), dtype=jnp.float32)
        return {'x': x, 'context': context, 'Wq': Wq, 'Wk': Wk, 'Wv': Wv, 'Wo': Wo, 'bo': bo}
    _L1_xattn_all = _L1_xattn_setup()
    _L1_xattn_in = {k: v for k, v in _L1_xattn_all.items() if k in ('Wq', 'Wk', 'Wv', 'Wo', 'bo')}
    del _L1_xattn_all

    def _L1_attn_setup():
        import jax, jax.numpy as jnp
        import numpy as np
        B, S, D = (2, 256, 128)
        H, DQ, DV = (16, 64, 64)
        key = jax.random.key(seed)
        k1, k2, k3, k4, k5 = jax.random.split(key, 5)
        scale = 0.02
        return {'x': jax.random.normal(k1, (B, S, D), dtype=jnp.float32), 'w_q': jax.random.normal(k2, (H, DQ, D), dtype=jnp.float32) * scale, 'w_k': jax.random.normal(k3, (H, DQ, D), dtype=jnp.float32) * scale, 'w_v': jax.random.normal(k4, (H, DV, D), dtype=jnp.float32) * scale, 'w_o': jax.random.normal(k5, (D, H * DV), dtype=jnp.float32) * scale}
    _L1_attn_all = _L1_attn_setup()
    _L1_attn_in = {k: v for k, v in _L1_attn_all.items() if k in ('w_q', 'w_k', 'w_v', 'w_o')}
    del _L1_attn_all

    def _L1_ffn_setup():
        import jax, jax.numpy as jnp
        import numpy as np
        NUM_EXPERTS = 8
        HIDDEN = 128
        FFN = 512
        BATCH = 2
        SEQ = 256
        key = jax.random.key(seed)
        k_x, k_g, k_u, k_d = jax.random.split(key, 4)
        scale_in = 1.0 / np.sqrt(HIDDEN)
        scale_mid = 1.0 / np.sqrt(FFN)
        return {'hidden_states': jax.random.normal(k_x, (BATCH, SEQ, HIDDEN), dtype=jnp.float32), 'Wg': jax.random.normal(k_g, (NUM_EXPERTS, HIDDEN, FFN), dtype=jnp.float32) * scale_in, 'Wu': jax.random.normal(k_u, (NUM_EXPERTS, HIDDEN, FFN), dtype=jnp.float32) * scale_in, 'Wd': jax.random.normal(k_d, (NUM_EXPERTS, FFN, HIDDEN), dtype=jnp.float32) * scale_mid}
    _L1_ffn_all = _L1_ffn_setup()
    _L1_ffn_in = {k: v for k, v in _L1_ffn_all.items() if k in ('Wg', 'Wu', 'Wd')}
    del _L1_ffn_all

    def _L2_xattn_setup():
        import jax, jax.numpy as jnp
        import numpy as np
        N_HEADS = 16
        D_HEAD = 64
        key = jax.random.key(seed)
        ks = jax.random.split(key, 7)
        B, SQ, SKV = (2, 256, 256)
        D_MODEL, D_COND, D_ATTN = (128, 96, N_HEADS * D_HEAD)
        return {'x': jax.random.normal(ks[0], (B, SQ, D_MODEL), jnp.float32), 'cond': jax.random.normal(ks[1], (B, SKV, D_COND), jnp.float32), 'w_q': jax.random.normal(ks[2], (D_MODEL, D_ATTN), jnp.float32) * D_MODEL ** (-0.5), 'w_k': jax.random.normal(ks[3], (D_COND, D_ATTN), jnp.float32) * D_COND ** (-0.5), 'w_v': jax.random.normal(ks[4], (D_COND, D_ATTN), jnp.float32) * D_COND ** (-0.5), 'w_out': jax.random.normal(ks[5], (D_ATTN, D_MODEL), jnp.float32) * D_ATTN ** (-0.5), 'b_out': jnp.zeros((D_MODEL,), jnp.float32)}
    _L2_xattn_all = _L2_xattn_setup()
    _L2_xattn_in = {k: v for k, v in _L2_xattn_all.items() if k in ('w_q', 'w_k', 'w_v', 'w_out', 'b_out')}
    del _L2_xattn_all

    def _L2_attn_setup():
        import jax, jax.numpy as jnp
        import numpy as np
        B, S, D, H = (2, 256, 128, 16)
        HD = D // H
        key = jax.random.key(seed)
        ks = jax.random.split(key, 5)
        return {'x': jax.random.normal(ks[0], (B, S, D), dtype=jnp.float32), 'qkv_w': jax.random.normal(ks[1], (3 * D, D), dtype=jnp.float32) * (1.0 / np.sqrt(D)), 'qkv_b': jax.random.normal(ks[2], (3 * D,), dtype=jnp.float32) * 0.02, 'proj_w': jax.random.normal(ks[3], (D, D), dtype=jnp.float32) * (1.0 / np.sqrt(D)), 'proj_b': jax.random.normal(ks[4], (D,), dtype=jnp.float32) * 0.02}
    _L2_attn_all = _L2_attn_setup()
    _L2_attn_in = {k: v for k, v in _L2_attn_all.items() if k in ('qkv_w', 'qkv_b', 'proj_w', 'proj_b')}
    del _L2_attn_all

    def _L2_ffn_setup():
        import jax, jax.numpy as jnp
        import numpy as np
        EPS = 1e-08
        key = jax.random.key(seed)
        kx, kw = jax.random.split(key)
        x = jax.random.normal(kx, (8, 512, 128), dtype=jnp.float32)
        weight = jax.random.normal(kw, (128, 128), dtype=jnp.float32) * (1.0 / np.sqrt(128))
        return {'x': x, 'weight': weight}
    _L2_ffn_all = _L2_ffn_setup()
    _L2_ffn_in = {k: v for k, v in _L2_ffn_all.items() if k in ('weight',)}
    del _L2_ffn_all

    def _L3_xattn_setup():
        import jax, jax.numpy as jnp
        import numpy as np
        B, T, DT, G, DV = (16, 64, 128, 72, 96)
        H, DH = (4, 32)
        INNER = H * DH
        HID = 4 * DT
        N_STATE = 64
        K_TOP = 32

        def layernorm(x, g, b, eps=1e-05):
            m = x.mean(-1, keepdims=True)
            v = x.var(-1, keepdims=True)
            return (x - m) * jax.lax.rsqrt(v + eps) * g + b

        def s4d(x, log_dt, A_re, A_im, C_re, C_im, D_skip):
            Bb, L, D = x.shape
            dt = jnp.exp(log_dt)
            A = A_re + 1j * A_im
            C = C_re + 1j * C_im
            dtA = dt[:, None] * A
            dC = C * (jnp.exp(dtA) - 1.0) / A
            powers = jnp.exp(dtA[:, :, None] * jnp.arange(L))
            K = 2.0 * jnp.einsum('dn,dnl->dl', dC, powers).real
            n = 2 * L
            Kf = jnp.fft.rfft(K, n=n, axis=-1)
            xf = jnp.fft.rfft(x, n=n, axis=1)
            y = jnp.fft.irfft(xf * Kf.T[None], n=n, axis=1)[:, :L]
            return y + x * D_skip
        key = jax.random.key(seed)
        ks = jax.random.split(key, 16)
        s = 0.02
        inp = {'x_text': jax.random.normal(ks[0], (B, T, DT), jnp.float32), 'x_vision': jax.random.normal(ks[1], (B, G, DV), jnp.float32), 'text_mask': jnp.ones((B, T), bool), 'vision_mask': jnp.ones((B, G), bool), 'Wq': jax.random.normal(ks[2], (DT, INNER), jnp.float32) * s, 'Wk': jax.random.normal(ks[3], (DV, INNER), jnp.float32) * s, 'Wv': jax.random.normal(ks[4], (DV, DT), jnp.float32) * s, 'W_film_in': jax.random.normal(ks[5], (DT, 2 * DT), jnp.float32) * s, 'b_film_in': jnp.zeros((2 * DT,), jnp.float32), 'W_film_out': jax.random.normal(ks[6], (DT, 2 * DT), jnp.float32) * s, 'b_film_out': jnp.zeros((2 * DT,), jnp.float32), 'g_norm_in': jnp.ones((DT,), jnp.float32), 'b_norm_in': jnp.zeros((DT,), jnp.float32), 'g_norm_out': jnp.ones((DT,), jnp.float32), 'b_norm_out': jnp.zeros((DT,), jnp.float32), 'g_ffn': jnp.ones((DT,), jnp.float32), 'b_ffn': jnp.zeros((DT,), jnp.float32), 'W1': jax.random.normal(ks[7], (DT, HID), jnp.float32) * s, 'b1': jnp.zeros((HID,), jnp.float32), 'W2': jax.random.normal(ks[8], (HID, DT), jnp.float32) * s, 'b2': jnp.zeros((DT,), jnp.float32), 'log_dt': jnp.log(0.001) + jax.random.uniform(ks[9], (DT,), jnp.float32) * (jnp.log(0.1) - jnp.log(0.001)), 'A_re': -0.5 * jnp.ones((DT, N_STATE), jnp.float32), 'A_im': jnp.tile(jnp.pi * jnp.arange(N_STATE, dtype=jnp.float32), (DT, 1)), 'C_re': jax.random.normal(ks[10], (DT, N_STATE), jnp.float32) * 0.5 ** 0.5, 'C_im': jax.random.normal(ks[11], (DT, N_STATE), jnp.float32) * 0.5 ** 0.5, 'D_skip': jax.random.normal(ks[12], (DT,), jnp.float32), 'mod_gate': jnp.array(0.5, jnp.float32)}
        return inp
    _L3_xattn_all = _L3_xattn_setup()
    _L3_xattn_in = {k: v for k, v in _L3_xattn_all.items() if k in ('Wq', 'Wk', 'Wv', 'W_film_in', 'b_film_in', 'W_film_out', 'b_film_out', 'g_norm_in', 'b_norm_in', 'g_norm_out', 'b_norm_out', 'g_ffn', 'b_ffn', 'W1', 'b1', 'W2', 'b2', 'log_dt', 'A_re', 'A_im', 'C_re', 'C_im', 'D_skip', 'mod_gate')}
    del _L3_xattn_all

    def _L3_attn_setup():
        import jax, jax.numpy as jnp
        import numpy as np
        DIM = 128
        HEADS = 16
        BATCH = 2
        SEQ = 256
        key = jax.random.key(seed)
        ks = jax.random.split(key, 7)
        s = DIM ** (-0.5)
        return {'x': jax.random.normal(ks[0], (BATCH, SEQ, DIM), dtype=jnp.float32), 'Wq': jax.random.normal(ks[1], (DIM, DIM), dtype=jnp.float32) * s, 'Wk': jax.random.normal(ks[2], (DIM, DIM), dtype=jnp.float32) * s, 'Wv': jax.random.normal(ks[3], (DIM, DIM), dtype=jnp.float32) * s, 'Wo': jax.random.normal(ks[4], (DIM, DIM), dtype=jnp.float32) * s, 'compressibility': jnp.ones((HEADS, 1, 1), dtype=jnp.float32) * 0.5, 'phase_threshold': jnp.zeros((HEADS, 1, 1), dtype=jnp.float32)}
    _L3_attn_all = _L3_attn_setup()
    _L3_attn_in = {k: v for k, v in _L3_attn_all.items() if k in ('Wq', 'Wk', 'Wv', 'Wo', 'compressibility', 'phase_threshold')}
    del _L3_attn_all

    def _L3_ffn_setup():
        import jax, jax.numpy as jnp
        import numpy as np
        N_EMBD = 128
        NUM_EXPERTS = 8
        TOP_K = 2
        D_FF = 4 * N_EMBD
        B, S = (4, 256)
        key = jax.random.key(seed)
        ks = jax.random.split(key, 7)
        scale = lambda fan_in: 1.0 / np.sqrt(fan_in)
        x = jax.random.normal(ks[0], (B, S, N_EMBD), dtype=jnp.float32)
        W_router = jax.random.normal(ks[1], (N_EMBD, NUM_EXPERTS), dtype=jnp.float32) * scale(N_EMBD)
        b_router = jnp.zeros((NUM_EXPERTS,), dtype=jnp.float32)
        W1 = jax.random.normal(ks[2], (NUM_EXPERTS, N_EMBD, D_FF), dtype=jnp.float32) * scale(N_EMBD)
        b1 = jnp.zeros((NUM_EXPERTS, D_FF), dtype=jnp.float32)
        W2 = jax.random.normal(ks[3], (NUM_EXPERTS, D_FF, N_EMBD), dtype=jnp.float32) * scale(D_FF)
        b2 = jnpp = jnp.zeros((NUM_EXPERTS, N_EMBD), dtype=jnp.float32)
        return {'x': x, 'W_router': W_router, 'b_router': b_router, 'W1': W1, 'b1': b1, 'W2': W2, 'b2': b2}
    _L3_ffn_all = _L3_ffn_setup()
    _L3_ffn_in = {k: v for k, v in _L3_ffn_all.items() if k in ('W_router', 'b_router', 'W1', 'b1', 'W2', 'b2')}
    del _L3_ffn_all
    return {'x': x, 'ctx_768': ctx_768, 'mask_BxS2_bk0': mask_BxS2_bk0, 'mask_BxS_bf1': mask_BxS_bf1, 'mask_BxS2_bf1': mask_BxS2_bf1, 'L0_xattn_ln_x_g': _L0_xattn_in['ln_x_g'], 'L0_xattn_ln_x_b': _L0_xattn_in['ln_x_b'], 'L0_xattn_ln_l_g': _L0_xattn_in['ln_l_g'], 'L0_xattn_ln_l_b': _L0_xattn_in['ln_l_b'], 'L0_xattn_qn_g': _L0_xattn_in['qn_g'], 'L0_xattn_kn_g': _L0_xattn_in['kn_g'], 'L0_xattn_Wq': _L0_xattn_in['Wq'], 'L0_xattn_Wkv': _L0_xattn_in['Wkv'], 'L0_xattn_Wlkv': _L0_xattn_in['Wlkv'], 'L0_xattn_Wo': _L0_xattn_in['Wo'], 'L0_xattn_bo': _L0_xattn_in['bo'], 'L0_attn_ln_weight': _L0_attn_in['ln_weight'], 'L0_attn_ln_bias': _L0_attn_in['ln_bias'], 'L0_attn_k_weight': _L0_attn_in['k_weight'], 'L0_attn_q_weight': _L0_attn_in['q_weight'], 'L0_attn_bias': _L0_attn_in['bias'], 'L0_ffn_clip_x': _L0_ffn_in['clip_x'], 'L0_ffn_clip_down': _L0_ffn_in['clip_down'], 'L0_ffn_w_gate': _L0_ffn_in['w_gate'], 'L0_ffn_w_up': _L0_ffn_in['w_up'], 'L0_ffn_w_down': _L0_ffn_in['w_down'], 'L1_xattn_Wq': _L1_xattn_in['Wq'], 'L1_xattn_Wk': _L1_xattn_in['Wk'], 'L1_xattn_Wv': _L1_xattn_in['Wv'], 'L1_xattn_Wo': _L1_xattn_in['Wo'], 'L1_xattn_bo': _L1_xattn_in['bo'], 'L1_attn_w_q': _L1_attn_in['w_q'], 'L1_attn_w_k': _L1_attn_in['w_k'], 'L1_attn_w_v': _L1_attn_in['w_v'], 'L1_attn_w_o': _L1_attn_in['w_o'], 'L1_ffn_Wg': _L1_ffn_in['Wg'], 'L1_ffn_Wu': _L1_ffn_in['Wu'], 'L1_ffn_Wd': _L1_ffn_in['Wd'], 'L2_xattn_w_q': _L2_xattn_in['w_q'], 'L2_xattn_w_k': _L2_xattn_in['w_k'], 'L2_xattn_w_v': _L2_xattn_in['w_v'], 'L2_xattn_w_out': _L2_xattn_in['w_out'], 'L2_xattn_b_out': _L2_xattn_in['b_out'], 'L2_attn_qkv_w': _L2_attn_in['qkv_w'], 'L2_attn_qkv_b': _L2_attn_in['qkv_b'], 'L2_attn_proj_w': _L2_attn_in['proj_w'], 'L2_attn_proj_b': _L2_attn_in['proj_b'], 'L2_ffn_weight': _L2_ffn_in['weight'], 'L3_xattn_Wq': _L3_xattn_in['Wq'], 'L3_xattn_Wk': _L3_xattn_in['Wk'], 'L3_xattn_Wv': _L3_xattn_in['Wv'], 'L3_xattn_W_film_in': _L3_xattn_in['W_film_in'], 'L3_xattn_b_film_in': _L3_xattn_in['b_film_in'], 'L3_xattn_W_film_out': _L3_xattn_in['W_film_out'], 'L3_xattn_b_film_out': _L3_xattn_in['b_film_out'], 'L3_xattn_g_norm_in': _L3_xattn_in['g_norm_in'], 'L3_xattn_b_norm_in': _L3_xattn_in['b_norm_in'], 'L3_xattn_g_norm_out': _L3_xattn_in['g_norm_out'], 'L3_xattn_b_norm_out': _L3_xattn_in['b_norm_out'], 'L3_xattn_g_ffn': _L3_xattn_in['g_ffn'], 'L3_xattn_b_ffn': _L3_xattn_in['b_ffn'], 'L3_xattn_W1': _L3_xattn_in['W1'], 'L3_xattn_b1': _L3_xattn_in['b1'], 'L3_xattn_W2': _L3_xattn_in['W2'], 'L3_xattn_b2': _L3_xattn_in['b2'], 'L3_xattn_log_dt': _L3_xattn_in['log_dt'], 'L3_xattn_A_re': _L3_xattn_in['A_re'], 'L3_xattn_A_im': _L3_xattn_in['A_im'], 'L3_xattn_C_re': _L3_xattn_in['C_re'], 'L3_xattn_C_im': _L3_xattn_in['C_im'], 'L3_xattn_D_skip': _L3_xattn_in['D_skip'], 'L3_xattn_mod_gate': _L3_xattn_in['mod_gate'], 'L3_attn_Wq': _L3_attn_in['Wq'], 'L3_attn_Wk': _L3_attn_in['Wk'], 'L3_attn_Wv': _L3_attn_in['Wv'], 'L3_attn_Wo': _L3_attn_in['Wo'], 'L3_attn_compressibility': _L3_attn_in['compressibility'], 'L3_attn_phase_threshold': _L3_attn_in['phase_threshold'], 'L3_ffn_W_router': _L3_ffn_in['W_router'], 'L3_ffn_b_router': _L3_ffn_in['b_router'], 'L3_ffn_W1': _L3_ffn_in['W1'], 'L3_ffn_b1': _L3_ffn_in['b1'], 'L3_ffn_W2': _L3_ffn_in['W2'], 'L3_ffn_b2': _L3_ffn_in['b2']}

def reference(x, ctx_768, mask_BxS2_bk0, mask_BxS_bf1, mask_BxS2_bf1, L0_xattn_ln_x_g, L0_xattn_ln_x_b, L0_xattn_ln_l_g, L0_xattn_ln_l_b, L0_xattn_qn_g, L0_xattn_kn_g, L0_xattn_Wq, L0_xattn_Wkv, L0_xattn_Wlkv, L0_xattn_Wo, L0_xattn_bo, L0_attn_ln_weight, L0_attn_ln_bias, L0_attn_k_weight, L0_attn_q_weight, L0_attn_bias, L0_ffn_clip_x, L0_ffn_clip_down, L0_ffn_w_gate, L0_ffn_w_up, L0_ffn_w_down, L1_xattn_Wq, L1_xattn_Wk, L1_xattn_Wv, L1_xattn_Wo, L1_xattn_bo, L1_attn_w_q, L1_attn_w_k, L1_attn_w_v, L1_attn_w_o, L1_ffn_Wg, L1_ffn_Wu, L1_ffn_Wd, L2_xattn_w_q, L2_xattn_w_k, L2_xattn_w_v, L2_xattn_w_out, L2_xattn_b_out, L2_attn_qkv_w, L2_attn_qkv_b, L2_attn_proj_w, L2_attn_proj_b, L2_ffn_weight, L3_xattn_Wq, L3_xattn_Wk, L3_xattn_Wv, L3_xattn_W_film_in, L3_xattn_b_film_in, L3_xattn_W_film_out, L3_xattn_b_film_out, L3_xattn_g_norm_in, L3_xattn_b_norm_in, L3_xattn_g_norm_out, L3_xattn_b_norm_out, L3_xattn_g_ffn, L3_xattn_b_ffn, L3_xattn_W1, L3_xattn_b1, L3_xattn_W2, L3_xattn_b2, L3_xattn_log_dt, L3_xattn_A_re, L3_xattn_A_im, L3_xattn_C_re, L3_xattn_C_im, L3_xattn_D_skip, L3_xattn_mod_gate, L3_attn_Wq, L3_attn_Wk, L3_attn_Wv, L3_attn_Wo, L3_attn_compressibility, L3_attn_phase_threshold, L3_ffn_W_router, L3_ffn_b_router, L3_ffn_W1, L3_ffn_b1, L3_ffn_W2, L3_ffn_b2):
    import jax
    import jax.numpy as jnp

    def _L0_xattn_ref(x, latents, mask, ln_x_g, ln_x_b, ln_l_g, ln_l_b, qn_g, kn_g, Wq, Wkv, Wlkv, Wo, bo):
        import jax, jax.numpy as jnp
        import numpy as np
        DIM_IN, DIM_LAT, DIM_HEAD = (96, 128, 64)
        INNER = max(DIM_LAT, DIM_IN)
        HEADS = INNER // DIM_HEAD
        SCALE = DIM_HEAD ** (-0.5)
        RMS_EPS = 1e-08
        LN_EPS = 1e-05

        def layernorm(x, g, b):
            mu = jnp.mean(x, axis=-1, keepdims=True)
            var = jnp.mean((x - mu) ** 2, axis=-1, keepdims=True)
            return (x - mu) * jax.lax.rsqrt(var + LN_EPS) * g + b

        def rmsnorm(x, gamma):
            norm = jnp.sqrt(jnp.sum(x * x, axis=-1, keepdims=True)) * x.shape[-1] ** (-0.5)
            return x / jnp.maximum(norm, RMS_EPS) * gamma
        b, n, _ = x.shape
        m = latents.shape[1]
        xn = layernorm(x, ln_x_g, ln_x_b)
        ln = layernorm(latents, ln_l_g, ln_l_b)
        q = ln @ Wq.T
        kv = jnp.concatenate([xn @ Wkv.T, ln @ Wlkv.T], axis=1)
        k, v = (kv[..., :INNER], kv[..., INNER:])
        split_heads = lambda t: t.reshape(t.shape[0], t.shape[1], HEADS, DIM_HEAD).transpose(0, 2, 1, 3)
        q, k, v = (split_heads(q), split_heads(k), split_heads(v))
        qn = rmsnorm(q, qn_g) * SCALE
        kn = rmsnorm(k, kn_g)
        attn = jnp.einsum('bhid,bhjd->bhij', qn, kn)
        full_mask = jnp.pad(mask, ((0, 0), (0, m)), constant_values=True)
        attn = jnp.where(full_mask[:, None, None, :], attn, -jnp.finfo(attn.dtype).max)
        attn = jax.nn.softmax(attn, axis=-1)
        out = jnp.einsum('bhij,bhjd->bhid', attn, v)
        out = out.transpose(0, 2, 1, 3).reshape(b, m, INNER)
        return out @ Wo.T + bo

    def _L0_attn_ref(hidden_states, ln_weight, ln_bias, k_weight, q_weight, bias):
        import jax, jax.numpy as jnp
        import numpy as np
        H = 128
        I = 512
        TAU = 9
        LN_EPS = 1e-12

        def _l2_normalize(x):
            n = jnp.sqrt(jnp.sum(x * x, axis=-1, keepdims=True))
            return x / jnp.maximum(n, 1e-12)
        lead_shape = hidden_states.shape[:-1]
        x = hidden_states.reshape(-1, H)
        mu = jnp.mean(x, axis=-1, keepdims=True)
        var = jnp.mean(jnp.square(x - mu), axis=-1, keepdims=True)
        x = (x - mu) * jax.lax.rsqrt(var + LN_EPS) * ln_weight + ln_bias
        Q = _l2_normalize(x)
        K = _l2_normalize(k_weight)
        s = jnp.clip(jnp.einsum('nh,ih->ni', Q, K), -1.0 + 1e-06, 1.0 - 1e-06)
        B = jnp.power(1.0 - jnp.arccos(s) / jnp.pi, TAU)
        X = jnp.einsum('ni,ih->nh', B, q_weight)
        X = _l2_normalize(X) + bias
        return X.reshape(*lead_shape, H)

    def _L0_ffn_ref(x, clip_x, clip_down, w_gate, w_up, w_down):
        import jax, jax.numpy as jnp
        import numpy as np
        QMAX = 127.0

        def _ste_round(v):
            return v + jax.lax.stop_gradient(jnp.round(v) - v)

        def _act_fake_quant(x, clip_factor):
            scale = jax.nn.sigmoid(clip_factor) * jnp.max(jnp.abs(x)) / QMAX
            return jnp.clip(_ste_round(x / scale), -QMAX - 1.0, QMAX) * scale

        def _weight_fake_quant(w):
            scale = jnp.max(jnp.abs(w), axis=1, keepdims=True) / QMAX
            return jnp.clip(_ste_round(w / scale), -QMAX - 1.0, QMAX) * scale
        xq = _act_fake_quant(x, clip_x[0])
        gate = jnp.einsum('bsh,ih->bsi', xq, _weight_fake_quant(w_gate))
        up = jnp.einsum('bsh,ih->bsi', xq, _weight_fake_quant(w_up))
        h = _act_fake_quant(jax.nn.silu(gate) * up, clip_down[0])
        return jnp.einsum('bsi,hi->bsh', h, _weight_fake_quant(w_down))

    def _L1_xattn_ref(x, context, Wq, Wk, Wv, Wo, bo):
        import jax, jax.numpy as jnp
        import numpy as np
        HEADS = 16
        DIM_HEAD = 64
        SCALE = DIM_HEAD ** (-0.5)
        QUERY_DIM = 128
        CONTEXT_DIM = 96
        INNER_DIM = HEADS * DIM_HEAD
        B, Nq, _ = x.shape
        Nk = context.shape[1]
        q = x @ Wq
        k = context @ Wk
        v = context @ Wv
        q = q.reshape(B, Nq, HEADS, DIM_HEAD).transpose(0, 2, 1, 3)
        k = k.reshape(B, Nk, HEADS, DIM_HEAD).transpose(0, 2, 1, 3)
        v = v.reshape(B, Nk, HEADS, DIM_HEAD).transpose(0, 2, 1, 3)
        sim = jnp.einsum('bhid,bhjd->bhij', q, k) * SCALE
        attn = jax.nn.softmax(sim, axis=-1)
        out = jnp.einsum('bhij,bhjd->bhid', attn, v)
        out = out.transpose(0, 2, 1, 3).reshape(B, Nq, INNER_DIM)
        return out @ Wo + bo

    def _L1_attn_ref(x, w_q, w_k, w_v, w_o):
        import jax, jax.numpy as jnp
        import numpy as np
        B, S, D = (2, 256, 128)
        H, DQ, DV = (16, 64, 64)
        b, s, d = x.shape
        q = jnp.einsum('bsd,hqd->bhsq', x, w_q)
        k = jnp.einsum('bsd,hqd->bhsq', x, w_k)
        v = jnp.einsum('bsd,hvd->bhsv', x, w_v)
        scores = jnp.einsum('bhsq,bhtq->bhst', q, k)
        causal = jnp.triu(jnp.ones((s, s), dtype=bool), k=1)
        masked = jnp.where(causal, -jnp.inf, scores)
        dq = w_q.shape[1]
        weights = jax.nn.softmax(masked / jnp.sqrt(jnp.float32(dq)), axis=-1)
        out = jnp.einsum('bhst,bhtv->bhsv', weights, v)
        cat = out.transpose(0, 2, 1, 3).reshape(b, s, -1)
        return jnp.einsum('bsf,df->bsd', cat, w_o)

    def _L1_ffn_ref(hidden_states, Wg, Wu, Wd):
        import jax, jax.numpy as jnp
        import numpy as np
        NUM_EXPERTS = 8
        HIDDEN = 128
        FFN = 512
        BATCH = 2
        SEQ = 256
        B, S, H = hidden_states.shape
        x = hidden_states.reshape(-1, H)

        def expert_step(acc, w):
            wg, wu, wd = w
            h = jax.nn.silu(x @ wg) * (x @ wu)
            return (acc + h @ wd, None)
        acc, _ = jax.lax.scan(expert_step, jnp.zeros_like(x), (Wg, Wu, Wd))
        return acc.reshape(B, S, H)

    def _L2_xattn_ref(x, cond, w_q, w_k, w_v, w_out, b_out):
        import jax, jax.numpy as jnp
        import numpy as np
        N_HEADS = 16
        D_HEAD = 64
        B, SQ, _ = x.shape
        SKV = cond.shape[1]
        scale = D_HEAD ** (-0.5)
        q = (x @ w_q).reshape(B, SQ, N_HEADS, D_HEAD)
        k = (cond @ w_k).reshape(B, SKV, N_HEADS, D_HEAD)
        v = (cond @ w_v).reshape(B, SKV, N_HEADS, D_HEAD)
        attn = jnp.einsum('bqhd,bkhd->bhqk', q, k) * scale
        attn = jax.nn.softmax(attn, axis=-1)
        out = jnp.einsum('bhqk,bkhd->bqhd', attn, v).reshape(B, SQ, N_HEADS * D_HEAD)
        return out @ w_out + b_out

    def _L2_attn_ref(x, qkv_w, qkv_b, proj_w, proj_b):
        import jax, jax.numpy as jnp
        import numpy as np
        B, S, D, H = (2, 256, 128, 16)
        HD = D // H
        b, s, d = x.shape
        qkv = jnp.einsum('bsd,ed->bse', x, qkv_w) + qkv_b
        qkv = qkv.reshape(b, s, 3, H, HD)
        q = jnp.transpose(qkv[:, :, 0], (0, 2, 1, 3))
        k = jnp.transpose(qkv[:, :, 1], (0, 2, 1, 3))
        v = jnp.transpose(qkv[:, :, 2], (0, 2, 1, 3))
        scale = 1.0 / jnp.sqrt(jnp.asarray(HD, dtype=x.dtype))
        scores = jnp.einsum('bhqe,bhke->bhqk', q, k) * scale
        attn = jax.nn.softmax(scores, axis=-1)
        out = jnp.einsum('bhqk,bhke->bhqe', attn, v)
        out = jnp.transpose(out, (0, 2, 1, 3)).reshape(b, s, d)
        out = jnp.einsum('bsd,ed->bse', out, proj_w) + proj_b
        return out

    def _L2_ffn_ref(x, weight):
        import jax, jax.numpy as jnp
        import numpy as np
        EPS = 1e-08
        w_scale = jnp.mean(jnp.abs(weight)) + EPS
        u = weight / w_scale
        w_quant = u + jax.lax.stop_gradient(jnp.clip(jnp.round(u), -1.0, 1.0) - u)
        a_scale = jnp.max(jnp.abs(x), axis=-1, keepdims=True) + EPS
        z = jnp.clip(x / a_scale * 127.0, -128.0, 127.0)
        a_quant = z + jax.lax.stop_gradient(jnp.round(z) - z)
        y = jnp.einsum('bsi,oi->bso', a_quant, w_quant)
        y = y * (w_scale * a_scale / 127.0)
        return y

    def _L3_xattn_ref(x_text, x_vision, text_mask, vision_mask, Wq, Wk, Wv, W_film_in, b_film_in, W_film_out, b_film_out, g_norm_in, b_norm_in, g_norm_out, b_norm_out, g_ffn, b_ffn, W1, b1, W2, b2, log_dt, A_re, A_im, C_re, C_im, D_skip, mod_gate):
        import jax, jax.numpy as jnp
        import numpy as np
        B, T, DT, G, DV = (16, 64, 128, 72, 96)
        H, DH = (4, 32)
        INNER = H * DH
        HID = 4 * DT
        N_STATE = 64
        K_TOP = 32

        def layernorm(x, g, b, eps=1e-05):
            m = x.mean(-1, keepdims=True)
            v = x.var(-1, keepdims=True)
            return (x - m) * jax.lax.rsqrt(v + eps) * g + b

        def s4d(x, log_dt, A_re, A_im, C_re, C_im, D_skip):
            Bb, L, D = x.shape
            dt = jnp.exp(log_dt)
            A = A_re + 1j * A_im
            C = C_re + 1j * C_im
            dtA = dt[:, None] * A
            dC = C * (jnp.exp(dtA) - 1.0) / A
            powers = jnp.exp(dtA[:, :, None] * jnp.arange(L))
            K = 2.0 * jnp.einsum('dn,dnl->dl', dC, powers).real
            n = 2 * L
            Kf = jnp.fft.rfft(K, n=n, axis=-1)
            xf = jnp.fft.rfft(x, n=n, axis=1)
            y = jnp.fft.irfft(xf * Kf.T[None], n=n, axis=1)[:, :L]
            return y + x * D_skip
        Bb, Tt, D = x_text.shape
        Gg = x_vision.shape[1]
        Q = (x_text @ Wq).reshape(Bb, Tt, H, DH)
        K = (x_vision @ Wk).reshape(Bb, Gg, H, DH)
        scores = jnp.einsum('bthd,bghd->bhtg', Q, K) / np.sqrt(DH).astype(np.float32)
        scores = jnp.where(vision_mask[:, None, None, :], scores, -jnp.inf)
        topv, topi = jax.lax.top_k(scores, K_TOP)
        probs = jax.nn.softmax(topv, axis=-1)
        bi = jnp.arange(Bb)[:, None, None, None]
        hi = jnp.arange(H)[None, :, None, None]
        ti = jnp.arange(Tt)[None, None, :, None]
        attn = jnp.zeros_like(scores).at[bi, hi, ti, topi].set(probs)
        attn_mean = attn.mean(axis=1)
        V = x_vision @ Wv
        c_t = jnp.einsum('btg,bgd->btd', attn_mean, V)
        c_t = c_t * text_mask[..., None]
        x = layernorm(x_text, g_norm_in, b_norm_in)
        scale_in, shift_in = jnp.split(c_t @ W_film_in + b_film_in, 2, axis=-1)
        x = x * (1.0 + mod_gate * scale_in) + mod_gate * shift_in
        y = s4d(x, log_dt, A_re, A_im, C_re, C_im, D_skip)
        scale_out, shift_out = jnp.split(c_t @ W_film_out + b_film_out, 2, axis=-1)
        y = y * (1.0 + mod_gate * scale_out) + mod_gate * shift_out
        xt = x_text + y
        h = layernorm(xt, g_ffn, b_ffn)
        h = jax.nn.gelu(h @ W1 + b1, approximate=False) @ W2 + b2
        xt = xt + h
        return layernorm(xt, g_norm_out, b_norm_out)

    def _L3_attn_ref(x, Wq, Wk, Wv, Wo, compressibility, phase_threshold):
        import jax, jax.numpy as jnp
        import numpy as np
        DIM = 128
        HEADS = 16
        BATCH = 2
        SEQ = 256
        b, l, d = x.shape
        h = compressibility.shape[0]
        hd = d // h
        scale = hd ** (-0.5)

        def proj(W):
            return (x @ W.T).reshape(b, l, h, hd).transpose(0, 2, 1, 3)
        q, k, v = (proj(Wq), proj(Wk), proj(Wv))
        pressure = jnp.einsum('bhid,bhjd->bhij', q, k) * scale
        causal = jnp.triu(jnp.ones((l, l), dtype=bool), k=1)
        pressure = jnp.where(causal, jnp.float32(-10000.0), pressure)
        tau = jax.nn.softplus(compressibility) + 1e-06
        energy = (pressure - phase_threshold) / tau
        attn = 1.0 - jnp.tanh(energy) ** 2
        attn = attn / (jnp.sum(attn, axis=-1, keepdims=True) + 1e-06)
        out = jnp.einsum('bhij,bhjd->bhid', attn, v)
        out = out.transpose(0, 2, 1, 3).reshape(b, l, d)
        return out @ Wo.T

    def _L3_ffn_ref(x, W_router, b_router, W1, b1, W2, b2):
        import jax, jax.numpy as jnp
        import numpy as np
        N_EMBD = 128
        NUM_EXPERTS = 8
        TOP_K = 2
        D_FF = 4 * N_EMBD
        B, S = (4, 256)
        Bv, Sv, D = x.shape
        flat_x = x.reshape(-1, D)
        T = flat_x.shape[0]
        logits = flat_x @ W_router + b_router
        top_vals, top_idx = jax.lax.top_k(logits, TOP_K)
        neg_inf = jnp.full_like(logits, -jnp.inf)
        sparse_logits = neg_inf.at[jnp.arange(T)[:, None], top_idx].set(top_vals)
        router_weights = jax.nn.softmax(sparse_logits, axis=-1)
        final_output = jnp.zeros_like(flat_x)
        for e in range(NUM_EXPERTS):
            expert_mask = jnp.any(top_idx == e, axis=-1)
            h = jax.nn.relu(flat_x @ W1[e] + b1[e])
            y = h @ W2[e] + b2[e]
            w = router_weights[:, e] * expert_mask.astype(x.dtype)
            final_output = final_output + y * w[:, None]
        return final_output.reshape(Bv, Sv, D)
    x = x + _L0_xattn_ref(ctx_768, _layernorm(x, axis=-1), mask_BxS2_bk0, L0_xattn_ln_x_g, L0_xattn_ln_x_b, L0_xattn_ln_l_g, L0_xattn_ln_l_b, L0_xattn_qn_g, L0_xattn_kn_g, L0_xattn_Wq, L0_xattn_Wkv, L0_xattn_Wlkv, L0_xattn_Wo, L0_xattn_bo)
    x = x + _L0_attn_ref(_layernorm(x, axis=-1), L0_attn_ln_weight, L0_attn_ln_bias, L0_attn_k_weight, L0_attn_q_weight, L0_attn_bias)
    x = x + _L0_ffn_ref(_layernorm(x, axis=-1), L0_ffn_clip_x, L0_ffn_clip_down, L0_ffn_w_gate, L0_ffn_w_up, L0_ffn_w_down)
    x = x + _L1_xattn_ref(_layernorm(x, axis=-1), ctx_768, L1_xattn_Wq, L1_xattn_Wk, L1_xattn_Wv, L1_xattn_Wo, L1_xattn_bo)
    x = x + _L1_attn_ref(_layernorm(x, axis=-1), L1_attn_w_q, L1_attn_w_k, L1_attn_w_v, L1_attn_w_o)
    x = x + _L1_ffn_ref(_layernorm(x, axis=-1), L1_ffn_Wg, L1_ffn_Wu, L1_ffn_Wd)
    x = x + _L2_xattn_ref(_layernorm(x, axis=-1), ctx_768, L2_xattn_w_q, L2_xattn_w_k, L2_xattn_w_v, L2_xattn_w_out, L2_xattn_b_out)
    x = x + _L2_attn_ref(_layernorm(x, axis=-1), L2_attn_qkv_w, L2_attn_qkv_b, L2_attn_proj_w, L2_attn_proj_b)
    x = x + _L2_ffn_ref(_layernorm(x, axis=-1), L2_ffn_weight)
    x = x + _L3_xattn_ref(_layernorm(x, axis=-1), ctx_768, mask_BxS_bf1, mask_BxS2_bf1, L3_xattn_Wq, L3_xattn_Wk, L3_xattn_Wv, L3_xattn_W_film_in, L3_xattn_b_film_in, L3_xattn_W_film_out, L3_xattn_b_film_out, L3_xattn_g_norm_in, L3_xattn_b_norm_in, L3_xattn_g_norm_out, L3_xattn_b_norm_out, L3_xattn_g_ffn, L3_xattn_b_ffn, L3_xattn_W1, L3_xattn_b1, L3_xattn_W2, L3_xattn_b2, L3_xattn_log_dt, L3_xattn_A_re, L3_xattn_A_im, L3_xattn_C_re, L3_xattn_C_im, L3_xattn_D_skip, L3_xattn_mod_gate)
    x = x + _L3_attn_ref(_layernorm(x, axis=-1), L3_attn_Wq, L3_attn_Wk, L3_attn_Wv, L3_attn_Wo, L3_attn_compressibility, L3_attn_phase_threshold)
    x = x + _L3_ffn_ref(_layernorm(x, axis=-1), L3_ffn_W_router, L3_ffn_b_router, L3_ffn_W1, L3_ffn_b1, L3_ffn_W2, L3_ffn_b2)
    return x

_drawn_inputs = setup_inputs


def setup_inputs(seed=0):
    import zlib

    import numpy as np

    out = dict(_drawn_inputs(seed))
    spreads = {'L0_xattn_ln_x_g': (1.0, 0.2),
     'L0_xattn_ln_x_b': (0.0, 0.1),
     'L0_xattn_ln_l_g': (1.0, 0.2),
     'L0_xattn_ln_l_b': (0.0, 0.1),
     'L0_xattn_qn_g': (1.0, 0.2),
     'L0_xattn_kn_g': (1.0, 0.2),
     'L0_xattn_bo': (0.0, 0.1),
     'L0_attn_ln_weight': (1.0, 0.6),
     'L0_attn_ln_bias': (0.0, 0.8),
     'L1_xattn_bo': (0.0, 0.1),
     'L2_xattn_b_out': (0.0, 0.1),
     'L3_xattn_b_film_in': (0.0, 0.343),
     'L3_xattn_b_film_out': (0.0, 0.411),
     'L3_xattn_g_norm_in': (1.0, 0.2),
     'L3_xattn_b_norm_in': (0.0, 0.1),
     'L3_xattn_g_norm_out': (1.0, 0.2),
     'L3_xattn_b_norm_out': (0.0, 0.1),
     'L3_xattn_g_ffn': (1.0, 0.6),
     'L3_xattn_b_ffn': (0.0, 0.8),
     'L3_xattn_b1': (0.0, 0.8),
     'L3_xattn_b2': (0.0, 0.331),
     'L3_xattn_A_re': (-0.5, 0.6),
     'L3_attn_compressibility': (0.5, 0.6),
     'L3_attn_phase_threshold': (0.0, 0.8),
     'L3_ffn_b_router': (0.0, 0.269),
     'L3_ffn_b1': (0.0, 0.497),
     'L3_ffn_b2': (0.0, 0.363)}
    factors = {'L0_attn_bias': 8.0,
     'L0_ffn_w_gate': 3.402,
     'L0_ffn_w_up': 3.241,
     'L0_ffn_w_down': 3.412,
     'L1_attn_w_q': 8.0,
     'L1_attn_w_k': 8.0,
     'L2_attn_qkv_b': 3.974,
     'L2_attn_proj_b': 5.333,
     'L3_xattn_Wq': 6.686,
     'L3_xattn_Wk': 7.891,
     'L3_xattn_Wv': 4.483,
     'L3_xattn_W_film_in': 7.678,
     'L3_xattn_W_film_out': 6.471,
     'L3_xattn_W1': 3.379,
     'L3_xattn_W2': 3.523}
    for name, (base, spread) in spreads.items():
        noise = np.random.default_rng([zlib.crc32(name.encode()), seed]).standard_normal(out[name].shape)
        drawn = base * np.exp(spread * noise) if base else spread * noise
        out[name] = jnp.asarray(drawn.astype(out[name].dtype))
    for name, factor in factors.items():
        out[name] = (out[name] * factor).astype(out[name].dtype)
    return out
```

```python
from contextlib import ExitStack

import concourse.bass as bass
import concourse.mybir as mybir

F32 = mybir.dt.float32
BF16 = mybir.dt.bfloat16
U8 = mybir.dt.uint8
ALU = mybir.AluOpType
ACT = mybir.ActivationFunctionType
AX = mybir.AxisListType

P = 128
B, S, D = 8, 64, 128
NK, DC = 1601, 96
TOK = B * S
NT = TOK // P
NCH = (NK + P - 1) // P
FULL = NK // P
LASTK = NK - FULL * P
BANK = 512
NEG = -1.0e30
PI = 3.141592653589793
HALF_ULP = 12582912.0
RS = [BANK * i for i in range((NK + BANK - 1) // BANK)]
KSPAN = [(a, min(BANK, NK - a)) for a in RS]


class Flag:

    def __init__(self, sem):
        self.sem, self.base = sem, 0

    def __call__(self, n):
        return self.base + n


class View(Flag):
    def __init__(self, flag, total):
        self.sem, self.base = flag.sem, flag.base
        flag.base += total


class Link:

    def __init__(self, eng, sem):
        self.eng, self.sem, self.n = eng, sem, 0

    def __call__(self, ins):
        self.n += 1
        ins.then_inc(self.sem, 1)
        self.eng.wait_ge(self.sem, self.n)


class Arena:

    def __init__(self, tile, cols):
        self.tile, self.cols, self.at = tile, cols, 0

    def take(self, cols, dt=F32):
        n = cols if dt == F32 else (cols + 1) // 2
        a = self.tile[:, self.at:self.at + n]
        self.at += n
        assert self.at <= self.cols, (self.at, self.cols)
        if dt != F32:
            a = a.bitcast(dt)
        return a


class G:
    pass


def flags(g, **totals):
    made = {}
    for name, total in totals.items():
        if name not in g.flag:
            g.flag[name] = Flag(g.new_sem(name))
        made[name] = View(g.flag[name], total)
    return made


def steps(g, f, **order):
    made = dict(f)
    for name, events in order.items():
        if name not in g.flag:
            g.flag[name] = Flag(g.new_sem(name))
        for event in events.split():
            made[event] = View(g.flag[name], 1)
    return made


VEC_ROWS = [
    ("l0x_gx", "L0_xattn_ln_x_g", 1, DC), ("l0x_bx", "L0_xattn_ln_x_b", 1, DC),
    ("l0x_gl", "L0_xattn_ln_l_g", 1, D), ("l0x_bl", "L0_xattn_ln_l_b", 1, D),
    ("l0x_bo", "L0_xattn_bo", 1, D),
    ("l1x_bo", "L1_xattn_bo", 1, D), ("l2x_bo", "L2_xattn_b_out", 1, D),
    ("l2a_qkvb", "L2_attn_qkv_b", 3, D), ("l2a_pb", "L2_attn_proj_b", 1, D),
    ("l3x_bfi", "L3_xattn_b_film_in", 2, D), ("l3x_bfo", "L3_xattn_b_film_out", 2, D),
    ("l3x_gi", "L3_xattn_g_norm_in", 1, D), ("l3x_bi", "L3_xattn_b_norm_in", 1, D),
    ("l3x_gf", "L3_xattn_g_ffn", 1, D), ("l3x_bf", "L3_xattn_b_ffn", 1, D),
    ("l3x_b1", "L3_xattn_b1", 4, D), ("l3x_b2", "L3_xattn_b2", 1, D),
    ("l3x_skip", "L3_xattn_D_skip", 1, D), ("l3x_dt", "L3_xattn_log_dt", 1, D),
]
BCAST = [("l0a_w", "L0_attn_ln_weight"), ("l0a_b", "L0_attn_ln_bias"), ("l0a_bias", "L0_attn_bias"),
         ("l3x_go", "L3_xattn_g_norm_out"), ("l3x_bo", "L3_xattn_b_norm_out")]


def stage_setup(g):
    f = flags(g, zeros=1, consts=1, x_in=16, vec_in=16 * (len(VEC_ROWS) + 6), vecs_T=1, vecs=1, bc_in=16 * (len(BCAST) + 4 + 4),
              mask_in=32, masks=1, vec_zero=1)
    names, n = {}, 0
    for name, _, rows, _ in VEC_ROWS:
        names[name] = n
        n += rows
    b1row = n
    n += 32
    nvec = n + 4
    g.col = lambda name, i=0, width=P: g.vcols[0:width, names[name] + i:names[name] + i + 1]
    g.moe_b1 = lambda e, c: g.vcols[:, b1row + 4 * e + c:b1row + 4 * e + c + 1]
    qg = n
    g.qn_col = g.vcols[:, qg:qg + 1]
    g.kn_col = g.vcols[:, qg + 1:qg + 2]

    def sp(e):
        e.dma_start(g.x[:, :, :], g.a["x"].rearrange("b s d -> (b s) d").rearrange("(t p) d -> p t d", p=P)).then_inc(f["x_in"].sem, 16)
        e.wait_ge(f["vec_zero"].sem, f["vec_zero"](1))
        for name, arg, rows, width in VEC_ROWS:
            r = names[name]
            e.dma_start(g.vrows[r:r + rows, 0:width], g.a[arg].rearrange("(r w) -> r w", w=width)).then_inc(f["vec_in"].sem, 16)
        e.dma_start(g.vrows[b1row:b1row + 32, :], g.a["L3_ffn_b1"].rearrange("e (c w) -> (e c) w", w=P)).then_inc(f["vec_in"].sem, 16)
        for i, arg in enumerate(("L0_xattn_qn_g", "L0_xattn_kn_g")):
            for h in range(2):
                e.dma_start(g.vrows[qg + i:qg + i + 1, 64 * h:64 * h + 64], g.a[arg].rearrange("(r w) -> r w", r=1)).then_inc(f["vec_in"].sem, 16)
        e.dma_start(g.vrows[qg + 2:qg + 3, :], g.a["L3_xattn_g_norm_out"].rearrange("(r w) -> r w", r=1)).then_inc(f["vec_in"].sem, 16)
        for i, (name, arg) in enumerate(BCAST):
            e.dma_start(g.bc[:, i, :], g.a[arg].partition_broadcast(P)).then_inc(f["bc_in"].sem, 16)
        for i, (arg, w) in enumerate((("L0_ffn_clip_x", 1), ("L0_ffn_clip_down", 1), ("L3_ffn_b_router", 8))):
            e.dma_start(g.scal[:, 8 * i:8 * i + w], g.a[arg].partition_broadcast(P)).then_inc(f["bc_in"].sem, 16)
        e.dma_start(g.scal[:, 24:25], g.a["L3_xattn_mod_gate"].partition_broadcast(P)).then_inc(f["bc_in"].sem, 16)
        e.dma_start(g.scal[:, 32:48], g.a["L3_attn_compressibility"].rearrange("h a b -> (h a b)").partition_broadcast(P)).then_inc(f["bc_in"].sem, 16)
        e.dma_start(g.scal[:, 48:64], g.a["L3_attn_phase_threshold"].rearrange("h a b -> (h a b)").partition_broadcast(P)).then_inc(f["bc_in"].sem, 16)
        e.dma_start(g.tmask8[:, :], g.a["mask_BxS_bf1"].rearrange("b s -> (b s)").partition_broadcast(P)).then_inc(f["bc_in"].sem, 16)
        e.dma_start(g.b2moe[0:8, :], g.a["L3_ffn_b2"]).then_inc(f["bc_in"].sem, 16)
        for i, name in enumerate(("A_re", "A_im", "C_re", "C_im")):
            e.dma_start(g.s4in[:, S * i:S * i + S], g.a["L3_xattn_" + name]).then_inc(g.s4_sem, 16)
        e.dma_start(g.m8[0:8, 0, :], g.a["mask_BxS2_bk0"]).then_inc(f["mask_in"].sem, 16)
        e.dma_start(g.m8[0:8, 1, :], g.a["mask_BxS2_bf1"]).then_inc(f["mask_in"].sem, 16)

    def pool(e):
        ln = g.link["pool"]
        nc = g.nc
        ln(nc.gpsimd.memset(g.ident, 0.0))
        ln(nc.gpsimd.affine_select(out=g.ident, in_=g.ident, compare_op=ALU.not_equal, fill=1.0, base=0,
                                   pattern=[[-1, P]], channel_multiplier=1))
        ln(nc.gpsimd.memset(g.sel, 0.0))
        ln(nc.gpsimd.affine_select(out=g.sel, in_=g.sel, compare_op=ALU.not_equal, fill=1.0, base=0,
                                   pattern=[[-1, B], [0, P]], channel_multiplier=1))
        ln(nc.gpsimd.memset(g.ones, 1.0))
        ln(nc.gpsimd.memset(g.half, 0.5))
        ln(nc.gpsimd.memset(g.blk, 0.0))
        ln(nc.gpsimd.memset(g.blk[0:64, 0:64], 1.0))
        ln(nc.gpsimd.memset(g.blk[64:128, 64:128], 1.0))
        ln(nc.gpsimd.memset(g.mask_bd, 0.0))
        ln(nc.gpsimd.memset(g.mask_bd[0:64, 64:128], NEG))
        ln(nc.gpsimd.memset(g.mask_bd[64:128, 0:64], NEG))
        ln(nc.gpsimd.memset(g.mask_ca, 0.0))
        ln(nc.gpsimd.affine_select(out=g.mask_ca, in_=g.mask_ca, compare_op=ALU.is_ge, fill=NEG, base=0,
                                   pattern=[[-1, P]], channel_multiplier=1))
        ln(nc.gpsimd.memset(g.mask_ca[64:128, 0:64], NEG))
        ln(nc.gpsimd.memset(g.tri_mul, 8.0 ** -0.5))
        ln(nc.gpsimd.affine_select(out=g.tri_mul, in_=g.tri_mul, compare_op=ALU.is_ge, fill=0.0, base=0,
                                   pattern=[[-1, P]], channel_multiplier=1))
        ln(nc.gpsimd.memset(g.tri_add, 0.0))
        ln(nc.gpsimd.affine_select(out=g.tri_add, in_=g.tri_add, compare_op=ALU.is_ge, fill=-10000.0, base=0,
                                   pattern=[[-1, P]], channel_multiplier=1))
        ln(nc.gpsimd.memset(g.head_of, 1.0))
        ln(nc.gpsimd.affine_select(out=g.head_of, in_=g.head_of, compare_op=ALU.is_ge, fill=0.0, base=0,
                                   pattern=[[-8, 16]], channel_multiplier=1))
        ln(nc.gpsimd.affine_select(out=g.head_of, in_=g.head_of, compare_op=ALU.is_ge, fill=0.0, base=7,
                                   pattern=[[8, 16]], channel_multiplier=-1))
        ln(nc.gpsimd.memset(g.before, 1.0))
        ln(nc.gpsimd.affine_select(out=g.before, in_=g.before, compare_op=ALU.is_gt, fill=0.0, base=0,
                                   pattern=[[1, 8], [-1, 8]], channel_multiplier=0))
        ln(nc.gpsimd.tensor_tensor(g.fold, g.ident[:, 0:64], g.ident[:, 64:128], ALU.add))
        ln(nc.gpsimd.memset(g.cT_hi[96:97, :, :], 1.0))
        ln(nc.gpsimd.memset(g.cT_lo[96:97, :, :], 0.0))
        ln(nc.gpsimd.memset(g.cr_hi[:, :, :, 96:97], 1.0))
        ln(nc.gpsimd.memset(g.cr_lo[:, :, :, 96:97], 0.0))
        ln(nc.gpsimd.memset(g.neg_blk[0:64, 0:64], -1.0))
        ln(nc.gpsimd.memset(g.neg_blk[64:128, 64:128], -1.0))
        ln(nc.gpsimd.memset(g.neg_blk[0:64, 64:128], 0.0))
        nc.gpsimd.memset(g.neg_blk[64:128, 0:64], 0.0).then_inc(f["consts"].sem, 1)

    def dve(e):
        nc = g.nc
        ln = g.link["dve"]
        nc.vector.memset(g.vrows, 0.0).then_inc(f["vec_zero"].sem, 1)
        e.wait_ge(f["vecs_T"].sem, f["vecs_T"](1))
        nc.vector.tensor_copy(g.vcols[:, 0:nvec], g.ps[:, 7, 0:nvec]).then_inc(f["vecs"].sem, 1)
        e.wait_ge(f["vecs"].sem, f["vecs"](1))
        e.wait_ge(f["consts"].sem, f["consts"](1))
        e.wait_ge(f["mask_in"].sem, f["mask_in"](32))
        ln(nc.vector.tensor_copy(g.mtmp[0:8, :, :], g.m8[0:8, :, :]))
        nc.vector.tensor_scalar(g.kmask[0:8, :, :], g.mtmp[0:8, :, :], -1.0, -NEG, ALU.add, ALU.mult).then_inc(f["masks"].sem, 1)
        e.wait_ge(f["bc_in"].sem, f["bc_in"](16 * (len(BCAST) + 8)))
        ln(nc.vector.tensor_copy(g.tmask, g.tmask8))
        e.wait_ge(f["x_in"].sem, f["x_in"](16))

    def pe(e):
        nc = g.nc
        e.wait_ge(f["consts"].sem, f["consts"](1))
        e.wait_ge(f["vec_in"].sem, f["vec_in"](16 * (len(VEC_ROWS) + 6)))
        nc.tensor.transpose(g.ps[:, 7, 0:nvec], g.vrows[0:nvec, :], g.ident[0:nvec, 0:nvec]).then_inc(f["vecs_T"].sem, 1)

    def act(e):
        e.wait_ge(f["consts"].sem, f["consts"](1))
        e.wait_ge(f["vecs"].sem, f["vecs"](1))
        e.wait_ge(f["bc_in"].sem, f["bc_in"](16 * (len(BCAST) + 8)))
    return dict(load=nothing, sp=sp, pool=pool, dve=dve, pe=pe, act=act)


def layernorm(g, src, out_rows, eps=1e-5, out_T=None, gain=None, shift=None, bank=7):
    turned = 0 if out_T is None else 1
    f = flags(g, ln_var=1, ln_std=1, ln_rows=1, ln_T=turned, ln_ready=turned)

    def dve(e):
        nc, ln = g.nc, g.link["dve"]
        for t in range(NT):
            ln(nc.vector.bn_stats(g.st[:, 6 * t:6 * t + 6], src[:, t, :]))
        for t in range(NT):
            i = nc.vector.bn_aggr(g.mv[:, 2 * t:2 * t + 2], g.st[:, 6 * t:6 * t + 6])
        ln(i)
        mv = g.mv.rearrange("p (t two) -> p t two", two=2)
        nc.vector.tensor_scalar(g.ve, mv[:, :, 1], eps, None, ALU.add).then_inc(f["ln_var"].sem, 1)
        e.wait_ge(f["ln_std"].sem, f["ln_std"](1))
        for t in range(NT):
            i = nc.vector.tensor_scalar(out_rows[:, t, :], src[:, t, :], g.mv[:, 2 * t:2 * t + 1],
                                        g.rstd[:, t:t + 1], ALU.subtract, ALU.mult)
        i.then_inc(f["ln_rows"].sem, 1)
        e.wait_ge(f["ln_rows"].sem, f["ln_rows"](1))
        if out_T is not None:
            e.wait_ge(f["ln_T"].sem, f["ln_T"](1))
            if gain is None:
                i = nc.vector.tensor_copy(out_T, g.ps[:, bank, :])
            else:
                i = nc.vector.tensor_scalar(out_T, g.ps[:, bank, :], gain, shift, ALU.mult, ALU.add)
            i.then_inc(f["ln_ready"].sem, 1)
            e.wait_ge(f["ln_ready"].sem, f["ln_ready"](1))

    def act(e):
        e.wait_ge(f["ln_var"].sem, f["ln_var"](1))
        g.link["act"](g.nc.scalar.activation(g.sd, g.ve, ACT.Ln))
        g.nc.scalar.activation(g.rstd, g.sd, ACT.Exp, scale=-0.5).then_inc(f["ln_std"].sem, 1)

    def pe(e):
        if out_T is None:
            return
        e.wait_ge(f["ln_rows"].sem, f["ln_rows"](1))
        for t in range(NT):
            i = g.nc.tensor.transpose(g.ps[:, bank, P * t:P * t + P], out_rows[:, t, :], g.ident)
        i.then_inc(f["ln_T"].sem, 1)

    return dict(dve=dve, act=act, pe=pe, ready=f["ln_ready"], f=f)


def add_back(g, yT, yT_flag, bank=7):
    f = flags(g, back_T=1, x_done=1)

    def pe(e):
        e.wait_ge(yT_flag.sem, yT_flag(1))
        for t in range(NT):
            i = g.nc.tensor.transpose(g.ps[:, bank, P * t:P * t + P], yT[:, P * t:P * t + P], g.ident)
        i.then_inc(f["back_T"].sem, 1)

    def dve(e):
        e.wait_ge(f["back_T"].sem, f["back_T"](1))
        g.nc.vector.tensor_tensor(g.x2d, g.x2d, g.ps[:, bank, :], ALU.add).then_inc(f["x_done"].sem, 1)
        e.wait_ge(f["x_done"].sem, f["x_done"](1))
    return dict(pe=pe, dve=dve, x_done=f["x_done"])


def add_rows(g, bank, ready):
    f = flags(g, x_done=1)

    def dve(e):
        e.wait_ge(ready.sem, ready(1))
        g.nc.vector.tensor_tensor(g.x2d, g.x2d, g.ps[:, bank, :], ALU.add).then_inc(f["x_done"].sem, 1)
        e.wait_ge(f["x_done"].sem, f["x_done"](1))
    return dict(dve=dve, x_done=f["x_done"])


def layer_l0_cross(g):
    nc = g.nc
    tmp = g.temps()
    NKL = NK + S
    pre = Arena(g.pre, 4096)
    raw = [tmp.take(NCH * DC).rearrange("p (c d) -> p c d", d=DC) for _ in range(2)]
    cst = tmp.take(6 * NCH)
    cmv = tmp.take(2 * NCH)
    cve, csd, crs = tmp.take(NCH), tmp.take(NCH), tmp.take(NCH)
    xnT = tmp.take(NK)
    ksq = tmp.take(NKL)
    prob = ksq
    kinv = tmp.take((NCH + 1) * P)
    PT = kinv.rearrange("p (c n) -> p c n", n=P)
    kinv = kinv[:, 0:NKL]
    knT = tmp.take(NKL)
    V = pre.take((NCH + 1) * P).rearrange("p (c n) -> p c n", n=P)
    lat = g.xn
    oT = tmp.take(TOK)
    lat2 = oT.rearrange("p (t d) -> p t d", d=D)
    lT = g.xnT
    qsq, qinv, yT = ksq[:, 0:TOK], kinv[:, 0:TOK], xnT[:, 0:TOK]
    Qbd = pre.take(B * P).rearrange("p (b n) -> p b n", b=B)
    diag = tmp.take(P)
    mx, nmx, z, zi = (tmp.take(B) for _ in range(4))
    qfac = tmp.take(1)
    wT = pre.take(6 * P)
    w = g.slot[0]
    wq, wo, wlk, wlv = (w[:, P * i:P * i + P] for i in range(4))
    wk, wv = w[:, 4 * P:4 * P + DC], w[:, 5 * P:5 * P + DC]
    A = g.ps[:, 0:4, :].rearrange("p a n -> p (a n)")
    Bk = g.ps[:, 4:8, :].rearrange("p a n -> p (a n)")
    wqT, woT, wlkT, wlvT = (wT[:, P * i:P * i + P] for i in range(4))
    wkT, wvT = wT[0:DC, 4 * P:5 * P], wT[0:DC, 5 * P:6 * P]

    ln1 = layernorm(g, g.x, lat)
    ln2 = layernorm(g, lat, lat2, out_T=lT, gain=g.col("l0x_gl"), shift=g.col("l0x_bl"))
    f = flags(g, raw_zero=1, l0_w_in=16 * 6, raw_in0=32 * 4, raw_in1=32 * 4, 
              cT_mm=B, cT_hi=B, c_var=B, c_std=B,
              c_rows=B, xh_T=B, xn_ready=B, k_mm=B, k_sq=B, k_ss=B, k_max=B, k_inv=B, k_ready=B, v_mm=B, v_ready=B,
              l0_s=B, l0_max=B, l0_p=B, l0_diag=B, l0_pt=B, l0_pt_a=B, l0_pt_d=B, l0_o=B, l0_o_sb=B)
    f = steps(g, f, rows_T="l0_wT", products="q_mm q_ss l0_y", dve_step="l0_w_ready q_max q_ready l0_yT", act_step="q_sq q_inv")
    back = add_back(g, yT, f["l0_yT"])
    raw_in = [f["raw_in0"], f["raw_in1"]]
    HALF = 8

    def load(e):
        a = g.a
        for dst, src in ((wq, a["L0_xattn_Wq"]), (wo, a["L0_xattn_Wo"]), (wlk, a["L0_xattn_Wlkv"][0:P, :]),
                         (wlv, a["L0_xattn_Wlkv"][P:2 * P, :]), (wk, a["L0_xattn_Wkv"][0:P, :]), (wv, a["L0_xattn_Wkv"][P:2 * P, :])):
            e.dma_start(dst, src).then_inc(f["l0_w_in"].sem, 16)

    def sp(e):
        e.wait_ge(f["raw_zero"].sem, f["raw_zero"](1))
        for b in range(B):
            if b >= 2:
                e.wait_ge(f["xh_T"].sem, f["xh_T"](b - 1))
            r, q = raw[b % 2], raw_in[b % 2]
            e.dma_start(r[:, 0:FULL, :], g.a["ctx_768"][b, 0:FULL * P, :].rearrange("(c p) d -> p c d", p=P)).then_inc(q.sem, 16)
            e.dma_start(r[0:LASTK, FULL, :], g.a["ctx_768"][b, FULL * P:NK, :]).then_inc(q.sem, 16)

    def dve(e):
        ln = g.link["dve"]
        v = nc.vector
        v.memset(raw[0][:, FULL, :], 0.0)
        v.memset(raw[1][:, FULL, :], 0.0).then_inc(f["raw_zero"].sem, 1)
        ln(v.memset(Qbd, 0.0))
        ln(v.tensor_scalar(qfac, g.qn_col, g.kn_col, 8.0, ALU.mult, ALU.mult))
        e.wait_ge(f["l0_wT"].sem, f["l0_wT"](1))
        v.tensor_copy(wT[:, 0:4 * P], A[:, 0:4 * P])
        v.tensor_copy(wT[0:DC, 4 * P:6 * P], A[0:DC, 4 * P:6 * P]).then_inc(f["l0_w_ready"].sem, 1)
        ln1["dve"](e)
        ln2["dve"](e)
        e.wait_ge(f["q_ss"].sem, f["q_ss"](1))
        v.tensor_scalar(qinv, Bk[:, 0:TOK], 64.0e-16, None, ALU.max).then_inc(f["q_max"].sem, 1)
        e.wait_ge(f["q_inv"].sem, f["q_inv"](1))
        for h in range(2):
            r = slice(64 * h, 64 * h + 64)
            i = v.scalar_tensor_tensor(out=Qbd[r, :, 64 * h:64 * h + 64], in0=A[r, 0:TOK].rearrange("p (b s) -> p b s", b=B),
                                       scalar=qfac[r, :], in1=qinv[r, :].rearrange("p (b s) -> p b s", b=B),
                                       op0=ALU.mult, op1=ALU.mult)
        i.then_inc(f["q_ready"].sem, 1)
        for b in range(B):
            r = raw[b % 2]
            e.wait_ge(raw_in[b % 2].sem, raw_in[b % 2](32 * (b // 2 + 1)))
            ln(v.tensor_copy(g.cr_hi[:, b, :, 0:DC], r))
            v.tensor_tensor(g.cr_lo[:, b, :, 0:DC], r, g.cr_hi[:, b, :, 0:DC], ALU.subtract)
            for c in range(NCH):
                v.bn_stats(cst[:, 6 * c:6 * c + 6], r[:, c, :])
            e.wait_ge(f["cT_hi"].sem, f["cT_hi"](b + 1))
            ln(v.tensor_tensor(g.cT_lo[0:DC, b, :], A[0:DC, 0:NK], g.cT_hi[0:DC, b, :], ALU.subtract))
            for c in range(NCH):
                i = v.bn_aggr(cmv[:, 2 * c:2 * c + 2], cst[:, 6 * c:6 * c + 6])
            ln(i)
            mv = cmv.rearrange("p (c two) -> p c two", two=2)
            i = v.tensor_scalar(cve, mv[:, :, 1], 1e-5, None, ALU.add)
            i.then_inc(f["c_var"].sem, 1)
            e.wait_ge(f["c_var"].sem, f["c_var"](b + 1))
            e.wait_ge(f["c_std"].sem, f["c_std"](b + 1))
            e.wait_ge(f["cT_mm"].sem, f["cT_mm"](b + 1))
            for c in range(NCH):
                i = v.tensor_scalar(r[:, c, :], r[:, c, :], cmv[:, 2 * c:2 * c + 1], crs[:, c:c + 1], ALU.subtract, ALU.mult)
            i.then_inc(f["c_rows"].sem, 1)
            e.wait_ge(f["k_ss"].sem, f["k_ss"](b + 1))
            v.tensor_scalar(kinv, Bk[:, 0:NKL], 64.0e-16, None, ALU.max).then_inc(f["k_max"].sem, 1)
            e.wait_ge(f["k_inv"].sem, f["k_inv"](b + 1))
            v.tensor_tensor(knT, A[:, 0:NKL], kinv, ALU.mult).then_inc(f["k_ready"].sem, 1)
            e.wait_ge(f["l0_s"].sem, f["l0_s"](b + 1))
            ln(v.tensor_reduce(mx[:, b:b + 1], A[:, 0:NKL], AX.X, ALU.max))
            v.tensor_scalar(nmx[:, b:b + 1], mx[:, b:b + 1], -1.0, None, ALU.mult).then_inc(f["l0_max"].sem, 1)
            e.wait_ge(f["l0_p"].sem, f["l0_p"](b + 1))
            ln(v.reciprocal(zi[:, b:b + 1], z[:, b:b + 1]))
            v.tensor_scalar(diag, g.ident, zi[:, b:b + 1], None, ALU.mult).then_inc(f["l0_diag"].sem, 1)
            e.wait_ge(f["l0_pt"].sem, f["l0_pt"](b + 1))
            v.tensor_copy(PT[:, HALF:FULL, :], Bk[:, HALF * P:FULL * P].rearrange("p (c n) -> p c n", n=P))
            v.tensor_copy(PT[0:LASTK, FULL, :], Bk[0:LASTK, FULL * P:FULL * P + P])
            v.tensor_copy(PT[0:S, NCH, :], Bk[0:S, NCH * P:NCH * P + P]).then_inc(f["l0_pt_d"].sem, 1)
            e.wait_ge(f["l0_o"].sem, f["l0_o"](b + 1))
            for h in range(2):
                q = slice(64 * h, 64 * h + 64)
                i = v.tensor_copy(oT[q, S * b:S * b + S], A[q, 64 * h:64 * h + 64])
            i.then_inc(f["l0_o_sb"].sem, 1)
        e.wait_ge(f["l0_y"].sem, f["l0_y"](1))
        v.tensor_scalar(yT, Bk[:, 0:TOK], g.col("l0x_bo"), None, ALU.add).then_inc(f["l0_yT"].sem, 1)
        back["dve"](e)

    def act(e):
        s = nc.scalar
        ln1["act"](e)
        ln2["act"](e)
        e.wait_ge(f["q_mm"].sem, f["q_mm"](1))
        s.activation(qsq, A[:, 0:TOK], ACT.Square).then_inc(f["q_sq"].sem, 1)
        e.wait_ge(f["q_max"].sem, f["q_max"](1))
        g.link["act"](s.activation(qsq, qinv, ACT.Ln))
        s.activation(qinv, qsq, ACT.Exp, scale=-0.5).then_inc(f["q_inv"].sem, 1)
        for b in range(B):
            e.wait_ge(f["cT_mm"].sem, f["cT_mm"](b + 1))
            s.activation(g.cT_hi[0:DC, b, :], A[0:DC, 0:NK], ACT.Copy).then_inc(f["cT_hi"].sem, 1)
            e.wait_ge(f["c_var"].sem, f["c_var"](b + 1))
            g.link["act"](s.activation(csd, cve, ACT.Ln))
            s.activation(crs, csd, ACT.Exp, scale=-0.5).then_inc(f["c_std"].sem, 1)
            e.wait_ge(f["xh_T"].sem, f["xh_T"](b + 1))
            s.activation(xnT[0:DC, :], Bk[0:DC, 0:NK], ACT.Identity, bias=g.col("l0x_bx", 0, DC),
                         scale=g.col("l0x_gx", 0, DC)).then_inc(f["xn_ready"].sem, 1)
            e.wait_ge(f["k_mm"].sem, f["k_mm"](b + 1))
            s.activation(ksq, A[:, 0:NKL], ACT.Square).then_inc(f["k_sq"].sem, 1)
            e.wait_ge(f["k_max"].sem, f["k_max"](b + 1))
            g.link["act"](s.activation(ksq, kinv, ACT.Ln))
            s.activation(kinv, ksq, ACT.Exp, scale=-0.5).then_inc(f["k_inv"].sem, 1)
            e.wait_ge(f["v_mm"].sem, f["v_mm"](b + 1))
            s.activation(V[:, 0:FULL, :], Bk[:, 0:FULL * P].rearrange("p (c n) -> p c n", n=P), ACT.Copy)
            s.activation(V[0:LASTK, FULL, :], Bk[0:LASTK, FULL * P:FULL * P + P], ACT.Copy)
            s.activation(V[0:S, NCH, :], Bk[0:S, NCH * P:NCH * P + P], ACT.Copy).then_inc(f["v_ready"].sem, 1)
            e.wait_ge(f["l0_max"].sem, f["l0_max"](b + 1))
            s.activation(prob, A[:, 0:NKL], ACT.Exp, bias=nmx[:, b:b + 1], accum_out=z[:, b:b + 1]).then_inc(f["l0_p"].sem, 1)
            e.wait_ge(f["l0_pt"].sem, f["l0_pt"](b + 1))
            s.activation(PT[:, 0:HALF, :], Bk[:, 0:HALF * P].rearrange("p (c n) -> p c n", n=P), ACT.Copy).then_inc(f["l0_pt_a"].sem, 1)

    def pe(e):
        t = nc.tensor
        e.wait_ge(f["l0_w_in"].sem, f["l0_w_in"](96))
        for i, m in enumerate((wq, wo, wlk, wlv)):
            t.transpose(A[:, P * i:P * i + P], m, g.ident)
        t.transpose(A[0:DC, 4 * P:5 * P], wk, g.ident)
        t.transpose(A[0:DC, 5 * P:6 * P], wv, g.ident).then_inc(f["l0_wT"].sem, 1)
        ln1["pe"](e)
        ln2["pe"](e)
        e.wait_ge(f["l0_w_ready"].sem, f["l0_w_ready"](1))
        e.wait_ge(ln2["ready"].sem, ln2["ready"](1))
        t.matmul(A[:, 0:TOK], wqT, lT, start=True, stop=True).then_inc(f["q_mm"].sem, 1)
        e.wait_ge(f["q_sq"].sem, f["q_sq"](1))
        t.matmul(Bk[:, 0:TOK], g.blk, qsq, start=True, stop=True).then_inc(f["q_ss"].sem, 1)
        e.wait_ge(f["q_ready"].sem, f["q_ready"](1))
        e.wait_ge(g.flag["masks"].sem, 1)
        for b in range(B):
            e.wait_ge(raw_in[b % 2].sem, raw_in[b % 2](32 * (b // 2 + 1)))
            if b:
                e.wait_ge(f["l0_o_sb"].sem, f["l0_o_sb"](b))
            for c in range(NCH):
                n = P if c < FULL else LASTK
                i = t.transpose(A[0:DC, P * c:P * c + n], raw[b % 2][0:n, c, :], g.ident[0:n, 0:n])
            i.then_inc(f["cT_mm"].sem, 1)
            e.wait_ge(f["c_rows"].sem, f["c_rows"](b + 1))
            if b:
                e.wait_ge(f["l0_pt_a"].sem, f["l0_pt_a"](b))
                e.wait_ge(f["l0_pt_d"].sem, f["l0_pt_d"](b))
            for c in range(NCH):
                n = P if c < FULL else LASTK
                i = t.transpose(Bk[0:DC, P * c:P * c + n], raw[b % 2][0:n, c, :], g.ident[0:n, 0:n])
            i.then_inc(f["xh_T"].sem, 1)
            e.wait_ge(f["xn_ready"].sem, f["xn_ready"](b + 1))
            e.wait_ge(f["c_var"].sem, f["c_var"](b + 1))
            for a, n in KSPAN:
                t.matmul(A[:, a:a + n], wkT, xnT[0:DC, a:a + n], start=True, stop=True)
            t.matmul(A[:, NK:NKL], wlkT, lT[:, S * b:S * b + S], start=True, stop=True).then_inc(f["k_mm"].sem, 1)
            e.wait_ge(f["k_sq"].sem, f["k_sq"](b + 1))
            for a in RS:
                n = min(BANK, NKL - a)
                i = t.matmul(Bk[:, a:a + n], g.blk, ksq[:, a:a + n], start=True, stop=True)
            i.then_inc(f["k_ss"].sem, 1)
            e.wait_ge(f["k_max"].sem, f["k_max"](b + 1))
            for c in range(NCH):
                n = P if c < FULL else LASTK
                t.matmul(Bk[0:n, P * c:P * c + P], xnT[0:DC, P * c:P * c + n], wvT, start=True, stop=True)
            t.matmul(Bk[0:S, P * NCH:P * NCH + P], lT[:, S * b:S * b + S], wlvT, start=True, stop=True).then_inc(f["v_mm"].sem, 1)
            e.wait_ge(f["k_ready"].sem, f["k_ready"](b + 1))
            for a, n in KSPAN:
                t.matmul(A[:, a:a + n], Qbd[:, b, :], knT[:, a:a + n], start=True, stop=False)
                t.matmul(A[:, a:a + n], g.sel[:, b, :], g.kmask[0:8, 0, a:a + n], start=False, stop=True)
            t.matmul(A[:, NK:NKL], Qbd[:, b, :], knT[:, NK:NKL], start=True, stop=True).then_inc(f["l0_s"].sem, 1)
            e.wait_ge(f["l0_diag"].sem, f["l0_diag"](b + 1))
            e.wait_ge(f["v_ready"].sem, f["v_ready"](b + 1))
            for c in range(NCH + 1):
                n = P if c < FULL else LASTK if c == FULL else S
                a = P * c if c <= FULL else NK
                i = t.matmul(Bk[0:n, P * c:P * c + P], prob[:, a:a + n], diag, start=True, stop=True)
            i.then_inc(f["l0_pt"].sem, 1)
            e.wait_ge(f["l0_pt_a"].sem, f["l0_pt_a"](b + 1))
            e.wait_ge(f["l0_pt_d"].sem, f["l0_pt_d"](b + 1))
            for c in range(NCH + 1):
                n = P if c < FULL else LASTK if c == FULL else S
                i = t.matmul(A[:, 0:P], V[0:n, c, :], PT[0:n, c, :], start=c == 0, stop=c == NCH)
            i.then_inc(f["l0_o"].sem, 1)
        e.wait_ge(f["l0_o_sb"].sem, f["l0_o_sb"](B))
        t.matmul(Bk[:, 0:TOK], woT, oT, start=True, stop=True).then_inc(f["l0_y"].sem, 1)
        back["pe"](e)

    def pool(e):
        pass

    return dict(load=load, sp=sp, dve=dve, act=act, pe=pe, pool=pool)


def wait_slot(g, e, layer):
    if layer >= 2:
        e.wait_ge(g.flag["x_done"].sem, layer - 1)


def layer_l0_cosine(g):
    nc = g.nc
    tmp = g.temps()
    NI = 4
    w = g.slot[1]
    kw = w[:, 0:NI * D].rearrange("p (c d) -> p c d", d=D)
    qw = w[:, NI * D:2 * NI * D].rearrange("p (c d) -> p c d", d=D)
    rows = tmp.take(NT * D).rearrange("p (t d) -> p t d", d=D)
    sq = tmp.take(NT * D).rearrange("p (t d) -> p t d", d=D)
    kn = tmp.take(NT * D).rearrange("p (t d) -> p t d", d=D)
    ss, sd, inv = (tmp.take(NT) for _ in range(3))
    kss, ksd, kin = (tmp.take(NT) for _ in range(3))
    QT, KT = tmp.take(TOK), tmp.take(TOK)
    c = tmp.take(NI * TOK)
    a = tmp.take(NI * TOK)
    t = tmp.take(NI * TOK)
    A = g.ps[:, 0:4, :].rearrange("p a n -> p (a n)")
    ln1 = layernorm(g, g.x, g.xn)
    ln2 = layernorm(g, g.xn, g.xn, eps=1e-12)
    f = steps(g, flags(g, a0_w_in=32, x_done=1), sums_ready="a0_kss a0_ss a0_xss", stds_ready="a0_kstd a0_std a0_xstd",
              rows_ready="a0_krows a0_rows", rows_T="a0_KT a0_QT", T_ready="a0_KT_sb a0_QT_sb", products="a0_s a0_X",
              act_step="a0_den a0_angle a0_p8", dve_step="a0_clip a0_ratio a0_B")

    def load(e):
        for dst, name in ((kw, "L0_attn_k_weight"), (qw, "L0_attn_q_weight")):
            e.dma_start(dst, g.a[name].rearrange("(c p) d -> p c d", p=P)).then_inc(f["a0_w_in"].sem, 16)

    def l2rows(e, src, ss, sq, flag):
        ln, v = g.link["dve"], nc.vector
        ln(v.tensor_tensor(sq, src, src, ALU.mult))
        ln(v.tensor_reduce(ss, sq, AX.X, ALU.add))
        v.tensor_scalar(ss, ss, 1e-24, None, ALU.max).then_inc(flag.sem, 1)

    def dve(e):
        ln, v = g.link["dve"], nc.vector
        e.wait_ge(f["a0_w_in"].sem, f["a0_w_in"](32))
        l2rows(e, kw, kss, sq, f["a0_kss"])
        e.wait_ge(f["a0_kstd"].sem, f["a0_kstd"](1))
        ln(v.reciprocal(kin, ksd))
        for j in range(NT):
            i = v.tensor_scalar(kn[:, j, :], kw[:, j, :], kin[:, j:j + 1], None, ALU.mult)
        i.then_inc(f["a0_krows"].sem, 1)
        e.wait_ge(f["a0_KT"].sem, f["a0_KT"](1))
        v.tensor_copy(KT, g.ps[:, 4, :]).then_inc(f["a0_KT_sb"].sem, 1)
        ln1["dve"](e)
        ln2["dve"](e)
        for j in range(NT):
            i = v.tensor_tensor(rows[:, j, :], g.xn[:, j, :], g.bcv["l0a_w"], ALU.mult)
        ln(i)
        for j in range(NT):
            i = v.tensor_tensor(rows[:, j, :], rows[:, j, :], g.bcv["l0a_b"], ALU.add)
        ln(i)
        l2rows(e, rows, ss, sq, f["a0_ss"])
        e.wait_ge(f["a0_std"].sem, f["a0_std"](1))
        ln(v.reciprocal(inv, sd))
        for j in range(NT):
            i = v.tensor_scalar(rows[:, j, :], rows[:, j, :], inv[:, j:j + 1], None, ALU.mult)
        i.then_inc(f["a0_rows"].sem, 1)
        e.wait_ge(f["a0_QT"].sem, f["a0_QT"](1))
        v.tensor_copy(QT, g.ps[:, 5, :]).then_inc(f["a0_QT_sb"].sem, 1)
        e.wait_ge(f["a0_s"].sem, f["a0_s"](1))
        v.tensor_scalar(c, A, -1.0 + 1e-6, 1.0 - 1e-6, ALU.max, ALU.min).then_inc(f["a0_clip"].sem, 1)
        e.wait_ge(f["a0_den"].sem, f["a0_den"](1))
        ln(v.tensor_scalar(t, t, 1.0, None, ALU.add))
        ln(v.tensor_tensor(t, t, a, ALU.mult))
        ln(v.tensor_scalar(t, t, -1.0, 2.0, ALU.mult, ALU.add))
        ln(v.tensor_tensor(a, a, t, ALU.mult))
        v.tensor_tensor(c, c, a, ALU.mult).then_inc(f["a0_ratio"].sem, 1)
        e.wait_ge(f["a0_angle"].sem, f["a0_angle"](1))
        ln(v.tensor_scalar(t, a, 2.0 / PI, 0.5, ALU.mult, ALU.add))
        e.wait_ge(f["a0_p8"].sem, f["a0_p8"](1))
        v.tensor_tensor(t, t, c, ALU.mult).then_inc(f["a0_B"].sem, 1)
        e.wait_ge(f["a0_X"].sem, f["a0_X"](1))
        ln(v.tensor_copy(rows, g.ps[:, 6, :].rearrange("p (t d) -> p t d", d=D)))
        l2rows(e, rows, ss, sq, f["a0_xss"])
        e.wait_ge(f["a0_xstd"].sem, f["a0_xstd"](1))
        ln(v.reciprocal(inv, sd))
        for j in range(NT):
            i = v.scalar_tensor_tensor(out=rows[:, j, :], in0=rows[:, j, :], scalar=inv[:, j:j + 1], in1=g.bcv["l0a_bias"],
                                       op0=ALU.mult, op1=ALU.add)
        ln(i)
        v.tensor_tensor(g.x[:, :, :], g.x[:, :, :], rows, ALU.add).then_inc(f["x_done"].sem, 1)
        e.wait_ge(f["x_done"].sem, f["x_done"](1))

    def act(e):
        s, ln = nc.scalar, g.link["act"]
        e.wait_ge(f["a0_kss"].sem, f["a0_kss"](1))
        s.activation(ksd, kss, ACT.Sqrt).then_inc(f["a0_kstd"].sem, 1)
        ln1["act"](e)
        ln2["act"](e)
        e.wait_ge(f["a0_ss"].sem, f["a0_ss"](1))
        s.activation(sd, ss, ACT.Sqrt).then_inc(f["a0_std"].sem, 1)
        e.wait_ge(f["a0_clip"].sem, f["a0_clip"](1))
        ln(s.activation(a, c, ACT.Square))
        ln(s.activation(t, a, ACT.Ln, scale=-1.0, bias=1.0))
        ln(s.activation(t, t, ACT.Exp, scale=0.5))
        ln(s.activation(a, t, ACT.Ln, bias=1.0))
        s.activation(a, a, ACT.Exp, scale=-1.0).then_inc(f["a0_den"].sem, 1)
        e.wait_ge(f["a0_ratio"].sem, f["a0_ratio"](1))
        s.activation(a, c, ACT.Arctan).then_inc(f["a0_angle"].sem, 1)
        e.wait_ge(f["a0_angle"].sem, f["a0_angle"](1))
        ln(s.activation(c, a, ACT.Square, scale=2.0 / PI, bias=g.half))
        ln(s.activation(c, c, ACT.Square))
        s.activation(c, c, ACT.Square).then_inc(f["a0_p8"].sem, 1)
        e.wait_ge(f["a0_xss"].sem, f["a0_xss"](1))
        s.activation(sd, ss, ACT.Sqrt).then_inc(f["a0_xstd"].sem, 1)

    def pe(e):
        m = nc.tensor
        e.wait_ge(f["a0_krows"].sem, f["a0_krows"](1))
        for j in range(NT):
            i = m.transpose(g.ps[:, 4, P * j:P * j + P], kn[:, j, :], g.ident)
        i.then_inc(f["a0_KT"].sem, 1)
        ln1["pe"](e)
        ln2["pe"](e)
        e.wait_ge(f["a0_rows"].sem, f["a0_rows"](1))
        for j in range(NT):
            i = m.transpose(g.ps[:, 5, P * j:P * j + P], rows[:, j, :], g.ident)
        i.then_inc(f["a0_QT"].sem, 1)
        e.wait_ge(f["a0_QT_sb"].sem, f["a0_QT_sb"](1))
        e.wait_ge(f["a0_KT_sb"].sem, f["a0_KT_sb"](1))
        for j in range(NI):
            i = m.matmul(g.ps[:, j, :], KT[:, P * j:P * j + P], QT, start=True, stop=True)
        i.then_inc(f["a0_s"].sem, 1)
        e.wait_ge(f["a0_B"].sem, f["a0_B"](1))
        for j in range(NT):
            for c_ in range(NI):
                i = m.matmul(g.ps[:, 6, P * j:P * j + P], t[:, TOK * c_ + P * j:TOK * c_ + P * j + P], qw[:, c_, :],
                             start=c_ == 0, stop=c_ == NI - 1)
        i.then_inc(f["a0_X"].sem, 1)

    return dict(load=load, sp=nothing, dve=dve, act=act, pe=pe, pool=nothing)


def nothing(e):
    pass


def global_max(g, src, n, dst, bank):
    f = flags(g, max_in=1, max_T=1, max_row=1, max_all=1)
    fin, fT, frow, fall = f["max_in"], f["max_T"], f["max_row"], f["max_all"]

    def pe(e):
        e.wait_ge(fin.sem, fin(1))
        g.nc.tensor.transpose(g.ps[0:1, bank, 0:n], src[0:n, :], g.ident[0:n, 0:n]).then_inc(fT.sem, 1)
        e.wait_ge(frow.sem, frow(1))
        g.nc.tensor.matmul(g.ps[:, bank, 128:129], g.ones[0:1, :], g.one_max, start=True, stop=True).then_inc(fall.sem, 1)

    def dve(e):
        e.wait_ge(fT.sem, fT(1))
        g.nc.vector.tensor_reduce(g.one_max, g.ps[0:1, bank, 0:n], AX.X, ALU.max).then_inc(frow.sem, 1)
        e.wait_ge(fall.sem, fall(1))
        g.link["dve"](g.nc.vector.tensor_copy(dst, g.ps[:, bank, 128:129]))
    return dict(pe=pe, dve=dve, ready=fin)


def layer_l0_quant_ffn(g):
    nc = g.nc
    tmp = g.temps()
    IC, NI = 88, 4
    w = g.slot[0]
    wg, wu = (w[0:IC, NI * D * i:NI * D * (i + 1)].rearrange("p (c d) -> p c d", d=D) for i in range(2))
    wd = w[:, 2 * NI * D:2 * NI * D + IC * NI]
    wgT, wuT = tmp.take(IC * NI, BF16), tmp.take(IC * NI, BF16)
    wdT = tmp.take(NI * D, BF16)
    swg, swu, iwg, iwu, sgx, sux = (tmp.take(NI)[0:IC, :] for _ in range(6))
    swd, iwd, sx, isx, sh, ish, gm, sig, amax, sdn = (tmp.take(1) for _ in range(10))
    sg2 = tmp.take(2)
    g.one_max = tmp.take(1)[0:1, :]
    xiT = tmp.take(TOK, BF16)
    sg = tmp.take(NI * TOK)[0:IC, :].rearrange("p (c n) -> p c n", c=NI)
    h = tmp.take(NI * TOK)[0:IC, :]
    hi = tmp.take(NI * TOK, BF16)[0:IC, :]
    yT = tmp.take(TOK)
    ln1 = layernorm(g, g.x, g.xn)
    f = steps(g, flags(g, f0_w_in=48), rows_ready="f0_wq f0_xi", rows_T="f0_wT f0_xiT", T_ready="f0_xiT_sb",
              products="f0_gu f0_y", act_step="f0_sig_e f0_silu", dve_step="f0_scale f0_hi f0_yT")
    gmx = global_max(g, amax, P, gm, 5)
    gmh = global_max(g, amax, IC, gm, 5)
    back = add_back(g, yT, f["f0_yT"])
    xrows = g.xn2d

    def load(e):
        wait_slot(g, e, 2)
        for dst, name in ((wg, "L0_ffn_w_gate"), (wu, "L0_ffn_w_up")):
            e.dma_start(dst, g.a[name].rearrange("(c p) d -> p c d", p=IC)).then_inc(f["f0_w_in"].sem, 16)
        e.dma_start(wd, g.a["L0_ffn_w_down"]).then_inc(f["f0_w_in"].sem, 16)

    def round_(v, ap, out, inv=None):
        ln = g.link["dve"]
        if inv is not None:
            ln(v.tensor_scalar(ap, ap, inv, -128.0, ALU.mult, ALU.max))
        else:
            ln(v.tensor_scalar(ap, ap, -128.0, None, ALU.max))
        ln(v.tensor_scalar(ap, ap, 127.0, HALF_ULP, ALU.min, ALU.add))
        return v.tensor_scalar(out, ap, HALF_ULP, None, ALU.subtract)

    def dve(e):
        ln, v = g.link["dve"], nc.vector
        e.wait_ge(f["f0_w_in"].sem, f["f0_w_in"](48))
        for wt, sw, iw in ((wg, swg, iwg), (wu, swu, iwu)):
            ln(v.tensor_reduce(iw, wt, AX.X, ALU.max, apply_absolute_value=True))
            ln(v.tensor_scalar(sw, iw, 1.0 / 127.0, None, ALU.mult))
            ln(v.reciprocal(iw, sw))
            for c in range(NI):
                i = v.tensor_scalar(wt[:, c, :], wt[:, c, :], iw[:, c:c + 1], None, ALU.mult)
            ln(i)
            ln(round_(v, wt, wt))
        ln(v.tensor_reduce(iwd, wd, AX.X, ALU.max, apply_absolute_value=True))
        ln(v.tensor_scalar(swd, iwd, 1.0 / 127.0, None, ALU.mult))
        ln(v.reciprocal(iwd, swd))
        round_(v, wd, wd, iwd).then_inc(f["f0_wq"].sem, 1)
        e.wait_ge(f["f0_wT"].sem, f["f0_wT"](1))
        v.tensor_copy(wgT, g.ps[:, 0, 0:IC * NI])
        v.tensor_copy(wuT, g.ps[:, 1, 0:IC * NI])
        ln(v.tensor_copy(wdT[0:IC, :], g.ps[0:IC, 2, :]))
        e.wait_ge(f["f0_sig_e"].sem, f["f0_sig_e"](1))
        ln(v.tensor_scalar(sg2, sg2, 1.0, None, ALU.add))
        ln(v.reciprocal(sg2, sg2))
        ln(v.tensor_scalar(sg2, sg2, 1.0 / 127.0, None, ALU.mult))
        ln1["dve"](e)
        v.tensor_reduce(amax, xrows, AX.X, ALU.max, apply_absolute_value=True).then_inc(gmx["ready"].sem, 1)
        gmx["dve"](e)
        ln(v.tensor_scalar(sx, gm, sg2[:, 0:1], None, ALU.mult))
        ln(v.reciprocal(isx, sx))
        round_(v, xrows, xrows, isx).then_inc(f["f0_xi"].sem, 1)
        e.wait_ge(f["f0_xiT"].sem, f["f0_xiT"](1))
        v.tensor_copy(xiT, g.ps[:, 6, :]).then_inc(f["f0_xiT_sb"].sem, 1)
        v.tensor_scalar(sgx, swg, sx[0:IC, :], None, ALU.mult)
        v.tensor_scalar(sux, swu, sx[0:IC, :], None, ALU.mult).then_inc(f["f0_scale"].sem, 1)
        e.wait_ge(f["f0_scale"].sem, f["f0_scale"](1))
        e.wait_ge(f["f0_silu"].sem, f["f0_silu"](1))
        for c in range(NI):
            i = v.scalar_tensor_tensor(out=h[:, TOK * c:TOK * c + TOK], in0=g.ps[0:IC, 4 + c, :], scalar=sux[:, c:c + 1],
                                       in1=sg[:, c, :], op0=ALU.mult, op1=ALU.mult)
        ln(i)
        v.tensor_reduce(amax[0:IC, :], h, AX.X, ALU.max, apply_absolute_value=True).then_inc(gmh["ready"].sem, 1)
        gmh["dve"](e)
        ln(v.tensor_scalar(sh, gm, sg2[:, 1:2], None, ALU.mult))
        ln(v.reciprocal(ish, sh))
        ln(v.tensor_scalar(sdn, swd, sh, None, ALU.mult))
        round_(v, h, hi, ish[0:IC, :]).then_inc(f["f0_hi"].sem, 1)
        e.wait_ge(f["f0_y"].sem, f["f0_y"](1))
        v.tensor_scalar(yT, g.ps[:, 0, :], sdn, None, ALU.mult).then_inc(f["f0_yT"].sem, 1)
        back["dve"](e)

    def act(e):
        s = nc.scalar
        e.wait_ge(g.flag["x_done"].sem, 2)
        s.activation(sg2, g.scal[:, 0:16:8], ACT.Exp, scale=-1.0).then_inc(f["f0_sig_e"].sem, 1)
        ln1["act"](e)
        e.wait_ge(f["f0_gu"].sem, f["f0_gu"](1))
        e.wait_ge(f["f0_scale"].sem, f["f0_scale"](1))
        for c in range(NI):
            i = s.activation(sg[:, c, :], g.ps[0:IC, c, :], ACT.Silu, scale=sgx[:, c:c + 1])
        i.then_inc(f["f0_silu"].sem, 1)

    def pe(e):
        m = nc.tensor
        e.wait_ge(f["f0_wq"].sem, f["f0_wq"](1))
        for c in range(NI):
            m.transpose(g.ps[:, 0, IC * c:IC * c + IC], wg[:, c, :], g.ident[0:IC, 0:IC])
            m.transpose(g.ps[:, 1, IC * c:IC * c + IC], wu[:, c, :], g.ident[0:IC, 0:IC])
            i = m.transpose(g.ps[0:IC, 2, D * c:D * c + D], wd[:, IC * c:IC * c + IC], g.ident)
        i.then_inc(f["f0_wT"].sem, 1)
        ln1["pe"](e)
        gmx["pe"](e)
        e.wait_ge(f["f0_xi"].sem, f["f0_xi"](1))
        for t in range(NT):
            i = m.transpose(g.ps[:, 6, P * t:P * t + P], g.xn[:, t, :], g.ident)
        i.then_inc(f["f0_xiT"].sem, 1)
        e.wait_ge(f["f0_xiT_sb"].sem, f["f0_xiT_sb"](1))
        for c in range(NI):
            m.matmul(g.ps[0:IC, c, :], wgT[:, IC * c:IC * c + IC], xiT, start=True, stop=True)
        for c in range(NI):
            i = m.matmul(g.ps[0:IC, 4 + c, :], wuT[:, IC * c:IC * c + IC], xiT, start=True, stop=True)
        i.then_inc(f["f0_gu"].sem, 1)
        gmh["pe"](e)
        e.wait_ge(f["f0_hi"].sem, f["f0_hi"](1))
        for c in range(NI):
            i = m.matmul(g.ps[:, 0, :], wdT[0:IC, D * c:D * c + D], hi[:, TOK * c:TOK * c + TOK], start=c == 0, stop=c == NI - 1)
        i.then_inc(f["f0_y"].sem, 1)
        back["pe"](e)

    return dict(load=load, sp=nothing, dve=dve, act=act, pe=pe, pool=nothing)


def start_layer(g, e, layer):
    e.wait_ge(g.flag["x_done"].sem, layer)


def cross_attention(g, layer, slot, names):
    nc = g.nc
    tmp = g.temps()
    H, DH = 16, 64
    PAIRS = H // 2
    R = H * S
    NR = R // P
    HB = R // BANK
    SCALE = DH ** -0.5
    w = g.slot[slot]
    wq, wk, wv = w[:, 0:R], w[0:DC, R:2 * R], w[0:DC, 2 * R:3 * R]
    wo = w[:, 3 * R:4 * R].rearrange("p (j n) -> p j n", j=PAIRS)
    G_ = g.pre[:, 0:H * DC]
    N_ = g.pre[0:DC, H * DC:H * DC + H * P]
    wT = [tmp.take(P + 2 * DC) for _ in range(2)]
    qh = [tmp.take(R, BF16) for _ in range(2)]
    ql = [tmp.take(R, BF16) for _ in range(2)]
    pf = [tmp.take(R) for _ in range(2)]
    ph = [tmp.take(R, BF16) for _ in range(2)]
    pl = [tmp.take(R, BF16) for _ in range(2)]
    pm = tmp.take(4 * NR).rearrange("p (j s) -> p j s", s=4)
    m = tmp.take(NR)
    mrow = tmp.take(P, BF16)[0:NR, :]
    pc = tmp.take(R)
    rz = tmp.take(R)[96:97, :]
    pcn = tmp.take(R)
    yT = tmp.take(TOK)
    ln1 = layernorm(g, g.x, g.xn, out_T=g.xnT)
    f = flags(g, x_w_in=64, x_wT=PAIRS, x_wT_sb=PAIRS, x_GN=PAIRS, x_GN_sb=PAIRS, x_zero=1, x_qk=B, x_qh=B, x_ql=B, x_unit=4 * NR * B,
              x_red=4 * NR * B, x_m=B, x_mT=B, x_mrow=B, x_m_in=16 * B, x_s=NCH * B, x_ph=NCH * B, x_pf=NCH * B, x_pl=NCH * B,
              x_pv=NCH * B, x_pc=B, x_rz=B, x_bc=B, x_pcn=B, x_y=B, x_y_sb=B)
    all_y = Flag(f["x_y_sb"].sem)
    all_y.base = f["x_y_sb"](B - 1)
    back = add_back(g, yT, all_y)
    S_ = [g.ps[:, 2 * i:2 * i + 2, :].rearrange("p a n -> p (a n)") for i in range(2)]
    ACC = g.ps[:, 4:6, :].rearrange("p a n -> p (a n)")
    MX = g.ps[:, 6:8, :].rearrange("p a n -> p (a n)")
    UNITS = {4: 5, 5: 5, 6: 5, 7: 5, 8: 4, 9: 4, 10: 4}
    assert sum(UNITS.values()) == 4 * NR

    def load(e):
        wait_slot(g, e, layer)
        e.dma_start(wq, g.a[names[0]]).then_inc(f["x_w_in"].sem, 16)
        e.dma_start(wk, g.a[names[1]]).then_inc(f["x_w_in"].sem, 16)
        e.dma_start(wv, g.a[names[2]]).then_inc(f["x_w_in"].sem, 16)
        e.dma_start(wo, g.a[names[3]].rearrange("(j p) n -> p j n", p=P)).then_inc(f["x_w_in"].sem, 16)

    def sp(e):
        for b in range(B):
            e.wait_ge(f["x_mrow"].sem, f["x_mrow"](b + 1))
            if b >= 2:
                e.wait_ge(f["x_s"].sem, f["x_s"](NCH * (b - 1)))
            e.dma_start(qh[b % 2][96:97, :], mrow).then_inc(f["x_m_in"].sem, 16)

    def pool(e):
        ln = g.link["pool"]
        start_layer(g, e, layer)
        ln(nc.gpsimd.memset(ql[0][96:97, :], 0.0))
        nc.gpsimd.memset(ql[1][96:97, :], 0.0).then_inc(f["x_zero"].sem, 1)
        for b in range(B):
            for c in range(NCH):
                k = NCH * b + c
                n = P if c < FULL else LASTK
                e.wait_ge(f["x_ph"].sem, f["x_ph"](k + 1))
                e.wait_ge(f["x_pf"].sem, f["x_pf"](k + 1))
                if k >= 2:
                    e.wait_ge(f["x_pv"].sem, f["x_pv"](k - 1))
                nc.gpsimd.tensor_tensor(pl[k % 2][0:n, :], pf[k % 2][0:n, :], ph[k % 2][0:n, :], ALU.subtract).then_inc(f["x_pl"].sem, 1)

    def act(e):
        s, ln = nc.scalar, g.link["act"]
        start_layer(g, e, layer)
        for j in range(PAIRS):
            e.wait_ge(f["x_wT"].sem, f["x_wT"](j + 1))
            if j >= 2:
                e.wait_ge(f["x_GN"].sem, f["x_GN"](j - 1))
            s.activation(wT[j % 2], g.ps[:, j % 2, 0:P + 2 * DC], ACT.Copy).then_inc(f["x_wT_sb"].sem, 1)
        ln1["act"](e)

        def q_high(b):
            e.wait_ge(f["x_qk"].sem, f["x_qk"](b + 1))
            if b >= 2:
                e.wait_ge(f["x_s"].sem, f["x_s"](NCH * (b - 1)))
            s.activation(qh[b % 2][0:DC, :], MX[0:DC, :], ACT.Copy).then_inc(f["x_qh"].sem, 1)

        def sums(b):
            e.wait_ge(f["x_pc"].sem, f["x_pc"](b + 1))
            if b >= 1:
                e.wait_ge(f["x_bc"].sem, f["x_bc"](b))
            ln(s.activation(rz, pc[96:97, :], ACT.Ln))
            s.activation(rz, rz, ACT.Exp, scale=-1.0).then_inc(f["x_rz"].sem, 1)

        q_high(0)
        for b in range(B):
            for c in range(NCH):
                k = NCH * b + c
                n = P if c < FULL else LASTK
                if c == 1 and b >= 1:
                    sums(b - 1)
                if c == 3 and b + 1 < B:
                    q_high(b + 1)
                e.wait_ge(f["x_s"].sem, f["x_s"](k + 1))
                if k >= 2:
                    e.wait_ge(f["x_pv"].sem, f["x_pv"](k - 1))
                    e.wait_ge(f["x_pl"].sem, f["x_pl"](k - 1))
                s.activation(ph[k % 2][0:n, :], S_[k % 2][0:n, :], ACT.Exp).then_inc(f["x_ph"].sem, 1)
                s.activation(pf[k % 2][0:n, :], S_[k % 2][0:n, :], ACT.Exp).then_inc(f["x_pf"].sem, 1)
        sums(B - 1)

    def dve(e):
        v, ln = nc.vector, g.link["dve"]
        for j in range(PAIRS):
            e.wait_ge(f["x_GN"].sem, f["x_GN"](j + 1))
            for o in range(2):
                h = 2 * j + o
                bank = g.ps[:, 2 + 2 * (j % 2) + o, :]
                v.tensor_scalar(G_[:, DC * h:DC * h + DC], bank[:, 0:DC], SCALE, None, ALU.mult)
                i = v.tensor_copy(N_[:, P * h:P * h + P], bank[0:DC, P:2 * P])
            i.then_inc(f["x_GN_sb"].sem, 1)
        ln1["dve"](e)

        def q_low(b):
            e.wait_ge(f["x_qh"].sem, f["x_qh"](b + 1))
            v.tensor_tensor(ql[b % 2][0:DC, :], MX[0:DC, :], qh[b % 2][0:DC, :], ALU.subtract).then_inc(f["x_ql"].sem, 1)

        def units(b, first, count):
            for u in range(first, first + count):
                k = 4 * NR * b + u
                n = KSPAN[u % 4][1]
                e.wait_ge(f["x_unit"].sem, f["x_unit"](k + 1))
                v.tensor_reduce(pm[:, u // 4, u % 4:u % 4 + 1], MX[:, BANK * (u % 2):BANK * (u % 2) + n], AX.X, ALU.max).then_inc(f["x_red"].sem, 1)

        def row_max(b):
            e.wait_ge(f["x_red"].sem, f["x_red"](4 * NR * (b + 1)))
            v.tensor_reduce(m, pm, AX.X, ALU.max).then_inc(f["x_m"].sem, 1)
            e.wait_ge(f["x_mT"].sem, f["x_mT"](b + 1))
            if b >= 1:
                e.wait_ge(f["x_m_in"].sem, f["x_m_in"](16 * b))
            v.tensor_scalar(mrow, MX[0:NR, 0:P], -1.0, None, ALU.mult).then_inc(f["x_mrow"].sem, 1)

        def acc_out(b):
            e.wait_ge(f["x_pv"].sem, f["x_pv"](NCH * (b + 1)))
            v.tensor_copy(pc[0:DC + 1, :], ACC[0:DC + 1, :]).then_inc(f["x_pc"].sem, 1)

        def norm(b):
            e.wait_ge(f["x_bc"].sem, f["x_bc"](b + 1))
            v.tensor_tensor(pcn[0:DC, :], pc[0:DC, :], MX[0:DC, :], ALU.mult).then_inc(f["x_pcn"].sem, 1)

        def y_out(b):
            e.wait_ge(f["x_y"].sem, f["x_y"](b + 1))
            v.tensor_scalar(yT[:, S * b:S * b + S], MX[:, 0:S], g.col(names[4]), None, ALU.add).then_inc(f["x_y_sb"].sem, 1)

        q_low(0)
        units(0, 0, 4 * NR)
        row_max(0)
        for b in range(B):
            done = 0
            for c in range(NCH):
                if c == 1 and b >= 1:
                    norm(b - 1)
                if c == 2 and b >= 1:
                    y_out(b - 1)
                if b + 1 < B:
                    if c == 3:
                        q_low(b + 1)
                    if c in UNITS:
                        units(b + 1, done, UNITS[c])
                        done += UNITS[c]
                    if c == 11:
                        row_max(b + 1)
            acc_out(b)
        norm(B - 1)
        y_out(B - 1)
        back["dve"](e)

    def pe(e):
        t = nc.tensor
        start_layer(g, e, layer)
        e.wait_ge(f["x_w_in"].sem, f["x_w_in"](64))
        for j in range(PAIRS):
            if j >= 2:
                e.wait_ge(f["x_wT_sb"].sem, f["x_wT_sb"](j - 1))
            t.transpose(g.ps[:, j % 2, 0:P], wq[:, P * j:P * j + P], g.ident)
            t.transpose(g.ps[:, j % 2, P:P + DC], wk[:, P * j:P * j + P], g.ident[0:DC, 0:DC])
            t.transpose(g.ps[:, j % 2, P + DC:P + 2 * DC], wv[:, P * j:P * j + P], g.ident[0:DC, 0:DC]).then_inc(f["x_wT"].sem, 1)
            e.wait_ge(f["x_wT_sb"].sem, f["x_wT_sb"](j + 1))
            if j >= 2:
                e.wait_ge(f["x_GN_sb"].sem, f["x_GN_sb"](j - 1))
            for o in range(2):
                r = slice(DH * o, DH * o + DH)
                bank = g.ps[:, 2 + 2 * (j % 2) + o, :]
                t.matmul(bank[:, 0:DC], wT[j % 2][r, 0:P], wT[j % 2][r, P:P + DC], start=True, stop=True)
                i = t.matmul(bank[0:DC, P:2 * P], wT[j % 2][r, P + DC:P + 2 * DC], wo[r, j, :], start=True, stop=True)
            i.then_inc(f["x_GN"].sem, 1)
        ln1["pe"](e)
        e.wait_ge(ln1["ready"].sem, ln1["ready"](1))
        e.wait_ge(f["x_GN_sb"].sem, f["x_GN_sb"](PAIRS))
        e.wait_ge(f["x_zero"].sem, f["x_zero"](1))

        def qk(b):
            if b >= 2:
                e.wait_ge(f["x_y_sb"].sem, f["x_y_sb"](b - 1))
            for h in range(H):
                i = t.matmul(MX[0:DC, S * h:S * h + S], G_[:, DC * h:DC * h + DC], g.xnT[:, S * b:S * b + S], start=True, stop=True)
            i.then_inc(f["x_qk"].sem, 1)

        def units(b, first, count):
            for u in range(first, first + count):
                k = 4 * NR * b + u
                a, n = KSPAN[u % 4]
                if u < 2:
                    e.wait_ge(f["x_ql"].sem, f["x_ql"](b + 1))
                else:
                    e.wait_ge(f["x_red"].sem, f["x_red"](k - 1))
                t.matmul(MX[:, BANK * (u % 2):BANK * (u % 2) + n], qh[b % 2][0:DC, P * (u // 4):P * (u // 4) + P],
                         g.cT_hi[0:DC, b, a:a + n], start=True, stop=True).then_inc(f["x_unit"].sem, 1)

        def max_T(b):
            e.wait_ge(f["x_m"].sem, f["x_m"](b + 1))
            t.transpose(MX[0:NR, 0:P], m, g.ident).then_inc(f["x_mT"].sem, 1)

        def bcast(b):
            e.wait_ge(f["x_rz"].sem, f["x_rz"](b + 1))
            e.wait_ge(f["x_mrow"].sem, f["x_mrow"](min(b + 2, B)))
            for q in range(HB):
                i = t.matmul(MX[0:DC, BANK * q:BANK * q + BANK], g.ones[96:97, 0:DC], rz[:, BANK * q:BANK * q + BANK], start=True, stop=True)
            i.then_inc(f["x_bc"].sem, 1)

        def y(b):
            e.wait_ge(f["x_pcn"].sem, f["x_pcn"](b + 1))
            for h in range(H):
                i = t.matmul(MX[:, 0:S], N_[:, P * h:P * h + P], pcn[0:DC, S * h:S * h + S], start=h == 0, stop=h == H - 1)
            i.then_inc(f["x_y"].sem, 1)

        def weighted(b, c):
            k = NCH * b + c
            n = P if c < FULL else LASTK
            e.wait_ge(f["x_ph"].sem, f["x_ph"](k + 1))
            if c == 0 and b >= 1:
                e.wait_ge(f["x_pc"].sem, f["x_pc"](b))
            hi, lo = g.cr_hi[0:n, b, c, :], g.cr_lo[0:n, b, c, :]
            for j, (lhs, p) in enumerate(((hi, ph), (lo, ph), (hi, pl))):
                if j == 2:
                    e.wait_ge(f["x_pl"].sem, f["x_pl"](k + 1))
                for q in range(HB):
                    i = t.matmul(ACC[0:DC + 1, BANK * q:BANK * q + BANK], lhs, p[k % 2][0:n, BANK * q:BANK * q + BANK],
                                 start=c == 0 and j == 0, stop=c == NCH - 1 and j == 2)
            i.then_inc(f["x_pv"].sem, 1)

        qk(0)
        units(0, 0, 4 * NR)
        max_T(0)
        for b in range(B):
            done = 0
            e.wait_ge(f["x_m_in"].sem, f["x_m_in"](16 * (b + 1)))
            for c in range(NCH):
                k = NCH * b + c
                n = P if c < FULL else LASTK
                if k >= 2:
                    e.wait_ge(f["x_pf"].sem, f["x_pf"](k - 1))
                hi, lo = g.cT_hi[0:DC + 1, b, P * c:P * c + n], g.cT_lo[0:DC + 1, b, P * c:P * c + n]
                for j, (lhs, q_) in enumerate(((hi, qh), (lo, qh), (hi, ql))):
                    for q in range(HB):
                        i = t.matmul(S_[k % 2][0:n, BANK * q:BANK * q + BANK], lhs, q_[b % 2][0:DC + 1, BANK * q:BANK * q + BANK],
                                     start=j == 0, stop=j == 2)
                i.then_inc(f["x_s"].sem, 1)
                if b >= 1 and c == 1:
                    bcast(b - 1)
                if b >= 1 and c == 2:
                    y(b - 1)
                if b + 1 < B:
                    if c == 3:
                        qk(b + 1)
                    if c in UNITS:
                        units(b + 1, done, UNITS[c])
                        done += UNITS[c]
                    if c == 11:
                        max_T(b + 1)
                if c >= 1:
                    weighted(b, c - 1)
            weighted(b, NCH - 1)
        bcast(B - 1)
        y(B - 1)
        back["pe"](e)

    return dict(load=load, sp=sp, dve=dve, act=act, pe=pe, pool=pool)


def layer_l1_cross(g):
    return cross_attention(g, 3, 1, ("L1_xattn_Wq", "L1_xattn_Wk", "L1_xattn_Wv", "L1_xattn_Wo", "l1x_bo"))


HG = 4
NG = 16 // HG


def self_attention(g, tmp, scores_of, value_of, out_of, soft, prep_pe=None, prep_act=None, prep_dve=None, itau=None, nthr=None):
    nc = g.nc
    GC = HG * P
    KG = NT * NG
    sm = [tmp.take(GC).rearrange("p (h k) -> p h k", h=HG) for _ in range(2)]
    pr = [tmp.take(GC).rearrange("p (h k) -> p h k", h=HG) for _ in range(3)]
    pT = [tmp.take(GC).rearrange("p (h k) -> p h k", h=HG) for _ in range(2)]
    mx = [tmp.take(HG) for _ in range(2)]
    nm = [tmp.take(HG) for _ in range(2)]
    z = [tmp.take(HG) for _ in range(2)]
    zi = [tmp.take(HG) for _ in range(2)]
    f = flags(g, s_scores=KG, s_masked=KG, s_prob=KG, s_zinv=KG, s_norm=KG, s_T=KG, s_T_sb=KG, s_out=KG)

    def bank(i):
        return g.ps[:, i, :].rearrange("p (h k) -> p h k", h=HG)

    def wide(m):
        return m[:, None, :].to_broadcast([P, HG, P])

    def pe(e):
        t = nc.tensor
        for k in range(KG + 3):
            if k < KG:
                if prep_pe:
                    prep_pe(e, k)
                if k >= 2:
                    e.wait_ge(f["s_masked"].sem, f["s_masked"](k - 1))
                for h in range(HG):
                    lhs, rhs = scores_of(k, h)
                    i = t.matmul(bank(k % 2)[:, h, :], lhs, rhs, start=True, stop=True)
                i.then_inc(f["s_scores"].sem, 1)
            if 0 <= k - 2 < KG:
                q = k - 2
                e.wait_ge(f["s_norm"].sem, f["s_norm"](q + 1))
                if q >= 2:
                    e.wait_ge(f["s_T_sb"].sem, f["s_T_sb"](q - 1))
                for h in range(HG):
                    i = t.transpose(bank(2 + q % 2)[:, h, :], pr[q % 3][:, h, :], g.ident)
                i.then_inc(f["s_T"].sem, 1)
            if 0 <= k - 3 < KG:
                q = k - 3
                e.wait_ge(f["s_T_sb"].sem, f["s_T_sb"](q + 1))
                for h in range(HG):
                    dst, start, stop = out_of(q, h)
                    i = t.matmul(dst, pT[q % 2][:, h, :], value_of(q, h), start=start, stop=stop)
                i.then_inc(f["s_out"].sem, 1)

    def dve(e):
        v, ln = nc.vector, g.link["dve"]

        def sums(q):
            e.wait_ge(f["s_prob"].sem, f["s_prob"](q + 1))
            if soft is None:
                if q >= 3:
                    e.wait_ge(f["s_T"].sem, f["s_T"](q - 2))
                ln(v.scalar_tensor_tensor(out=pr[q % 3], in0=pr[q % 3], scalar=1.0, in1=wide(g.neg_blk), op0=ALU.subtract, op1=ALU.mult))
                ln(v.tensor_reduce(z[q % 2], pr[q % 3], AX.X, ALU.add))
                ln(v.tensor_scalar(z[q % 2], z[q % 2], 1e-6, None, ALU.add))
            if q >= 2:
                e.wait_ge(f["s_norm"].sem, f["s_norm"](q - 1))
            v.reciprocal(zi[q % 2], z[q % 2]).then_inc(f["s_zinv"].sem, 1)

        for k in range(KG):
            if prep_dve:
                prep_dve(e, k)
            if k >= 1:
                sums(k - 1)
            e.wait_ge(f["s_scores"].sem, f["s_scores"](k + 1))
            if k >= 2:
                e.wait_ge(f["s_prob"].sem, f["s_prob"](k - 1))
            if soft is not None:
                ln(v.tensor_tensor(sm[k % 2], bank(k % 2), wide(soft), ALU.add))
                ln(v.tensor_reduce(mx[k % 2], sm[k % 2], AX.X, ALU.max))
                v.tensor_scalar(nm[k % 2], mx[k % 2], -1.0, None, ALU.mult).then_inc(f["s_masked"].sem, 1)
            else:
                ln(v.tensor_tensor(sm[k % 2], bank(k % 2), wide(g.tri_mul), ALU.mult))
                v.tensor_tensor(sm[k % 2], sm[k % 2], wide(g.tri_add), ALU.add).then_inc(f["s_masked"].sem, 1)
        sums(KG - 1)

    def act(e):
        s, ln = nc.scalar, g.link["act"]
        for k in range(KG + 2):
            if k < KG:
                if prep_act:
                    prep_act(e, k)
                e.wait_ge(f["s_masked"].sem, f["s_masked"](k + 1))
                if k >= 3:
                    e.wait_ge(f["s_T"].sem, f["s_T"](k - 2))
                if k >= 2:
                    e.wait_ge(f["s_zinv"].sem, f["s_zinv"](k - 1))
                for h in range(HG):
                    if soft is not None:
                        i = s.activation(pr[k % 3][:, h, :], sm[k % 2][:, h, :], ACT.Exp, bias=nm[k % 2][:, h:h + 1],
                                         accum_out=z[k % 2][:, h:h + 1])
                    else:
                        hh = HG * (k % NG) + h
                        i = s.activation(pr[k % 3][:, h, :], sm[k % 2][:, h, :], ACT.Tanh, bias=nthr[:, hh:hh + 1],
                                         scale=itau[:, hh:hh + 1])
                if soft is None:
                    ln(i)
                    i = s.activation(pr[k % 3], pr[k % 3], ACT.Square)
                i.then_inc(f["s_prob"].sem, 1)
            if 0 <= k - 2 < KG:
                q = k - 2
                e.wait_ge(f["s_T"].sem, f["s_T"](q + 1))
                if q >= 2:
                    e.wait_ge(f["s_out"].sem, f["s_out"](q - 1))
                s.activation(pT[q % 2], bank(2 + q % 2), ACT.Copy).then_inc(f["s_T_sb"].sem, 1)

    def pool(e):
        for k in range(KG):
            e.wait_ge(f["s_zinv"].sem, f["s_zinv"](k + 1))
            nc.gpsimd.tensor_tensor(pr[k % 3], pr[k % 3], zi[k % 2][:, :, None].to_broadcast([P, HG, P]), ALU.mult).then_inc(f["s_norm"].sem, 1)
    return dict(pe=pe, dve=dve, act=act, pool=pool, out=f["s_out"], f=f, KG=KG)


def layer_l1_self(g):
    nc = g.nc
    tmp = g.temps()
    H, DH = 16, 64
    PAIRS = H // 2
    w = g.slot[0]
    wq, wk, wv = (w[:, PAIRS * D * i:PAIRS * D * (i + 1)].rearrange("p (j d) -> p j d", d=D) for i in range(3))
    wo = w[:, 3 * PAIRS * D:4 * PAIRS * D]
    M_ = g.pre[:, 0:H * D]
    N_ = g.pre[:, H * D:2 * H * D]
    woT = [tmp.take(P) for _ in range(2)]
    tT = [tmp.take(HG * P) for _ in range(2)]
    vN = [tmp.take(HG * P) for _ in range(4)]
    ln1 = layernorm(g, g.x, g.xn, out_T=g.xnT)
    KG = NT * NG
    f = flags(g, l1_w_in=64, x_wT=PAIRS, x_wT_sb=PAIRS, x_GN=PAIRS, x_GN_sb=PAIRS, p_t=KG, p_t_sb=KG, p_v=KG, p_v_sb=KG)

    def tile(k):
        return slice(P * (k // NG), P * (k // NG) + P)

    def prep_pe(e, k):
        t = nc.tensor
        hs = HG * (k % NG)
        if k >= 1:
            e.wait_ge(f["p_t_sb"].sem, f["p_t_sb"](k))
            e.wait_ge(f["p_v_sb"].sem, f["p_v_sb"](k))
        for h in range(HG):
            i = t.matmul(g.ps[:, 5, P * h:P * h + P], M_[:, D * (hs + h):D * (hs + h) + D], g.xnT[:, tile(k)], start=True, stop=True)
        i.then_inc(f["p_t"].sem, 1)
        t.matmul(g.ps[:, 6, :], g.xnT[:, tile(k)], N_[:, D * hs:D * (hs + HG)], start=True, stop=True).then_inc(f["p_v"].sem, 1)
        e.wait_ge(f["p_t_sb"].sem, f["p_t_sb"](k + 1))

    def prep_act(e, k):
        e.wait_ge(f["p_t"].sem, f["p_t"](k + 1))
        if k >= 2:
            e.wait_ge(core["f"]["s_scores"].sem, core["f"]["s_scores"](k - 1))
        nc.scalar.activation(tT[k % 2], g.ps[:, 5, :], ACT.Copy).then_inc(f["p_t_sb"].sem, 1)

    def prep_dve(e, k):
        e.wait_ge(f["p_v"].sem, f["p_v"](k + 1))
        if k >= 4:
            e.wait_ge(core["f"]["s_out"].sem, core["f"]["s_out"](k - 3))
        nc.vector.tensor_copy(vN[k % 4], g.ps[:, 6, :]).then_inc(f["p_v_sb"].sem, 1)

    core = self_attention(
        g, tmp, lambda k, h: (tT[k % 2][:, P * h:P * h + P], g.xnT[:, tile(k)]),
        lambda k, h: vN[k % 4][:, P * h:P * h + P],
        lambda k, h: (g.ps[:, 4, tile(k)], k % NG == 0 and h == 0, k % NG == NG - 1 and h == HG - 1),
        soft=g.mask_ca, prep_pe=prep_pe, prep_act=prep_act, prep_dve=prep_dve)
    last = Flag(core["out"].sem)
    last.base = core["out"](KG - 1)
    add = add_rows(g, 4, last)

    def load(e):
        wait_slot(g, e, 4)
        for dst, name in ((wq, "L1_attn_w_q"), (wk, "L1_attn_w_k"), (wv, "L1_attn_w_v")):
            e.dma_start(dst, g.a[name].rearrange("h q d -> (h q) d").rearrange("(j p) d -> p j d", p=P)).then_inc(f["l1_w_in"].sem, 16)
        e.dma_start(wo, g.a["L1_attn_w_o"]).then_inc(f["l1_w_in"].sem, 16)

    def pe(e):
        t = nc.tensor
        start_layer(g, e, 4)
        e.wait_ge(f["l1_w_in"].sem, f["l1_w_in"](64))
        for j in range(PAIRS):
            if j >= 2:
                e.wait_ge(f["x_wT_sb"].sem, f["x_wT_sb"](j - 1))
            t.transpose(g.ps[:, j % 2, 0:P], wo[:, P * j:P * j + P], g.ident).then_inc(f["x_wT"].sem, 1)
            e.wait_ge(f["x_wT_sb"].sem, f["x_wT_sb"](j + 1))
            if j >= 2:
                e.wait_ge(f["x_GN_sb"].sem, f["x_GN_sb"](j - 1))
            for o in range(2):
                r = slice(DH * o, DH * o + DH)
                bank = g.ps[:, 2 + 2 * (j % 2) + o, :]
                t.matmul(bank[:, 0:P], wq[r, j, :], wk[r, j, :], start=True, stop=True)
                i = t.matmul(bank[:, P:2 * P], wv[r, j, :], woT[j % 2][r, :], start=True, stop=True)
            i.then_inc(f["x_GN"].sem, 1)
        ln1["pe"](e)
        e.wait_ge(ln1["ready"].sem, ln1["ready"](1))
        e.wait_ge(f["x_GN_sb"].sem, f["x_GN_sb"](PAIRS))
        core["pe"](e)

    def act(e):
        start_layer(g, e, 4)
        for j in range(PAIRS):
            e.wait_ge(f["x_wT"].sem, f["x_wT"](j + 1))
            if j >= 2:
                e.wait_ge(f["x_GN"].sem, f["x_GN"](j - 1))
            nc.scalar.activation(woT[j % 2], g.ps[:, j % 2, 0:P], ACT.Copy).then_inc(f["x_wT_sb"].sem, 1)
        ln1["act"](e)
        core["act"](e)

    def dve(e):
        for j in range(PAIRS):
            e.wait_ge(f["x_GN"].sem, f["x_GN"](j + 1))
            for o in range(2):
                h = 2 * j + o
                bank = g.ps[:, 2 + 2 * (j % 2) + o, :]
                nc.vector.tensor_scalar(M_[:, D * h:D * h + D], bank[:, 0:P], DH ** -0.5, None, ALU.mult)
                i = nc.vector.tensor_copy(N_[:, D * h:D * h + D], bank[:, P:2 * P])
            i.then_inc(f["x_GN_sb"].sem, 1)
        ln1["dve"](e)
        core["dve"](e)
        add["dve"](e)

    def pool(e):
        start_layer(g, e, 4)
        core["pool"](e)
    return dict(load=load, sp=nothing, dve=dve, act=act, pe=pe, pool=pool)


def layer_l1_moe(g):
    nc = g.nc
    tmp = g.temps()
    E, FC = 8, 4
    K = E * FC
    EW = 3 * 512
    place = [g.slot[1], g.slot[0], g.pre, g.slot[1]]
    sg = [tmp.take(TOK) for _ in range(2)]
    hb = [tmp.take(TOK) for _ in range(3)]
    yT = g.pre[:, 2 * EW:2 * EW + TOK]
    ln1 = layernorm(g, g.x, g.xn, out_T=g.xnT)
    f = flags(g, m_w_in0=96, m_w_in1=96, m_w_in2=96, m_w_in3=96, m_gate=K, m_up=K, m_act=K, m_h=K, m_y=K)
    s4 = s4d_kernel(g, tmp)
    f = steps(g, f, dve_step="m_yT")
    arrived = [f["m_w_in0"], f["m_w_in1"], f["m_w_in2"], f["m_w_in3"]]
    back = add_back(g, yT, f["m_yT"])

    def views(x):
        w = place[x // 2][:, EW * (x % 2):EW * (x % 2) + EW]
        return w[:, 0:512], w[:, 512:1024], w[:, 1024:1536].rearrange("p (c d) -> p c d", d=D)

    def load_pair(e, p):
        for x in (2 * p, 2 * p + 1):
            wg, wu, wd = views(x)
            e.dma_start(wg, g.a["L1_ffn_Wg"][x]).then_inc(arrived[p].sem, 16)
            e.dma_start(wu, g.a["L1_ffn_Wu"][x]).then_inc(arrived[p].sem, 16)
            e.dma_start(wd, g.a["L1_ffn_Wd"][x].rearrange("(c p) d -> p c d", p=P)).then_inc(arrived[p].sem, 16)

    def load(e):
        wait_slot(g, e, 5)
        load_pair(e, 0)

    def sp(e):
        start_layer(g, e, 5)
        load_pair(e, 1)
        load_pair(e, 2)
        e.wait_ge(f["m_y"].sem, f["m_y"](2 * FC))
        load_pair(e, 3)
        e.wait_ge(f["m_y"].sem, f["m_y"](4 * FC))

    def pe(e):
        t = nc.tensor
        ln1["pe"](e)
        e.wait_ge(ln1["ready"].sem, ln1["ready"](1))
        for k in range(K + 2):
            if k < K:
                x, c = divmod(k, FC)
                wg, wu, _ = views(x)
                if x % 2 == 0 and c == 0:
                    e.wait_ge(arrived[x // 2].sem, arrived[x // 2](96))
                if k >= 2:
                    e.wait_ge(f["m_act"].sem, f["m_act"](k - 1))
                t.matmul(g.ps[:, k % 2, :], wg[:, P * c:P * c + P], g.xnT, start=True, stop=True).then_inc(f["m_gate"].sem, 1)
                if k >= 2:
                    e.wait_ge(f["m_h"].sem, f["m_h"](k - 1))
                t.matmul(g.ps[:, 2 + k % 2, :], wu[:, P * c:P * c + P], g.xnT, start=True, stop=True).then_inc(f["m_up"].sem, 1)
            if k >= 2:
                q = k - 2
                x, c = divmod(q, FC)
                e.wait_ge(f["m_h"].sem, f["m_h"](q + 1))
                t.matmul(g.ps[:, 4, :], views(x)[2][:, c, :], hb[q % 3], start=q == 0, stop=q == K - 1).then_inc(f["m_y"].sem, 1)
        back["pe"](e)

    def act(e):
        start_layer(g, e, 5)
        s4["act"](e)
        ln1["act"](e)
        for k in range(K):
            e.wait_ge(f["m_gate"].sem, f["m_gate"](k + 1))
            if k >= 2:
                e.wait_ge(f["m_h"].sem, f["m_h"](k - 1))
            nc.scalar.activation(sg[k % 2], g.ps[:, k % 2, :], ACT.Silu).then_inc(f["m_act"].sem, 1)

    def dve(e):
        s4["dve"](e)
        ln1["dve"](e)
        for k in range(K):
            e.wait_ge(f["m_act"].sem, f["m_act"](k + 1))
            e.wait_ge(f["m_up"].sem, f["m_up"](k + 1))
            if k >= 3:
                e.wait_ge(f["m_y"].sem, f["m_y"](k - 2))
            nc.vector.tensor_tensor(hb[k % 3], g.ps[:, 2 + k % 2, :], sg[k % 2], ALU.mult).then_inc(f["m_h"].sem, 1)
        s4["dve_end"](e)
        e.wait_ge(f["m_y"].sem, f["m_y"](K))
        nc.vector.tensor_copy(yT, g.ps[:, 4, :]).then_inc(f["m_yT"].sem, 1)
        back["dve"](e)

    def pool(e):
        start_layer(g, e, 5)
        s4["pool"](e)
    return dict(own_loads_first=True, load=load, sp=sp, dve=dve, act=act, pe=pe, pool=pool)


def s4d_kernel(g, tmp):
    nc = g.nc
    N = 64
    HL = S // 2
    ar, ai, cr, ci = (g.s4in[:, N * i:N * i + N] for i in range(4))
    Vr = tmp.take(HL * N).rearrange("p (l n) -> p l n", n=N)
    Vi = tmp.take(HL * N).rearrange("p (l n) -> p l n", n=N)
    T1 = tmp.take(HL * N).rearrange("p (l n) -> p l n", n=N)
    T2 = tmp.take(HL * N).rearrange("p (l n) -> p l n", n=N)
    small = T2.rearrange("p l n -> p (l n)")
    names = "re er th r1 r2 sn cs wr wi nr ni pr pi den t1 t2 w2r w2i".split()
    q = {n: small[:, N * i:N * i + N] for i, n in enumerate(names)}
    W = [T1.rearrange("p l n -> p (l n)")[:, 1024 + N * i:1024 + N * i + N] for i in range(2)]
    keep = g.pre[:, 4096 - 2 * N:4096]
    wr, wi = keep[:, 0:N], keep[:, N:2 * N]
    f = flags(g, s4_pool=1)
    f = steps(g, f, dve_step="s4_arg s4_start", act_step="s4_dt s4_trig")

    def act(e):
        s, ln = nc.scalar, g.link["act"]
        s.activation(g.s4dt, g.col("l3x_dt"), ACT.Exp).then_inc(f["s4_dt"].sem, 1)
        e.wait_ge(f["s4_arg"].sem, f["s4_arg"](1))
        s.activation(q["er"], q["re"], ACT.Exp)
        s.activation(q["sn"], q["r1"], ACT.Sin)
        s.activation(q["cs"], q["r2"], ACT.Sin).then_inc(f["s4_trig"].sem, 1)

    def reduce_angle(v, ln, out, src, shift):
        ln(v.tensor_scalar(q["t1"], src, 1.0 / (2.0 * PI), shift / (2.0 * PI), ALU.mult, ALU.add))
        ln(v.tensor_scalar(q["t1"], q["t1"], HALF_ULP, HALF_ULP, ALU.add, ALU.subtract))
        ln(v.scalar_tensor_tensor(out=q["t2"], in0=q["t1"], scalar=-6.28125, in1=src, op0=ALU.mult, op1=ALU.add))
        ln(v.scalar_tensor_tensor(out=q["t2"], in0=q["t1"], scalar=-(2.0 * PI - 6.28125), in1=q["t2"], op0=ALU.mult, op1=ALU.add))
        ln(v.tensor_scalar(out, q["t2"], shift, -3.1415925, ALU.add, ALU.max))
        return v.tensor_scalar(out, out, 3.1415925, None, ALU.min)

    def dve(e):
        v, ln = nc.vector, g.link["dve"]
        e.wait_ge(g.s4_sem, 64)
        e.wait_ge(f["s4_dt"].sem, f["s4_dt"](1))
        v.tensor_scalar(q["re"], ar, g.s4dt, None, ALU.mult)
        ln(v.tensor_scalar(q["th"], ai, g.s4dt, None, ALU.mult))
        ln(reduce_angle(v, ln, q["r1"], q["th"], 0.0))
        reduce_angle(v, ln, q["r2"], q["th"], PI / 2.0).then_inc(f["s4_arg"].sem, 1)
        e.wait_ge(f["s4_trig"].sem, f["s4_trig"](1))
        v.tensor_tensor(wr, q["er"], q["cs"], ALU.mult)
        ln(v.tensor_tensor(wi, q["er"], q["sn"], ALU.mult))
        ln(v.tensor_scalar(q["nr"], wr, -1.0, None, ALU.add))
        v.tensor_tensor(q["pr"], cr, q["nr"], ALU.mult)
        v.tensor_tensor(q["t1"], ci, wi, ALU.mult)
        v.tensor_tensor(q["pi"], cr, wi, ALU.mult)
        ln(v.tensor_tensor(q["t2"], ci, q["nr"], ALU.mult))
        v.tensor_tensor(q["pr"], q["pr"], q["t1"], ALU.subtract)
        ln(v.tensor_tensor(q["pi"], q["pi"], q["t2"], ALU.add))
        v.tensor_tensor(q["t1"], ar, ar, ALU.mult)
        ln(v.tensor_tensor(q["t2"], ai, ai, ALU.mult))
        ln(v.tensor_tensor(q["den"], q["t1"], q["t2"], ALU.add))
        ln(v.reciprocal(q["den"], q["den"]))
        v.tensor_tensor(q["t1"], q["pr"], ar, ALU.mult)
        ln(v.tensor_tensor(q["t2"], q["pi"], ai, ALU.mult))
        ln(v.tensor_tensor(q["t1"], q["t1"], q["t2"], ALU.add))
        ln(v.tensor_tensor(Vr[:, 0, :], q["t1"], q["den"], ALU.mult))
        v.tensor_tensor(q["t1"], q["pi"], ar, ALU.mult)
        ln(v.tensor_tensor(q["t2"], q["pr"], ai, ALU.mult))
        ln(v.tensor_tensor(q["t1"], q["t1"], q["t2"], ALU.subtract))
        v.tensor_tensor(Vi[:, 0, :], q["t1"], q["den"], ALU.mult).then_inc(f["s4_start"].sem, 1)
        e.wait_ge(f["s4_start"].sem, f["s4_start"](1))

    def pool(e):
        p, ln = nc.gpsimd, g.link["pool"]
        e.wait_ge(f["s4_start"].sem, f["s4_start"](1))
        m = 1
        while m <= HL:
            br = wr[:, None, :].to_broadcast([P, m, N])
            bi = wi[:, None, :].to_broadcast([P, m, N])
            src_r, src_i = Vr[:, 0:m, :], Vi[:, 0:m, :]
            if m == HL:
                ln(p.tensor_tensor(T1, src_r, br, ALU.mult))
                ln(p.tensor_tensor(T2, src_i, bi, ALU.mult))
                p.tensor_tensor(T1, T1, T2, ALU.subtract).then_inc(f["s4_pool"].sem, 1)
                break
            dr, di, t = Vr[:, m:2 * m, :], Vi[:, m:2 * m, :], T2[:, 0:m, :]
            ln(p.tensor_tensor(dr, src_r, br, ALU.mult))
            ln(p.tensor_tensor(t, src_i, bi, ALU.mult))
            ln(p.tensor_tensor(dr, dr, t, ALU.subtract))
            ln(p.tensor_tensor(di, src_r, bi, ALU.mult))
            ln(p.tensor_tensor(t, src_i, br, ALU.mult))
            ln(p.tensor_tensor(di, di, t, ALU.add))
            ln(p.tensor_tensor(W[0], wr, wr, ALU.mult))
            ln(p.tensor_tensor(W[1], wi, wi, ALU.mult))
            ln(p.tensor_tensor(W[0], W[0], W[1], ALU.subtract))
            ln(p.tensor_tensor(W[1], wr, wi, ALU.mult))
            ln(p.tensor_tensor(wi, W[1], W[1], ALU.add))
            ln(p.tensor_copy(wr, W[0]))
            m *= 2

    def dve_end(e):
        v, ln = nc.vector, g.link["dve"]
        e.wait_ge(f["s4_pool"].sem, f["s4_pool"](1))
        v.tensor_reduce(g.s4k[:, 0:HL], Vr, AX.X, ALU.add)
        ln(v.tensor_reduce(g.s4k[:, HL:S], T1, AX.X, ALU.add))
        ln(v.tensor_scalar(g.s4k, g.s4k, 2.0, None, ALU.mult))
        ln(v.tensor_tensor(g.s4k[:, 0:1], g.s4k[:, 0:1], g.col("l3x_skip"), ALU.add))
    return dict(act=act, dve=dve, pool=pool, dve_end=dve_end)


def layer_l2_cross(g):
    return cross_attention(g, 6, 0, ("L2_xattn_w_q", "L2_xattn_w_k", "L2_xattn_w_v", "L2_xattn_w_out", "l2x_bo"))


def narrow_self(g, layer, slot, load_weights, w_count, soft, bias):
    nc = g.nc
    tmp = g.temps()
    HD = 8
    w = g.slot[slot]
    wT = tmp.take(4 * P)
    qT, kT = tmp.take(TOK), tmp.take(TOK)
    V = tmp.take(NT * P).rearrange("p (t d) -> p t d", d=D)
    qm = [tmp.take(HG * P).rearrange("p (h q) -> p h q", h=HG) for _ in range(2)]
    orow = tmp.take(NT * P)
    oT, yT = tmp.take(TOK), tmp.take(TOK)
    itau, nthr, sp1, sp2 = (tmp.take(16) for _ in range(4))
    ln1 = layernorm(g, g.x, g.xn, out_T=g.xnT)
    KG = NT * NG
    f = flags(g, **{"n_w_in%d" % slot: 16 * w_count}, p_v_sb=KG)
    w_in = f["n_w_in%d" % slot]
    f = steps(g, f, rows_T="n_wT n_oT", T_ready="n_wT_sb n_oT_sb", products="n_q n_k n_v n_y",
          dve_step=("" if soft is not None else "n_tau0 ") + "n_q_sb n_k_sb n_v_sb n_rows n_yT", act_step="" if soft is not None else "n_tau1")
    back = add_back(g, yT, f["n_yT"])

    def tile(k):
        return slice(P * (k // NG), P * (k // NG) + P)

    def prep_dve(e, k):
        hs = HG * (k % NG)
        if k >= 2:
            e.wait_ge(core["f"]["s_scores"].sem, core["f"]["s_scores"](k - 1))
        nc.vector.tensor_tensor(qm[k % 2], qT[:, None, tile(k)].to_broadcast([P, HG, P]),
                                g.head_of[:, hs:hs + HG, None].to_broadcast([P, HG, P]), ALU.mult).then_inc(f["p_v_sb"].sem, 1)

    def prep_pe(e, k):
        e.wait_ge(f["p_v_sb"].sem, f["p_v_sb"](k + 1))

    core = self_attention(
        g, tmp, lambda k, h: (qm[k % 2][:, h, :], kT[:, tile(k)]),
        lambda k, h: V[:, k // NG, HD * (HG * (k % NG) + h):HD * (HG * (k % NG) + h) + HD],
        lambda k, h: (g.ps[:, 4, P * (k // NG) + HD * (HG * (k % NG) + h):P * (k // NG) + HD * (HG * (k % NG) + h) + HD], True, True),
        soft=soft, prep_pe=prep_pe, prep_dve=prep_dve, itau=itau, nthr=nthr)

    def load(e):
        wait_slot(g, e, layer)
        load_weights(e, w, w_in)

    def pe(e):
        t = nc.tensor
        start_layer(g, e, layer)
        e.wait_ge(w_in.sem, w_in(16 * w_count))
        for i in range(4):
            m = t.transpose(g.ps[:, 0, P * i:P * i + P], w[:, P * i:P * i + P], g.ident)
        m.then_inc(f["n_wT"].sem, 1)
        ln1["pe"](e)
        e.wait_ge(ln1["ready"].sem, ln1["ready"](1))
        e.wait_ge(f["n_wT_sb"].sem, f["n_wT_sb"](1))
        t.matmul(g.ps[:, 1, :], wT[:, 0:P], g.xnT, start=True, stop=True).then_inc(f["n_q"].sem, 1)
        t.matmul(g.ps[:, 2, :], wT[:, P:2 * P], g.xnT, start=True, stop=True).then_inc(f["n_k"].sem, 1)
        for j in range(NT):
            m = t.matmul(g.ps[:, 3, P * j:P * j + P], g.xnT[:, P * j:P * j + P], wT[:, 2 * P:3 * P], start=True, stop=True)
        m.then_inc(f["n_v"].sem, 1)
        e.wait_ge(f["n_v_sb"].sem, f["n_v_sb"](1))
        core["pe"](e)
        e.wait_ge(f["n_rows"].sem, f["n_rows"](1))
        for j in range(NT):
            m = t.transpose(g.ps[:, 5, P * j:P * j + P], orow[:, P * j:P * j + P], g.ident)
        m.then_inc(f["n_oT"].sem, 1)
        e.wait_ge(f["n_oT_sb"].sem, f["n_oT_sb"](1))
        t.matmul(g.ps[:, 6, :], wT[:, 3 * P:4 * P], oT, start=True, stop=True).then_inc(f["n_y"].sem, 1)
        back["pe"](e)

    def act(e):
        s, ln = nc.scalar, g.link["act"]
        start_layer(g, e, layer)
        if soft is None:
            e.wait_ge(f["n_tau0"].sem, f["n_tau0"](1))
            ln(s.activation(sp2, sp1, ACT.Exp, scale=-1.0))
            s.activation(sp2, sp2, ACT.Ln, bias=1.0).then_inc(f["n_tau1"].sem, 1)
        ln1["act"](e)
        core["act"](e)

    def dve(e):
        v, ln = nc.vector, g.link["dve"]
        if soft is None:
            comp, thr = g.scal[:, 32:48], g.scal[:, 48:64]
            ln(v.tensor_scalar(sp2, comp, -1.0, None, ALU.mult))
            v.tensor_tensor(sp1, comp, sp2, ALU.max).then_inc(f["n_tau0"].sem, 1)
            e.wait_ge(f["n_tau1"].sem, f["n_tau1"](1))
            ln(v.tensor_scalar(itau, comp, 0.0, 1e-6, ALU.max, ALU.add))
            ln(v.tensor_tensor(itau, itau, sp2, ALU.add))
            ln(v.reciprocal(itau, itau))
            ln(v.scalar_tensor_tensor(out=nthr, in0=thr, scalar=-1.0, in1=itau, op0=ALU.mult, op1=ALU.mult))
        e.wait_ge(f["n_wT"].sem, f["n_wT"](1))
        v.tensor_copy(wT, g.ps[:, 0, :]).then_inc(f["n_wT_sb"].sem, 1)
        ln1["dve"](e)
        e.wait_ge(f["n_q"].sem, f["n_q"](1))
        if bias:
            v.tensor_scalar(qT, g.ps[:, 1, :], g.col(bias[0], 0), HD ** -0.5, ALU.add, ALU.mult).then_inc(f["n_q_sb"].sem, 1)
        else:
            v.tensor_copy(qT, g.ps[:, 1, :]).then_inc(f["n_q_sb"].sem, 1)
        e.wait_ge(f["n_k"].sem, f["n_k"](1))
        if bias:
            v.tensor_scalar(kT, g.ps[:, 2, :], g.col(bias[0], 1), None, ALU.add).then_inc(f["n_k_sb"].sem, 1)
        else:
            v.tensor_copy(kT, g.ps[:, 2, :]).then_inc(f["n_k_sb"].sem, 1)
        e.wait_ge(f["n_v"].sem, f["n_v"](1))
        v.tensor_copy(V, g.ps[:, 3, :].rearrange("p (t d) -> p t d", d=D)).then_inc(f["n_v_sb"].sem, 1)
        e.wait_ge(f["n_v_sb"].sem, f["n_v_sb"](1))
        core["dve"](e)
        e.wait_ge(core["out"].sem, core["out"](KG))
        v.tensor_copy(orow, g.ps[:, 4, :]).then_inc(f["n_rows"].sem, 1)
        e.wait_ge(f["n_oT"].sem, f["n_oT"](1))
        if bias:
            v.tensor_scalar(oT, g.ps[:, 5, :], g.col(bias[0], 2), None, ALU.add).then_inc(f["n_oT_sb"].sem, 1)
        else:
            v.tensor_copy(oT, g.ps[:, 5, :]).then_inc(f["n_oT_sb"].sem, 1)
        e.wait_ge(f["n_y"].sem, f["n_y"](1))
        if bias:
            v.tensor_scalar(yT, g.ps[:, 6, :], g.col(bias[1]), None, ALU.add).then_inc(f["n_yT"].sem, 1)
        else:
            v.tensor_copy(yT, g.ps[:, 6, :]).then_inc(f["n_yT"].sem, 1)
        back["dve"](e)

    def pool(e):
        start_layer(g, e, layer)
        core["pool"](e)
    return dict(load=load, sp=nothing, dve=dve, act=act, pe=pe, pool=pool)


def layer_l2_self(g):
    def load_weights(e, w, w_in):
        e.dma_start(w[:, 0:3 * P].rearrange("p (j d) -> p j d", d=D), g.a["L2_attn_qkv_w"].rearrange("(j p) d -> p j d", p=P)).then_inc(w_in.sem, 16)
        e.dma_start(w[:, 3 * P:4 * P], g.a["L2_attn_proj_w"]).then_inc(w_in.sem, 16)
    return narrow_self(g, 7, 1, load_weights, 2, g.mask_bd, ("l2a_qkvb", "l2a_pb"))


def layer_l2_quant(g):
    nc = g.nc
    tmp = g.temps()
    w = g.slot[0][:, 0:D]
    wqT = tmp.take(P, BF16)
    aqT = tmp.take(TOK, BF16)
    asum, ws, iws, sc = (tmp.take(1) for _ in range(4))
    am, ia, ys = (tmp.take(NT) for _ in range(3))
    ln1 = layernorm(g, g.x, g.xn)
    f = flags(g, l2f_w_in=16, x_done=1)
    f = steps(g, f, products="t_sum t_y", rows_ready="t_abs t_wq t_rows", rows_T="t_wqT t_aT", T_ready="t_T_sb")

    def load(e):
        wait_slot(g, e, 8)
        e.dma_start(w, g.a["L2_ffn_weight"]).then_inc(f["l2f_w_in"].sem, 16)

    def dve(e):
        v, ln = nc.vector, g.link["dve"]
        e.wait_ge(f["l2f_w_in"].sem, f["l2f_w_in"](16))
        v.tensor_reduce(asum, w, AX.X, ALU.add, apply_absolute_value=True).then_inc(f["t_abs"].sem, 1)
        e.wait_ge(f["t_sum"].sem, f["t_sum"](1))
        ln(v.tensor_scalar(ws, g.ps[:, 0, 0:1], 1.0 / (D * D), 1e-8, ALU.mult, ALU.add))
        ln(v.reciprocal(iws, ws))
        ln(v.tensor_scalar(w, w, iws, HALF_ULP, ALU.mult, ALU.add))
        ln(v.tensor_scalar(w, w, HALF_ULP, 1.0, ALU.subtract, ALU.min))
        v.tensor_scalar(w, w, -1.0, None, ALU.max).then_inc(f["t_wq"].sem, 1)
        ln1["dve"](e)
        ln(v.tensor_reduce(am, g.xn[:, :, :], AX.X, ALU.max, apply_absolute_value=True))
        ln(v.tensor_scalar(am, am, 1e-8, None, ALU.add))
        ln(v.reciprocal(ia, am))
        ln(v.tensor_scalar(ia, ia, 127.0, None, ALU.mult))
        for j in range(NT):
            i = v.tensor_scalar(g.xn[:, j, :], g.xn[:, j, :], ia[:, j:j + 1], -128.0, ALU.mult, ALU.max)
        ln(i)
        ln(v.tensor_scalar(g.xn2d, g.xn2d, 127.0, HALF_ULP, ALU.min, ALU.add))
        v.tensor_scalar(g.xn2d, g.xn2d, HALF_ULP, None, ALU.subtract).then_inc(f["t_rows"].sem, 1)
        ln(v.tensor_scalar(ys, am, ws, 1.0 / 127.0, ALU.mult, ALU.mult))
        e.wait_ge(f["t_wqT"].sem, f["t_wqT"](1))
        v.tensor_copy(wqT, g.ps[:, 1, 0:P])
        e.wait_ge(f["t_aT"].sem, f["t_aT"](1))
        v.tensor_copy(aqT, g.ps[:, 2, :]).then_inc(f["t_T_sb"].sem, 1)
        e.wait_ge(f["t_y"].sem, f["t_y"](1))
        for j in range(NT):
            i = v.scalar_tensor_tensor(out=g.x[:, j, :], in0=g.ps[:, 3, P * j:P * j + P], scalar=ys[:, j:j + 1], in1=g.x[:, j, :],
                                       op0=ALU.mult, op1=ALU.add)
        i.then_inc(f["x_done"].sem, 1)
        e.wait_ge(f["x_done"].sem, f["x_done"](1))

    def act(e):
        ln1["act"](e)

    def pe(e):
        t = nc.tensor
        e.wait_ge(f["t_abs"].sem, f["t_abs"](1))
        t.matmul(g.ps[:, 0, 0:1], g.ones, asum, start=True, stop=True).then_inc(f["t_sum"].sem, 1)
        e.wait_ge(f["t_wq"].sem, f["t_wq"](1))
        t.transpose(g.ps[:, 1, 0:P], w, g.ident).then_inc(f["t_wqT"].sem, 1)
        ln1["pe"](e)
        e.wait_ge(f["t_rows"].sem, f["t_rows"](1))
        for j in range(NT):
            i = t.transpose(g.ps[:, 2, P * j:P * j + P], g.xn[:, j, :], g.ident)
        i.then_inc(f["t_aT"].sem, 1)
        e.wait_ge(f["t_T_sb"].sem, f["t_T_sb"](1))
        for j in range(NT):
            i = t.matmul(g.ps[:, 3, P * j:P * j + P], aqT[:, P * j:P * j + P], wqT, start=True, stop=True)
        i.then_inc(f["t_y"].sem, 1)
    return dict(load=load, sp=nothing, dve=dve, act=act, pe=pe, pool=nothing)


def layer_l3_cross(g):
    nc = g.nc
    tmp = g.temps()
    H, DH, TOPK = 4, 32, 32
    REPL = -3.0e38
    NTL = 2 * B
    w = g.slot[1]
    wcols = dict(wq=(0, P, P), wk=(P, DC, P), wv=(2 * P, DC, P), wfi=(3 * P, P, 2 * P), wfo=(5 * P, P, 2 * P), w1=(7 * P, P, 512), w2=(7 * P + 512, P, 512))
    wq, wk, wv, wfi, wfo, w1, w2 = (w[0:r, a:a + n] for a, r, n in wcols.values())
    w2 = w2.rearrange("p (c d) -> p c d", d=D)
    pre = Arena(g.pre, 4096)
    Gm = pre.take(H * DC)
    qh = pre.take(B * H * S, BF16)[0:DC, :].rearrange("p (b h q) -> p b h q", b=B, h=H)
    ql = pre.take(B * H * S, BF16)[0:DC, :].rearrange("p (b h q) -> p b h q", b=B, h=H)
    aTh = pre.take(NCH * S, BF16)
    aTl = pre.take(NCH * S, BF16)
    xiT = pre.take(TOK)
    wT = pre.take(2 * P)
    sc = [tmp.take(NK) for _ in range(2)]
    work = tmp.take(NK)
    low = tmp.take(NK)
    at = [tmp.take(NK) for _ in range(2)]
    top = tmp.take(TOPK)
    ex = tmp.take(TOPK)
    nm, z, zi = (tmp.take(2) for _ in range(3))
    sel = [tmp.take(S) for _ in range(2)]
    c1, ctT = tmp.take(TOK), tmp.take(TOK)
    late = g.temps()
    m1, b1_, m2, b2_, y, xt, hT, yT = (late.take(TOK) for _ in range(8))
    rows = late.take(NT * P).rearrange("p (t d) -> p t d", d=D)
    h1 = late.take(4 * TOK)
    SB = g.ps[:, 0:4, :].rearrange("p a n -> p (a n)")
    AT = g.ps[:, 4:6, :].rearrange("p a n -> p (a n)")
    ln1 = layernorm(g, g.x, g.xn, out_T=g.xnT)
    xin = low[:, 0:TOK].rearrange("p (t d) -> p t d", d=D)
    ln2 = layernorm(g, g.xn, xin, out_T=xiT, gain=g.col("l3x_gi"), shift=g.col("l3x_bi"))
    ln3 = layernorm(g, rows, rows, out_T=hT, gain=g.col("l3x_gf"), shift=g.col("l3x_bf"))
    ln4 = layernorm(g, rows, rows)
    f = flags(g, n_w_in1=112, k_scores=NTL, k_copied=NTL, k_lo=1, k_max=NTL, k_top=NTL, k_exp=NTL, k_att=NTL, k_sel=NTL, k_aT=B, k_aT_hi=B,
              k_aT_lo=B, k_c1=B, x_done=1)
    f = steps(g, f, rows_T="k_wT k_xtT k_x2T", products="k_G k_qk k_ct k_film k_h0 k_h1 k_h2 k_h3 k_y", T_ready="k_wT_sb k_rows k_rows2",
          dve_step="k_G_sb k_qlo k_c1_sb k_ct_sb k_xt k_xt2", act_step="k_qhi k_gelu")
    w_in = f["n_w_in1"]

    def load(e):
        wait_slot(g, e, 9)
        for dst, name in ((wq, "Wq"), (wk, "Wk"), (wv, "Wv"), (wfi, "W_film_in"), (wfo, "W_film_out"), (w1, "W1")):
            e.dma_start(dst, g.a["L3_xattn_" + name]).then_inc(w_in.sem, 16)
        e.dma_start(w2, g.a["L3_xattn_W2"].rearrange("(c p) d -> p c d", p=P)).then_inc(w_in.sem, 16)

    def pe(e):
        t = nc.tensor
        start_layer(g, e, 9)
        e.wait_ge(w_in.sem, w_in(112))
        t.transpose(g.ps[:, 4, 0:P], wq, g.ident)
        t.transpose(g.ps[:, 4, P:P + DC], wk, g.ident[0:DC, 0:DC]).then_inc(f["k_wT"].sem, 1)
        e.wait_ge(f["k_wT_sb"].sem, f["k_wT_sb"](1))
        for h in range(H):
            r = slice(DH * h, DH * h + DH)
            i = t.matmul(g.ps[:, h, 0:DC], wT[r, 0:P], wT[r, P:P + DC], start=True, stop=True)
        i.then_inc(f["k_G"].sem, 1)
        ln1["pe"](e)
        ln2["pe"](e)
        e.wait_ge(ln1["ready"].sem, ln1["ready"](1))
        e.wait_ge(f["k_G_sb"].sem, f["k_G_sb"](1))
        for h in range(H):
            i = t.matmul(g.ps[0:DC, h, :], Gm[:, DC * h:DC * h + DC], g.xnT, start=True, stop=True)
        i.then_inc(f["k_qk"].sem, 1)
        e.wait_ge(f["k_qlo"].sem, f["k_qlo"](1))

        def attend(b):
            e.wait_ge(f["k_sel"].sem, f["k_sel"](2 * b + 2))
            e.wait_ge(f["k_att"].sem, f["k_att"](2 * b + 2))
            if b >= 1:
                e.wait_ge(f["k_aT_lo"].sem, f["k_aT_lo"](b))
            for c in range(NCH):
                n = P if c < FULL else LASTK
                for j in range(2):
                    i = t.matmul(AT[0:n, S * c:S * c + S], at[j][:, P * c:P * c + n], sel[j], start=j == 0, stop=j == 1)
            i.then_inc(f["k_aT"].sem, 1)
            e.wait_ge(f["k_aT_lo"].sem, f["k_aT_lo"](b + 1))
            for c in range(NCH):
                n = P if c < FULL else LASTK
                for j, (lhs, rhs) in enumerate(((g.cr_hi, aTh), (g.cr_lo, aTh), (g.cr_hi, aTl))):
                    i = t.matmul(g.ps[0:DC, 6, S * b:S * b + S], lhs[0:n, b, c, 0:DC], rhs[0:n, S * c:S * c + S],
                                 start=c == 0 and j == 0, stop=c == NCH - 1 and j == 2)
            i.then_inc(f["k_c1"].sem, 1)

        for k in range(NTL):
            b, j = divmod(k, 2)
            if k >= 1:
                e.wait_ge(f["k_copied"].sem, f["k_copied"](k))
            for a, n in KSPAN:
                q_hi = qh[:, b, 2 * j:2 * j + 2, :].rearrange("p h q -> p (h q)")
                q_lo = ql[:, b, 2 * j:2 * j + 2, :].rearrange("p h q -> p (h q)")
                t.matmul(SB[:, a:a + n], q_hi, g.cT_hi[0:DC, b, a:a + n], start=True, stop=False)
                t.matmul(SB[:, a:a + n], q_lo, g.cT_hi[0:DC, b, a:a + n], start=False, stop=False)
                t.matmul(SB[:, a:a + n], q_hi, g.cT_lo[0:DC, b, a:a + n], start=False, stop=False)
                i = t.matmul(SB[:, a:a + n], g.sel[:, b, :], g.kmask[0:8, 1, a:a + n], start=False, stop=True)
            i.then_inc(f["k_scores"].sem, 1)
            if j == 0 and b >= 1:
                attend(b - 1)
        attend(B - 1)
        e.wait_ge(f["k_c1_sb"].sem, f["k_c1_sb"](1))
        t.matmul(g.ps[:, 7, :], wv, c1[0:DC, :], start=True, stop=True).then_inc(f["k_ct"].sem, 1)
        e.wait_ge(f["k_ct_sb"].sem, f["k_ct_sb"](1))
        for i_, (wf, half) in enumerate(((wfi, 0), (wfi, 1), (wfo, 0), (wfo, 1))):
            i = t.matmul(g.ps[:, i_, :], wf[:, P * half:P * half + P], ctT, start=True, stop=True)
        i.then_inc(f["k_film"].sem, 1)
        e.wait_ge(f["k_xt"].sem, f["k_xt"](1))
        for j in range(NT):
            i = t.transpose(g.ps[:, 4, P * j:P * j + P], xt[:, P * j:P * j + P], g.ident)
        i.then_inc(f["k_xtT"].sem, 1)
        ln3["pe"](e)
        e.wait_ge(ln3["ready"].sem, ln3["ready"](1))
        for c, flag in enumerate((f["k_h0"], f["k_h1"], f["k_h2"], f["k_h3"])):
            t.matmul(g.ps[:, c, :], w1[:, P * c:P * c + P], hT, start=True, stop=True).then_inc(flag.sem, 1)
        e.wait_ge(f["k_gelu"].sem, f["k_gelu"](1))
        for c in range(4):
            i = t.matmul(g.ps[:, 5, :], w2[:, c, :], h1[:, TOK * c:TOK * c + TOK], start=c == 0, stop=c == 3)
        i.then_inc(f["k_y"].sem, 1)
        e.wait_ge(f["k_xt2"].sem, f["k_xt2"](1))
        for j in range(NT):
            i = t.transpose(g.ps[:, 6, P * j:P * j + P], yT[:, P * j:P * j + P], g.ident)
        i.then_inc(f["k_x2T"].sem, 1)

    def act(e):
        s, ln = nc.scalar, g.link["act"]
        start_layer(g, e, 9)
        ln1["act"](e)
        ln2["act"](e)
        e.wait_ge(f["k_qk"].sem, f["k_qk"](1))
        for h in range(H):
            i = s.activation(qh[:, :, h, :], g.ps[0:DC, h, :].rearrange("p (b q) -> p b q", b=B), ACT.Copy)
        i.then_inc(f["k_qhi"].sem, 1)

        def copy(k):
            e.wait_ge(f["k_scores"].sem, f["k_scores"](k + 1))
            if k >= 2:
                e.wait_ge(f["k_exp"].sem, f["k_exp"](k - 1))
                e.wait_ge(f["k_max"].sem, f["k_max"](k - 1))
            s.activation(sc[k % 2], SB[:, 0:NK], ACT.Copy).then_inc(f["k_copied"].sem, 1)

        copy(0)
        for k in range(NTL):
            if k + 1 < NTL:
                copy(k + 1)
            e.wait_ge(f["k_top"].sem, f["k_top"](k + 1))
            if k >= 2:
                e.wait_ge(f["k_aT"].sem, f["k_aT"](k // 2))
            if k >= 1:
                e.wait_ge(f["k_att"].sem, f["k_att"](k))
            s.activation(ex, top, ACT.Exp, bias=nm[:, 0:1], accum_out=z[:, 0:1])
            s.activation(at[k % 2], sc[k % 2], ACT.Exp, bias=nm[:, 0:1])
            s.activation(low, work, ACT.Exp, bias=nm[:, 0:1]).then_inc(f["k_exp"].sem, 1)
            if k % 2 == 1:
                b = k // 2
                e.wait_ge(f["k_aT"].sem, f["k_aT"](b + 1))
                if b >= 1:
                    e.wait_ge(f["k_c1"].sem, f["k_c1"](b))
                s.activation(aTh[:, 0:FULL * S], AT[:, 0:FULL * S], ACT.Copy)
                s.activation(aTh[0:LASTK, FULL * S:NCH * S], AT[0:LASTK, FULL * S:NCH * S], ACT.Copy).then_inc(f["k_aT_hi"].sem, 1)
        ln3["act"](e)
        for c, flag in enumerate((f["k_h0"], f["k_h1"], f["k_h2"], f["k_h3"])):
            e.wait_ge(flag.sem, flag(1))
            i = s.activation(h1[:, TOK * c:TOK * c + TOK], g.ps[:, c, :], ACT.Gelu, bias=g.col("l3x_b1", c))
        i.then_inc(f["k_gelu"].sem, 1)
        ln4["act"](e)

    def dve(e):
        v, ln = nc.vector, g.link["dve"]
        e.wait_ge(f["k_wT"].sem, f["k_wT"](1))
        v.tensor_copy(wT[:, 0:P + DC], g.ps[:, 4, 0:P + DC]).then_inc(f["k_wT_sb"].sem, 1)
        e.wait_ge(f["k_G"].sem, f["k_G"](1))
        for h in range(H):
            i = v.tensor_scalar(Gm[:, DC * h:DC * h + DC], g.ps[:, h, 0:DC], DH ** -0.5, None, ALU.mult)
        i.then_inc(f["k_G_sb"].sem, 1)
        ln1["dve"](e)
        ln2["dve"](e)
        e.wait_ge(f["k_qhi"].sem, f["k_qhi"](1))
        for h in range(H):
            i = v.tensor_tensor(ql[:, :, h, :], g.ps[0:DC, h, :].rearrange("p (b q) -> p b q", b=B), qh[:, :, h, :], ALU.subtract)
        i.then_inc(f["k_qlo"].sem, 1)

        def lows(b):
            e.wait_ge(f["k_aT_hi"].sem, f["k_aT_hi"](b + 1))
            v.tensor_tensor(aTl[:, 0:FULL * S], AT[:, 0:FULL * S], aTh[:, 0:FULL * S], ALU.subtract)
            v.tensor_tensor(aTl[0:LASTK, FULL * S:NCH * S], AT[0:LASTK, FULL * S:NCH * S], aTh[0:LASTK, FULL * S:NCH * S],
                            ALU.subtract).then_inc(f["k_aT_lo"].sem, 1)

        for k in range(NTL):
            e.wait_ge(f["k_copied"].sem, f["k_copied"](k + 1))
            if k >= 1:
                e.wait_ge(f["k_exp"].sem, f["k_exp"](k))
            for r in range(TOPK // 8):
                src = sc[k % 2] if r == 0 else work
                ln(v.max(out=top[:, 8 * r:8 * r + 8], in_=src))
                i = v.match_replace(out=work, in_to_replace=top[:, 8 * r:8 * r + 8], in_values=src, imm_value=REPL)
                if r == 0:
                    i.then_inc(f["k_max"].sem, 1)
                    e.wait_ge(f["k_max"].sem, f["k_max"](k + 1))
                else:
                    ln(i)
            v.tensor_scalar(nm[:, 0:1], top[:, 0:1], -1.0, None, ALU.mult).then_inc(f["k_top"].sem, 1)
            e.wait_ge(f["k_exp"].sem, f["k_exp"](k + 1))
            ln(v.reciprocal(zi[:, 0:1], z[:, 0:1]))
            if k >= 2:
                e.wait_ge(f["k_aT"].sem, f["k_aT"](k // 2))
            v.tensor_scalar(sel[k % 2], g.fold, zi[:, 0:1], 1.0 / H, ALU.mult, ALU.mult).then_inc(f["k_sel"].sem, 1)
            if k % 2 == 1:
                lows(k // 2)
        e.wait_ge(f["k_c1"].sem, f["k_c1"](B))
        v.tensor_copy(c1[0:DC, :], g.ps[0:DC, 6, :]).then_inc(f["k_c1_sb"].sem, 1)
        e.wait_ge(f["k_ct"].sem, f["k_ct"](1))
        v.tensor_tensor(ctT, g.ps[:, 7, :], g.tmask, ALU.mult).then_inc(f["k_ct_sb"].sem, 1)
        e.wait_ge(f["k_film"].sem, f["k_film"](1))
        gate = g.scal[:, 24:25]
        for i_, (dst, name, half) in enumerate(((m1, "l3x_bfi", 0), (b1_, "l3x_bfi", 1), (m2, "l3x_bfo", 0), (b2_, "l3x_bfo", 1))):
            i = v.tensor_scalar(dst, g.ps[:, i_, :], g.col(name, half), gate, ALU.add, ALU.mult)
        ln(i)
        v.tensor_scalar(m1, m1, 1.0, None, ALU.add)
        ln(v.tensor_scalar(m2, m2, 1.0, None, ALU.add))
        ln(v.tensor_tensor(xiT, xiT, m1, ALU.mult))
        ln(v.tensor_tensor(xiT, xiT, b1_, ALU.add))
        ln(v.tensor_scalar(y, xiT, g.s4k[:, 0:1], None, ALU.mult))
        xv, yv = (a.rearrange("p (b s) -> p b s", b=B) for a in (xiT, y))
        for j in range(1, S):
            ln(v.scalar_tensor_tensor(out=yv[:, :, j:S], in0=xv[:, :, 0:S - j], scalar=g.s4k[:, j:j + 1], in1=yv[:, :, j:S],
                                      op0=ALU.mult, op1=ALU.add))
        ln(v.tensor_tensor(y, y, m2, ALU.mult))
        ln(v.tensor_tensor(y, y, b2_, ALU.add))
        v.tensor_tensor(xt, y, g.xnT, ALU.add).then_inc(f["k_xt"].sem, 1)
        e.wait_ge(f["k_xtT"].sem, f["k_xtT"](1))
        v.tensor_copy(rows, g.ps[:, 4, :].rearrange("p (t d) -> p t d", d=D)).then_inc(f["k_rows"].sem, 1)
        e.wait_ge(f["k_rows"].sem, f["k_rows"](1))
        ln3["dve"](e)
        e.wait_ge(f["k_y"].sem, f["k_y"](1))
        v.scalar_tensor_tensor(out=yT, in0=g.ps[:, 5, :], scalar=g.col("l3x_b2"), in1=xt, op0=ALU.add, op1=ALU.add).then_inc(f["k_xt2"].sem, 1)
        e.wait_ge(f["k_x2T"].sem, f["k_x2T"](1))
        v.tensor_copy(rows, g.ps[:, 6, :].rearrange("p (t d) -> p t d", d=D)).then_inc(f["k_rows2"].sem, 1)
        e.wait_ge(f["k_rows2"].sem, f["k_rows2"](1))
        ln4["dve"](e)
        for j in range(NT):
            i = v.tensor_tensor(rows[:, j, :], rows[:, j, :], g.bcv["l3x_go"], ALU.mult)
        ln(i)
        for j in range(NT):
            i = v.tensor_tensor(rows[:, j, :], rows[:, j, :], g.bcv["l3x_bo"], ALU.add)
        ln(i)
        v.tensor_tensor(g.x[:, :, :], g.x[:, :, :], rows, ALU.add).then_inc(f["x_done"].sem, 1)
        e.wait_ge(f["x_done"].sem, f["x_done"](1))

    def pool(e):
        start_layer(g, e, 9)
        for k in range(NTL):
            e.wait_ge(f["k_exp"].sem, f["k_exp"](k + 1))
            nc.gpsimd.tensor_tensor(at[k % 2], at[k % 2], low, ALU.subtract).then_inc(f["k_att"].sem, 1)
    return dict(load=load, sp=nothing, dve=dve, act=act, pe=pe, pool=pool)


def layer_l3_self(g):
    def load_weights(e, w, w_in):
        for i, name in enumerate(("Wq", "Wk", "Wv", "Wo")):
            e.dma_start(w[:, P * i:P * i + P], g.a["L3_attn_" + name]).then_inc(w_in.sem, 16)
    return narrow_self(g, 10, 0, load_weights, 4, None, None)


def layer_l3_moe(g):
    nc = g.nc
    tmp = g.temps()
    E, FC = 8, 4
    K = E * FC
    EW = 2 * 512
    place = [g.slot[1], g.slot[0]]
    wr = tmp.take(E)
    hb = [tmp.take(TOK) for _ in range(8)]
    acc = tmp.take(NT * P).rearrange("p (t d) -> p t d", d=D)
    lg, ga, se, ew, wt = (tmp.take(NT * E).rearrange("p (t e) -> p t e", e=E) for _ in range(5))
    pair = tmp.take(NT * E * E).rearrange("p (t a b) -> p t a b", t=NT, a=E)
    eq = tmp.take(NT * E * E).rearrange("p (t a b) -> p t a b", t=NT, a=E)
    mx, zs, zi = (tmp.take(NT) for _ in range(3))
    wTt = tmp.take(TOK)
    ln1 = layernorm(g, g.x, g.xn, out_T=g.xnT)
    f = flags(g, e_w_in0=144, e_w_in1=128, m_gate=K, m_act=K, m_y=E, m_acc=E, x_done=1)
    f = steps(g, f, products="r_logits r_b2", dve_step="r_shift r_weights r_wT_sb", rows_T="r_wT", act_step="r_exp")
    arrived, total = [f["e_w_in0"], f["e_w_in1"]], [144, 128]

    def views(x):
        w = place[x // 4][:, EW * (x % 4):EW * (x % 4) + EW]
        return w[:, 0:512], w[:, 512:1024].rearrange("p (c d) -> p c d", d=D)

    def load_four(e, p):
        for x in range(4 * p, 4 * p + 4):
            w1, w2 = views(x)
            e.dma_start(w1, g.a["L3_ffn_W1"][x]).then_inc(arrived[p].sem, 16)
            e.dma_start(w2, g.a["L3_ffn_W2"][x].rearrange("(c p) d -> p c d", p=P)).then_inc(arrived[p].sem, 16)

    def load(e):
        wait_slot(g, e, 11)
        load_four(e, 0)

    def sp(e):
        start_layer(g, e, 11)
        e.dma_start(wr, g.a["L3_ffn_W_router"]).then_inc(f["e_w_in0"].sem, 16)
        load_four(e, 1)

    def pe(e):
        t = nc.tensor
        ln1["pe"](e)
        e.wait_ge(ln1["ready"].sem, ln1["ready"](1))
        e.wait_ge(f["e_w_in0"].sem, f["e_w_in0"](144))
        for j in range(NT):
            i = t.matmul(g.ps[:, 4, E * j:E * j + E], g.xnT[:, P * j:P * j + P], wr, start=True, stop=True)
        i.then_inc(f["r_logits"].sem, 1)

        def up(k):
            x, c = divmod(k, FC)
            if k == K // 2:
                e.wait_ge(f["e_w_in1"].sem, f["e_w_in1"](128))
            if k >= 2:
                e.wait_ge(f["m_act"].sem, f["m_act"](k - 1))
            t.matmul(g.ps[:, k % 2, :], views(x)[0][:, P * c:P * c + P], g.xnT, start=True, stop=True).then_inc(f["m_gate"].sem, 1)

        for c in range(FC):
            up(c)
        e.wait_ge(f["r_weights"].sem, f["r_weights"](1))
        for j in range(NT):
            i = t.transpose(g.ps[0:E, 5, P * j:P * j + P], wt[:, j, :], g.ident)
        i.then_inc(f["r_wT"].sem, 1)
        e.wait_ge(f["r_wT_sb"].sem, f["r_wT_sb"](1))
        for j in range(NT):
            i = t.matmul(g.ps[:, 6, P * j:P * j + P], wTt[0:E, P * j:P * j + P], g.b2moe[0:E, :], start=True, stop=True)
        i.then_inc(f["r_b2"].sem, 1)
        for x in range(E):
            if x + 1 < E:
                for c in range(FC):
                    up(FC * (x + 1) + c)
            e.wait_ge(f["m_act"].sem, f["m_act"](FC * (x + 1)))
            if x >= 2:
                e.wait_ge(f["m_acc"].sem, f["m_acc"](x - 1))
            for j in range(NT):
                for c in range(FC):
                    i = t.matmul(g.ps[:, 2 + x % 2, P * j:P * j + P], hb[(FC * x + c) % 8][:, P * j:P * j + P], views(x)[1][:, c, :],
                                 start=c == 0, stop=c == FC - 1)
            i.then_inc(f["m_y"].sem, 1)

    def act(e):
        s = nc.scalar
        start_layer(g, e, 11)
        ln1["act"](e)

        def relu(k):
            x, c = divmod(k, FC)
            e.wait_ge(f["m_gate"].sem, f["m_gate"](k + 1))
            if x >= 2:
                e.wait_ge(f["m_y"].sem, f["m_y"](x - 1))
            s.activation(hb[k % 8], g.ps[:, k % 2, :], ACT.Relu, bias=g.moe_b1(x, c)).then_inc(f["m_act"].sem, 1)
        e.wait_ge(f["r_shift"].sem, f["r_shift"](1))
        s.activation(ew, ga, ACT.Exp).then_inc(f["r_exp"].sem, 1)
        for k in range(K):
            relu(k)

    def dve(e):
        v, ln = nc.vector, g.link["dve"]
        ln1["dve"](e)
        e.wait_ge(f["r_logits"].sem, f["r_logits"](1))
        ln(v.tensor_tensor(lg, g.ps[:, 4, 0:NT * E].rearrange("p (t e) -> p t e", e=E),
                           g.scal[:, None, 16:24].to_broadcast([P, NT, E]), ALU.add))
        ln(v.tensor_reduce(mx, lg, AX.X, ALU.max))
        v.tensor_tensor(ga, lg, mx[:, :, None].to_broadcast([P, NT, E]), ALU.subtract).then_inc(f["r_shift"].sem, 1)
        A4 = [P, NT, E, E]
        va, vb = lg[:, :, :, None].to_broadcast(A4), lg[:, :, None, :].to_broadcast(A4)
        v.tensor_tensor(pair, vb, va, ALU.is_gt)
        ln(v.tensor_tensor(eq, vb, va, ALU.is_equal))
        ln(v.tensor_tensor(eq, eq, g.before[:, None, :, :].to_broadcast(A4), ALU.mult))
        ln(v.tensor_tensor(pair, pair, eq, ALU.add))
        ln(v.tensor_reduce(se, pair, AX.X, ALU.add))
        ln(v.tensor_scalar(se, se, 2.0, None, ALU.is_lt))
        e.wait_ge(f["r_exp"].sem, f["r_exp"](1))
        ln(v.tensor_tensor(ew, ew, se, ALU.mult))
        ln(v.tensor_reduce(zs, ew, AX.X, ALU.add))
        ln(v.reciprocal(zi, zs))
        v.tensor_tensor(wt, ew, zi[:, :, None].to_broadcast([P, NT, E]), ALU.mult).then_inc(f["r_weights"].sem, 1)
        e.wait_ge(f["r_wT"].sem, f["r_wT"](1))
        v.tensor_copy(wTt[0:E, :], g.ps[0:E, 5, :]).then_inc(f["r_wT_sb"].sem, 1)
        e.wait_ge(f["r_b2"].sem, f["r_b2"](1))
        ln(v.tensor_tensor(acc, g.x[:, :, :], g.ps[:, 6, :].rearrange("p (t d) -> p t d", d=D), ALU.add))
        for x in range(E):
            e.wait_ge(f["m_y"].sem, f["m_y"](x + 1))
            for j in range(NT):
                i = v.scalar_tensor_tensor(out=acc[:, j, :], in0=g.ps[:, 2 + x % 2, P * j:P * j + P], scalar=wt[:, j, x:x + 1],
                                           in1=acc[:, j, :], op0=ALU.mult, op1=ALU.add)
            i.then_inc(f["m_acc"].sem, 1)
            e.wait_ge(f["m_acc"].sem, f["m_acc"](x + 1))
        v.tensor_copy(g.x[:, :, :], acc).then_inc(f["x_done"].sem, 1)
    return dict(own_loads_first=True, load=load, sp=sp, dve=dve, act=act, pe=pe, pool=nothing)


LAYERS = [layer_l0_cross,layer_l0_cosine,layer_l0_quant_ffn,layer_l1_cross,layer_l1_self,layer_l1_moe,layer_l2_cross,layer_l2_self,layer_l2_quant,layer_l3_cross,layer_l3_self,layer_l3_moe]
ROOM = 11300


def build(nc, args, out, layers=12):
    g = G()
    g.nc, g.a = nc, args
    with ExitStack() as ctx:
        def sb(name, shape, dt=F32):
            return ctx.enter_context(nc.sbuf_tensor(name, shape, dt))

        g.new_sem = lambda name: ctx.enter_context(nc.semaphore(name))
        g.flag = {}
        g.x = sb("x_rows", [P, NT, D])
        g.x2d = g.x[:, :, :].rearrange("p t d -> p (t d)")
        g.cT_hi = sb("ctxT_hi", [P, B, NK], BF16)
        g.cT_lo = sb("ctxT_lo", [P, B, NK], BF16)
        g.cr_hi = sb("ctx_hi", [P, B, NCH, DC + 1], BF16)
        g.cr_lo = sb("ctx_lo", [P, B, NCH, DC + 1], BF16)
        slots = sb("weight_slots", [P, 2, 4096])
        g.slot = [slots[:, i, :] for i in range(2)]
        g.vrows = sb("vector_rows", [P, P])[:, :]
        g.vcols = sb("vector_cols", [P, P])[:, :]
        g.bc = sb("row_vectors", [P, len(BCAST), D])
        g.bcv = {name: g.bc[:, i, :] for i, (name, _) in enumerate(BCAST)}
        g.scal = sb("scalars", [P, 64])[:, :]
        g.tmask8 = sb("token_mask_bytes", [P, TOK], U8)[:, :]
        g.tmask = sb("token_mask", [P, TOK], BF16)[:, :]
        g.kmask = sb("key_mask_terms", [8, 2, NK], BF16)
        g.b2moe = sb("moe_b2", [8, D])
        g.ident = sb("ident", [P, P])[:, :]
        g.ones = sb("ones", [P, P])[:, :]
        g.blk = sb("blk", [P, P])[:, :]
        g.mask_bd = sb("mask_bd", [P, P])[:, :]
        g.mask_ca = sb("mask_ca", [P, P])[:, :]
        g.tri_mul = sb("tri_mul", [P, P])[:, :]
        g.tri_add = sb("tri_add", [P, P])[:, :]
        g.neg_blk = sb("neg_blk", [P, P])[:, :]
        g.head_of = sb("head_of", [P, 16])[:, :]
        g.fold = sb("fold", [P, 64])[:, :]
        g.st = sb("st", [P, 6 * NT])[:, :]
        g.mv = sb("mv", [P, 2 * NT])[:, :]
        g.ve = sb("ve", [P, NT])[:, :]
        g.sd = sb("sd", [P, NT])[:, :]
        g.rstd = sb("rstd", [P, NT])[:, :]
        g.xnT = sb("xnT", [P, TOK])[:, :]
        g.sel = sb("sel", [8, B, P], BF16)[:, :, :]
        g.before = sb("before", [P, 8, 8])[:, :, :]
        g.xn = sb("x_normed", [P, NT, D])
        g.xn2d = g.xn[:, :, :].rearrange("p t d -> p (t d)")
        g.s4in = sb("s4d_in", [P, 4 * S])[:, :]
        g.s4k = sb("s4d_kernel", [P, S])[:, :]
        g.s4dt = sb("s4d_dt", [P, 1])[:, :]
        g.s4_sem = g.new_sem("s4d_in_loaded")
        g.half = sb("half", [P, 1])[:, :]
        g.pre = sb("folded_weights", [P, 4096])[:, :]
        g.ps = ctx.enter_context(nc.psum_tensor("banks", [P, 8, BANK], F32))
        room = sb("temporaries", [P, ROOM])
        g.m8 = room[0:8, 2 * NK:2 * NK + (2 * NK + 3) // 4].bitcast(U8)[:, 0:2 * NK].rearrange("p (m k) -> p m k", m=2)
        g.mtmp = room[0:8, 0:2 * NK].rearrange("p (m k) -> p m k", m=2)
        g.temps = lambda: Arena(room, ROOM)
        chain = {n: g.new_sem(n + "_order") for n in ("dve", "act", "pool")}
        g.link = {}
        out_done = g.new_sem("out_done")

        stages = [stage_setup(g)] + [LAYERS[i](g) for i in range(layers)]

        with nc.Block() as block:
            @block.sync
            def _(sp):
                stages[0]["sp"](sp)
                stages[1]["load"](sp)
                for i in range(1, len(stages)):
                    if "own_loads_first" in stages[i]:
                        stages[i]["sp"](sp)
                    if i + 1 < len(stages):
                        stages[i + 1]["load"](sp)
                    if "own_loads_first" not in stages[i]:
                        stages[i]["sp"](sp)
                sp.wait_ge(g.flag["x_done"].sem, layers)
                sp.dma_start(out.rearrange("b s d -> (b s) d").rearrange("(t p) d -> p t d", p=P), g.x[:, :, :]).then_inc(out_done, 16)
                sp.wait_ge(out_done, 16)

            @block.tensor
            def _(pe):
                for s in stages:
                    s["pe"](pe)

            @block.scalar
            def _(act):
                g.link["act"] = Link(act, chain["act"])
                for s in stages:
                    s["act"](act)

            @block.vector
            def _(dve):
                g.link["dve"] = Link(dve, chain["dve"])
                for s in stages:
                    s["dve"](dve)

            @block.gpsimd
            def _(pool):
                g.link["pool"] = Link(pool, chain["pool"])
                for s in stages:
                    s["pool"](pool)


def kernel(**inputs):
    import numpy as _np
    import concourse.bacc as _bacc
    from concourse import mybir as _mybir
    from concourse.bass_utils import run_bass_kernel_spmd as _run

    nc = _bacc.Bacc("TRN2", target_bir_lowering=False, num_devices=1)
    arrays, args = {}, {}
    for name in inputs:
        a = _np.ascontiguousarray(inputs[name])
        a = a.reshape(inputs[name].shape or (1,))
        if a.dtype == _np.bool_:
            words = a.reshape(-1).view(_np.int32)
            ap = nc.dram_tensor(f"in_{name}", words.shape, _mybir.dt.from_np(words.dtype), kind="ExternalInput").ap()
            arrays[f"in_{name}"] = words
            args[name] = ap.bitcast(U8).rearrange("(b s) -> b s", b=B)
        else:
            arrays[f"in_{name}"] = a
            args[name] = nc.dram_tensor(f"in_{name}", a.shape, _mybir.dt.from_np(a.dtype), kind="ExternalInput").ap()
    out = nc.dram_tensor("out", (B, S, D), F32, kind="ExternalOutput").ap()
    build(nc, args, out)
    r = _run(nc, [arrays], core_ids=[0])
    return r.results[0]["out"]
```

```python
from contextlib import ExitStack

import concourse.bass as bass
import concourse.mybir as mybir

F32 = mybir.dt.float32
BF16 = mybir.dt.bfloat16
U8 = mybir.dt.uint8
ALU = mybir.AluOpType
ACT = mybir.ActivationFunctionType
AX = mybir.AxisListType

P = 128
B, S, D = 8, 64, 128
NK, DC = 1601, 96
TOK = B * S
NT = TOK // P
NCH = (NK + P - 1) // P
FULL = NK // P
LASTK = NK - FULL * P
BANK = 512
NEG = -1.0e30
PI = 3.141592653589793
HALF_ULP = 12582912.0
RS = [BANK * i for i in range((NK + BANK - 1) // BANK)]
KSPAN = [(a, min(BANK, NK - a)) for a in RS]


class Flag:

    def __init__(self, sem):
        self.sem, self.base = sem, 0

    def __call__(self, n):
        return self.base + n


class View(Flag):
    def __init__(self, flag, total):
        self.sem, self.base = flag.sem, flag.base
        flag.base += total


class Link:

    def __init__(self, eng, sem):
        self.eng, self.sem, self.n = eng, sem, 0

    def __call__(self, ins):
        self.n += 1
        ins.then_inc(self.sem, 1)
        self.eng.wait_ge(self.sem, self.n)


class Arena:

    def __init__(self, tile, cols):
        self.tile, self.cols, self.at = tile, cols, 0

    def take(self, cols, dt=F32):
        n = cols if dt == F32 else (cols + 1) // 2
        a = self.tile[:, self.at:self.at + n]
        self.at += n
        assert self.at <= self.cols, (self.at, self.cols)
        if dt != F32:
            a = a.bitcast(dt)
        return a


class G:
    pass


def flags(g, **totals):
    made = {}
    for name, total in totals.items():
        if name not in g.flag:
            g.flag[name] = Flag(g.new_sem(name))
        made[name] = View(g.flag[name], total)
    return made


def steps(g, f, **order):
    made = dict(f)
    for name, events in order.items():
        if name not in g.flag:
            g.flag[name] = Flag(g.new_sem(name))
        for event in events.split():
            made[event] = View(g.flag[name], 1)
    return made


VEC_ROWS = [
    ("l0x_gx", "L0_xattn_ln_x_g", 1, DC), ("l0x_bx", "L0_xattn_ln_x_b", 1, DC),
    ("l0x_gl", "L0_xattn_ln_l_g", 1, D), ("l0x_bl", "L0_xattn_ln_l_b", 1, D),
    ("l0x_bo", "L0_xattn_bo", 1, D),
    ("l1x_bo", "L1_xattn_bo", 1, D), ("l2x_bo", "L2_xattn_b_out", 1, D),
    ("l2a_qkvb", "L2_attn_qkv_b", 3, D), ("l2a_pb", "L2_attn_proj_b", 1, D),
    ("l3x_bfi", "L3_xattn_b_film_in", 2, D), ("l3x_bfo", "L3_xattn_b_film_out", 2, D),
    ("l3x_gi", "L3_xattn_g_norm_in", 1, D), ("l3x_bi", "L3_xattn_b_norm_in", 1, D),
    ("l3x_gf", "L3_xattn_g_ffn", 1, D), ("l3x_bf", "L3_xattn_b_ffn", 1, D),
    ("l3x_b1", "L3_xattn_b1", 4, D), ("l3x_b2", "L3_xattn_b2", 1, D),
    ("l3x_skip", "L3_xattn_D_skip", 1, D), ("l3x_dt", "L3_xattn_log_dt", 1, D),
]
BCAST = [("l0a_w", "L0_attn_ln_weight"), ("l0a_b", "L0_attn_ln_bias"), ("l0a_bias", "L0_attn_bias"),
         ("l3x_go", "L3_xattn_g_norm_out"), ("l3x_bo", "L3_xattn_b_norm_out")]


def stage_setup(g):
    f = flags(g, zeros=1, consts=1, late_consts=1, x_in=16, vec_in=16 * (len(VEC_ROWS) + 6), vecs_T=1, vecs=1, bc_in=16 * (len(BCAST) + 4 + 4),
              mask_in=32, masks=1, vec_zero=1)
    names, n = {}, 0
    for name, _, rows, _ in VEC_ROWS:
        names[name] = n
        n += rows
    b1row = n
    n += 32
    nvec = n + 4
    g.col = lambda name, i=0, width=P: g.vcols[0:width, names[name] + i:names[name] + i + 1]
    g.moe_b1 = lambda e, c: g.vcols[:, b1row + 4 * e + c:b1row + 4 * e + c + 1]
    qg = n
    g.qn_col = g.vcols[:, qg:qg + 1]
    g.kn_col = g.vcols[:, qg + 1:qg + 2]

    def first(e):
        e.dma_start(g.x[:, :, :], g.a["x"].rearrange("b s d -> (b s) d").rearrange("(t p) d -> p t d", p=P)).then_inc(f["x_in"].sem, 16)

    def sp(e):
        e.wait_ge(f["vec_zero"].sem, f["vec_zero"](1))
        for name, arg, rows, width in VEC_ROWS:
            r = names[name]
            e.dma_start(g.vrows[r:r + rows, 0:width], g.a[arg].rearrange("(r w) -> r w", w=width)).then_inc(f["vec_in"].sem, 16)
        e.dma_start(g.vrows[b1row:b1row + 32, :], g.a["L3_ffn_b1"].rearrange("e (c w) -> (e c) w", w=P)).then_inc(f["vec_in"].sem, 16)
        for i, arg in enumerate(("L0_xattn_qn_g", "L0_xattn_kn_g")):
            for h in range(2):
                e.dma_start(g.vrows[qg + i:qg + i + 1, 64 * h:64 * h + 64], g.a[arg].rearrange("(r w) -> r w", r=1)).then_inc(f["vec_in"].sem, 16)
        e.dma_start(g.vrows[qg + 2:qg + 3, :], g.a["L3_xattn_g_norm_out"].rearrange("(r w) -> r w", r=1)).then_inc(f["vec_in"].sem, 16)
        e.dma_start(g.m8[0:8, 0, :], g.a["mask_BxS2_bk0"]).then_inc(f["mask_in"].sem, 16)
        e.dma_start(g.m8[0:8, 1, :], g.a["mask_BxS2_bf1"]).then_inc(f["mask_in"].sem, 16)
        for i, (name, arg) in enumerate(BCAST):
            e.dma_start(g.bc[:, i, :], g.a[arg].partition_broadcast(P)).then_inc(f["bc_in"].sem, 16)
        for i, (arg, w) in enumerate((("L0_ffn_clip_x", 1), ("L0_ffn_clip_down", 1), ("L3_ffn_b_router", 8))):
            e.dma_start(g.scal[:, 8 * i:8 * i + w], g.a[arg].partition_broadcast(P)).then_inc(f["bc_in"].sem, 16)
        e.dma_start(g.scal[:, 24:25], g.a["L3_xattn_mod_gate"].partition_broadcast(P)).then_inc(f["bc_in"].sem, 16)
        e.dma_start(g.scal[:, 32:48], g.a["L3_attn_compressibility"].rearrange("h a b -> (h a b)").partition_broadcast(P)).then_inc(f["bc_in"].sem, 16)
        e.dma_start(g.scal[:, 48:64], g.a["L3_attn_phase_threshold"].rearrange("h a b -> (h a b)").partition_broadcast(P)).then_inc(f["bc_in"].sem, 16)
        e.dma_start(g.tmask8[:, :], g.a["mask_BxS_bf1"].rearrange("b s -> (b s)").partition_broadcast(P)).then_inc(f["bc_in"].sem, 16)
        e.dma_start(g.b2moe[0:8, :], g.a["L3_ffn_b2"]).then_inc(f["bc_in"].sem, 16)
        for i, name in enumerate(("A_re", "A_im", "C_re", "C_im")):
            e.dma_start(g.s4in[:, S * i:S * i + S], g.a["L3_xattn_" + name]).then_inc(g.s4_sem, 16)

    def pool(e):
        ln = g.link["pool"]
        nc = g.nc
        ln(nc.gpsimd.memset(g.ident, 0.0))
        ln(nc.gpsimd.affine_select(out=g.ident, in_=g.ident, compare_op=ALU.not_equal, fill=1.0, base=0,
                                   pattern=[[-1, P]], channel_multiplier=1))
        ln(nc.gpsimd.memset(g.sel, 0.0))
        ln(nc.gpsimd.affine_select(out=g.sel, in_=g.sel, compare_op=ALU.not_equal, fill=1.0, base=0,
                                   pattern=[[-1, B], [0, P]], channel_multiplier=1))
        ln(nc.gpsimd.memset(g.ones, 1.0))
        ln(nc.gpsimd.memset(g.half, 0.5))
        ln(nc.gpsimd.memset(g.blk, 0.0))
        ln(nc.gpsimd.memset(g.blk[0:64, 0:64], 1.0))
        nc.gpsimd.memset(g.blk[64:128, 64:128], 1.0).then_inc(f["consts"].sem, 1)
        e.wait_ge(f["consts"].sem, f["consts"](1))
        ln(nc.gpsimd.memset(g.mask_bd, 0.0))
        ln(nc.gpsimd.memset(g.mask_bd[0:64, 64:128], NEG))
        ln(nc.gpsimd.memset(g.mask_bd[64:128, 0:64], NEG))
        ln(nc.gpsimd.memset(g.mask_ca, 0.0))
        ln(nc.gpsimd.affine_select(out=g.mask_ca, in_=g.mask_ca, compare_op=ALU.is_ge, fill=NEG, base=0,
                                   pattern=[[-1, P]], channel_multiplier=1))
        ln(nc.gpsimd.memset(g.mask_ca[64:128, 0:64], NEG))
        ln(nc.gpsimd.memset(g.tri_mul, 8.0 ** -0.5))
        ln(nc.gpsimd.affine_select(out=g.tri_mul, in_=g.tri_mul, compare_op=ALU.is_ge, fill=0.0, base=0,
                                   pattern=[[-1, P]], channel_multiplier=1))
        ln(nc.gpsimd.memset(g.tri_add, 0.0))
        ln(nc.gpsimd.affine_select(out=g.tri_add, in_=g.tri_add, compare_op=ALU.is_ge, fill=-10000.0, base=0,
                                   pattern=[[-1, P]], channel_multiplier=1))
        ln(nc.gpsimd.memset(g.head_of, 1.0))
        ln(nc.gpsimd.affine_select(out=g.head_of, in_=g.head_of, compare_op=ALU.is_ge, fill=0.0, base=0,
                                   pattern=[[-8, 16]], channel_multiplier=1))
        ln(nc.gpsimd.affine_select(out=g.head_of, in_=g.head_of, compare_op=ALU.is_ge, fill=0.0, base=7,
                                   pattern=[[8, 16]], channel_multiplier=-1))
        ln(nc.gpsimd.memset(g.before, 1.0))
        ln(nc.gpsimd.affine_select(out=g.before, in_=g.before, compare_op=ALU.is_gt, fill=0.0, base=0,
                                   pattern=[[1, 8], [-1, 8]], channel_multiplier=0))
        ln(nc.gpsimd.tensor_tensor(g.fold, g.ident[:, 0:64], g.ident[:, 64:128], ALU.add))
        ln(nc.gpsimd.memset(g.cT_hi[96:97, :, :], 1.0))
        ln(nc.gpsimd.memset(g.cT_lo[96:97, :, :], 0.0))
        ln(nc.gpsimd.memset(g.cr_hi[:, :, :, 96:97], 1.0))
        ln(nc.gpsimd.memset(g.cr_lo[:, :, :, 96:97], 0.0))
        ln(nc.gpsimd.memset(g.neg_blk[0:64, 0:64], -1.0))
        ln(nc.gpsimd.memset(g.neg_blk[64:128, 64:128], -1.0))
        ln(nc.gpsimd.memset(g.neg_blk[0:64, 64:128], 0.0))
        nc.gpsimd.memset(g.neg_blk[64:128, 0:64], 0.0).then_inc(f["late_consts"].sem, 1)

    def dve(e):
        nc = g.nc
        ln = g.link["dve"]
        nc.vector.memset(g.vrows, 0.0).then_inc(f["vec_zero"].sem, 1)
        e.wait_ge(f["x_in"].sem, f["x_in"](16))

    def dve_vectors(e):
        e.wait_ge(f["vecs_T"].sem, f["vecs_T"](1))
        g.nc.vector.tensor_copy(g.vcols[:, 0:nvec], g.ps[:, 7, 0:nvec]).then_inc(f["vecs"].sem, 1)
        e.wait_ge(f["vecs"].sem, f["vecs"](1))

    def dve_masks(e):
        v = g.nc.vector
        e.wait_ge(f["consts"].sem, f["consts"](1))
        e.wait_ge(f["mask_in"].sem, f["mask_in"](32))
        g.link["dve"](v.tensor_copy(g.mtmp[0:8, :, :], g.m8[0:8, :, :]))
        v.tensor_scalar(g.kmask[0:8, :, :], g.mtmp[0:8, :, :], -1.0, -NEG, ALU.add, ALU.mult).then_inc(f["masks"].sem, 1)

    def pe_vectors(e):
        e.wait_ge(f["vec_in"].sem, f["vec_in"](16 * (len(VEC_ROWS) + 6)))
        g.nc.tensor.transpose(g.ps[:, 7, 0:nvec], g.vrows[0:nvec, :], g.ident[0:nvec, 0:nvec]).then_inc(f["vecs_T"].sem, 1)

    def wait_rest(e):
        e.wait_ge(f["late_consts"].sem, f["late_consts"](1))
        e.wait_ge(f["bc_in"].sem, f["bc_in"](16 * (len(BCAST) + 8)))

    g.dve_vectors, g.dve_masks, g.pe_vectors, g.wait_rest = dve_vectors, dve_masks, pe_vectors, wait_rest
    return dict(first=first, load=nothing, sp=sp, pool=pool, dve=dve, pe=nothing, act=nothing)


def table(g):
    g.nc.scalar.preload_act_table_set("natural_log_exp_and_others")


def layernorm(g, src, out_rows, eps=1e-5, out_T=None, gain=None, shift=None, bank=7):
    turned = 0 if out_T is None else 1
    f = flags(g, ln_var=1, ln_std=1, ln_rows=1, ln_T=turned, ln_ready=turned)

    def dve(e):
        nc, ln = g.nc, g.link["dve"]
        for t in range(NT):
            ln(nc.vector.bn_stats(g.st[:, 6 * t:6 * t + 6], src[:, t, :]))
        for t in range(NT):
            i = nc.vector.bn_aggr(g.mv[:, 2 * t:2 * t + 2], g.st[:, 6 * t:6 * t + 6])
        ln(i)
        mv = g.mv.rearrange("p (t two) -> p t two", two=2)
        nc.vector.tensor_scalar(g.ve, mv[:, :, 1], eps, None, ALU.add).then_inc(f["ln_var"].sem, 1)
        e.wait_ge(f["ln_std"].sem, f["ln_std"](1))
        for t in range(NT):
            i = nc.vector.tensor_scalar(out_rows[:, t, :], src[:, t, :], g.mv[:, 2 * t:2 * t + 1],
                                        g.rstd[:, t:t + 1], ALU.subtract, ALU.mult)
        i.then_inc(f["ln_rows"].sem, 1)
        e.wait_ge(f["ln_rows"].sem, f["ln_rows"](1))
        if out_T is not None:
            e.wait_ge(f["ln_T"].sem, f["ln_T"](1))
            if gain is None:
                i = nc.vector.tensor_copy(out_T, g.ps[:, bank, :])
            else:
                i = nc.vector.tensor_scalar(out_T, g.ps[:, bank, :], gain, shift, ALU.mult, ALU.add)
            i.then_inc(f["ln_ready"].sem, 1)
            e.wait_ge(f["ln_ready"].sem, f["ln_ready"](1))

    def act(e):
        e.wait_ge(f["ln_var"].sem, f["ln_var"](1))
        g.link["act"](g.nc.scalar.activation(g.sd, g.ve, ACT.Ln))
        g.nc.scalar.activation(g.rstd, g.sd, ACT.Exp, scale=-0.5).then_inc(f["ln_std"].sem, 1)

    def pe(e):
        if out_T is None:
            return
        e.wait_ge(f["ln_rows"].sem, f["ln_rows"](1))
        for t in range(NT):
            i = g.nc.tensor.transpose(g.ps[:, bank, P * t:P * t + P], out_rows[:, t, :], g.ident)
        i.then_inc(f["ln_T"].sem, 1)

    return dict(dve=dve, act=act, pe=pe, ready=f["ln_ready"], f=f)


def add_back(g, yT, yT_flag, bank=7):
    f = flags(g, back_T=1, x_done=1)

    def pe(e):
        e.wait_ge(yT_flag.sem, yT_flag(1))
        for t in range(NT):
            i = g.nc.tensor.transpose(g.ps[:, bank, P * t:P * t + P], yT[:, P * t:P * t + P], g.ident)
        i.then_inc(f["back_T"].sem, 1)

    def dve(e):
        e.wait_ge(f["back_T"].sem, f["back_T"](1))
        g.nc.vector.tensor_tensor(g.x2d, g.x2d, g.ps[:, bank, :], ALU.add).then_inc(f["x_done"].sem, 1)
        e.wait_ge(f["x_done"].sem, f["x_done"](1))
    return dict(pe=pe, dve=dve, x_done=f["x_done"])


def add_rows(g, bank, ready):
    f = flags(g, x_done=1)

    def dve(e):
        e.wait_ge(ready.sem, ready(1))
        g.nc.vector.tensor_tensor(g.x2d, g.x2d, g.ps[:, bank, :], ALU.add).then_inc(f["x_done"].sem, 1)
        e.wait_ge(f["x_done"].sem, f["x_done"](1))
    return dict(dve=dve, x_done=f["x_done"])


def layer_l0_cross(g):
    nc = g.nc
    tmp = g.temps()
    NKL = NK + S
    pre = Arena(g.pre, 4096)
    spare = Arena(g.slot[1][:, 8 * P:4096], 4096 - 8 * P)
    raw = [a.take(NCH * DC).rearrange("p (c d) -> p c d", d=DC) for a in (tmp, spare)]
    cst = tmp.take(6 * NCH)
    cmv = tmp.take(2 * NCH)
    cve, csd, crs = tmp.take(NCH), tmp.take(NCH), tmp.take(NCH)
    xnT = tmp.take(NK)
    ksq = tmp.take(NKL)
    prob = tmp.take(NKL)
    kinv = tmp.take(NKL)
    PT = spare.take((NCH + 1) * P).rearrange("p (c n) -> p c n", n=P)
    knT = tmp.take(NKL)
    V = pre.take((NCH + 1) * P).rearrange("p (c n) -> p c n", n=P)
    lat = g.xn
    oT = tmp.take(TOK)
    lat2 = oT.rearrange("p (t d) -> p t d", d=D)
    lT = g.xnT
    qsq, qinv, yT = ksq[:, 0:TOK], kinv[:, 0:TOK], xnT[:, 0:TOK]
    Qbd = pre.take(B * P).rearrange("p (b n) -> p b n", b=B)
    diag = tmp.take(P)
    mx, nmx, z, zi = (tmp.take(B) for _ in range(4))
    qfac = tmp.take(1)
    wT = pre.take(6 * P)
    w = g.slot[0]
    wq, wo, wlk, wlv = (w[:, P * i:P * i + P] for i in range(4))
    wk, wv = w[:, 4 * P:4 * P + DC], w[:, 5 * P:5 * P + DC]
    A = g.ps[:, 0:4, :].rearrange("p a n -> p (a n)")
    Bk = g.ps[:, 4:8, :].rearrange("p a n -> p (a n)")
    wqT, woT, wlkT, wlvT = (wT[:, P * i:P * i + P] for i in range(4))
    wkT, wvT = wT[0:DC, 4 * P:5 * P], wT[0:DC, 5 * P:6 * P]

    ln1 = layernorm(g, g.x, lat)
    ln2 = layernorm(g, lat, lat2, out_T=lT, gain=g.col("l0x_gl"), shift=g.col("l0x_bl"))
    f = flags(g, raw_zero=1, l0_w_in=16 * 6, raw_in0=32 * 4, raw_in1=32 * 4, 
              cT_mm=B, cT_hi=B, c_var=B, c_std=B,
              c_rows=B, xh_T=B, xn_ready=B, k_mm=B, k_sq=B, k_ss=B, k_max=B, k_inv=B, k_ready=B, v_mm=B, v_ready=B,
              l0_s=B, l0_max=B, l0_p=B, l0_diag=B, l0_pt=B, l0_pt_a=B, l0_pt_d=B, l0_o=B, l0_o_sb=B)
    f = steps(g, f, rows_T="l0_wT", products="q_mm q_ss l0_y", dve_step="l0_w_ready q_max q_ready l0_yT", act_step="q_sq q_inv")
    back = add_back(g, yT, f["l0_yT"])
    raw_in = [f["raw_in0"], f["raw_in1"]]
    HALF = 8

    def load(e):
        a = g.a
        for dst, src in ((wq, a["L0_xattn_Wq"]), (wo, a["L0_xattn_Wo"]), (wlk, a["L0_xattn_Wlkv"][0:P, :]),
                         (wlv, a["L0_xattn_Wlkv"][P:2 * P, :]), (wk, a["L0_xattn_Wkv"][0:P, :]), (wv, a["L0_xattn_Wkv"][P:2 * P, :])):
            e.dma_start(dst, src).then_inc(f["l0_w_in"].sem, 16)

    def fetch(e, b):
        r, q = raw[b % 2], raw_in[b % 2]
        e.dma_start(r[:, 0:FULL, :], g.a["ctx_768"][b, 0:FULL * P, :].rearrange("(c p) d -> p c d", p=P)).then_inc(q.sem, 16)
        e.dma_start(r[0:LASTK, FULL, :], g.a["ctx_768"][b, FULL * P:NK, :]).then_inc(q.sem, 16)

    def early(e):
        e.wait_ge(f["raw_zero"].sem, f["raw_zero"](1))
        fetch(e, 0)

    def sp(e):
        fetch(e, 1)
        for b in range(2, B):
            e.wait_ge(f["xh_T"].sem, f["xh_T"](b - 1))
            fetch(e, b)

    def dve(e):
        ln = g.link["dve"]
        v = nc.vector

        def split_rows(b):
            r = raw[b % 2]
            e.wait_ge(raw_in[b % 2].sem, raw_in[b % 2](32 * (b // 2 + 1)))
            ln(v.tensor_copy(g.cr_hi[:, b, :, 0:DC], r))
            v.tensor_tensor(g.cr_lo[:, b, :, 0:DC], r, g.cr_hi[:, b, :, 0:DC], ALU.subtract)
            for c in range(NCH):
                i = v.bn_stats(cst[:, 6 * c:6 * c + 6], r[:, c, :])
            ln(i)
            for c in range(NCH):
                i = v.bn_aggr(cmv[:, 2 * c:2 * c + 2], cst[:, 6 * c:6 * c + 6])
            ln(i)
            mv = cmv.rearrange("p (c two) -> p c two", two=2)
            v.tensor_scalar(cve, mv[:, :, 1], 1e-5, None, ALU.add).then_inc(f["c_var"].sem, 1)

        v.memset(raw[0][:, FULL, :], 0.0)
        v.memset(raw[1][:, FULL, :], 0.0).then_inc(f["raw_zero"].sem, 1)
        ln(v.memset(Qbd, 0.0))
        ln1["dve"](e)
        e.wait_ge(f["l0_wT"].sem, f["l0_wT"](1))
        v.tensor_copy(wT[:, 0:4 * P], A[:, 0:4 * P])
        v.tensor_copy(wT[0:DC, 4 * P:6 * P], A[0:DC, 4 * P:6 * P]).then_inc(f["l0_w_ready"].sem, 1)
        split_rows(0)
        g.dve_vectors(e)
        ln(v.tensor_scalar(qfac, g.qn_col, g.kn_col, 8.0, ALU.mult, ALU.mult))
        ln2["dve"](e)
        e.wait_ge(f["q_ss"].sem, f["q_ss"](1))
        v.tensor_scalar(qinv, Bk[:, 0:TOK], 64.0e-16, None, ALU.max).then_inc(f["q_max"].sem, 1)
        e.wait_ge(f["q_inv"].sem, f["q_inv"](1))
        for h in range(2):
            r = slice(64 * h, 64 * h + 64)
            i = v.scalar_tensor_tensor(out=Qbd[r, :, 64 * h:64 * h + 64], in0=A[r, 0:TOK].rearrange("p (b s) -> p b s", b=B),
                                       scalar=qfac[r, :], in1=qinv[r, :].rearrange("p (b s) -> p b s", b=B),
                                       op0=ALU.mult, op1=ALU.mult)
        i.then_inc(f["q_ready"].sem, 1)

        def norm_rows(b):
            r = raw[b % 2]
            e.wait_ge(f["cT_hi"].sem, f["cT_hi"](b + 1))
            v.tensor_tensor(g.cT_lo[0:DC, b, :], A[0:DC, 0:NK], g.cT_hi[0:DC, b, :], ALU.subtract)
            e.wait_ge(f["c_std"].sem, f["c_std"](b + 1))
            e.wait_ge(f["cT_mm"].sem, f["cT_mm"](b + 1))
            for c in range(NCH):
                i = v.tensor_scalar(r[:, c, :], r[:, c, :], cmv[:, 2 * c:2 * c + 1], crs[:, c:c + 1], ALU.subtract, ALU.mult)
            i.then_inc(f["c_rows"].sem, 1)

        def key_squares(b):
            e.wait_ge(f["k_ss"].sem, f["k_ss"](b + 1))
            v.tensor_scalar(kinv, A[:, 0:NKL], 64.0e-16, None, ALU.max).then_inc(f["k_max"].sem, 1)

        def keys(b):
            e.wait_ge(f["k_inv"].sem, f["k_inv"](b + 1))
            v.tensor_tensor(knT, knT, kinv, ALU.mult).then_inc(f["k_ready"].sem, 1)

        def row_max(b):
            e.wait_ge(f["l0_s"].sem, f["l0_s"](b + 1))
            ln(v.tensor_reduce(mx[:, b:b + 1], Bk[:, 0:NKL], AX.X, ALU.max))
            v.tensor_scalar(nmx[:, b:b + 1], mx[:, b:b + 1], -1.0, None, ALU.mult).then_inc(f["l0_max"].sem, 1)

        def inverse_sum(b):
            e.wait_ge(f["l0_p"].sem, f["l0_p"](b + 1))
            ln(v.reciprocal(zi[:, b:b + 1], z[:, b:b + 1]))
            v.tensor_scalar(diag, g.ident, zi[:, b:b + 1], None, ALU.mult).then_inc(f["l0_diag"].sem, 1)

        def probs_T(b):
            e.wait_ge(f["l0_pt"].sem, f["l0_pt"](b + 1))
            v.tensor_copy(PT[:, HALF:FULL, :], Bk[:, HALF * P:FULL * P].rearrange("p (c n) -> p c n", n=P))
            v.tensor_copy(PT[0:LASTK, FULL, :], Bk[0:LASTK, FULL * P:FULL * P + P])
            v.tensor_copy(PT[0:S, NCH, :], Bk[0:S, NCH * P:NCH * P + P]).then_inc(f["l0_pt_d"].sem, 1)

        def out_heads(b):
            e.wait_ge(f["l0_o"].sem, f["l0_o"](b + 1))
            for h in range(2):
                q = slice(64 * h, 64 * h + 64)
                i = v.tensor_copy(oT[q, S * b:S * b + S], Bk[q, 64 * h:64 * h + 64])
            i.then_inc(f["l0_o_sb"].sem, 1)

        norm_rows(0)
        key_squares(0)
        g.dve_masks(e)
        split_rows(1)
        keys(0)
        for b in range(B):
            more = b + 1 < B
            if more:
                norm_rows(b + 1)
            row_max(b)
            inverse_sum(b)
            probs_T(b)
            if more:
                key_squares(b + 1)
            out_heads(b)
            if b + 2 < B:
                split_rows(b + 2)
            if more:
                keys(b + 1)
        e.wait_ge(f["l0_y"].sem, f["l0_y"](1))
        v.tensor_scalar(yT, Bk[:, 0:TOK], g.col("l0x_bo"), None, ALU.add).then_inc(f["l0_yT"].sem, 1)
        back["dve"](e)

    def act(e):
        s = nc.scalar
        ln1["act"](e)
        e.wait_ge(g.flag["vecs"].sem, 1)
        ln2["act"](e)
        e.wait_ge(f["q_mm"].sem, f["q_mm"](1))
        s.activation(qsq, A[:, 0:TOK], ACT.Square).then_inc(f["q_sq"].sem, 1)
        e.wait_ge(f["q_max"].sem, f["q_max"](1))
        g.link["act"](s.activation(qsq, qinv, ACT.Ln))
        s.activation(qinv, qsq, ACT.Exp, scale=-0.5).then_inc(f["q_inv"].sem, 1)

        def context_T(b):
            e.wait_ge(f["cT_mm"].sem, f["cT_mm"](b + 1))
            s.activation(g.cT_hi[0:DC, b, :], A[0:DC, 0:NK], ACT.Copy).then_inc(f["cT_hi"].sem, 1)

        def row_std(b):
            e.wait_ge(f["c_var"].sem, f["c_var"](b + 1))
            g.link["act"](s.activation(csd, cve, ACT.Ln))
            s.activation(crs, csd, ACT.Exp, scale=-0.5).then_inc(f["c_std"].sem, 1)

        def gains(b):
            e.wait_ge(f["xh_T"].sem, f["xh_T"](b + 1))
            s.activation(xnT[0:DC, :], A[0:DC, 0:NK], ACT.Identity, bias=g.col("l0x_bx", 0, DC),
                         scale=g.col("l0x_gx", 0, DC)).then_inc(f["xn_ready"].sem, 1)

        def squares(b):
            e.wait_ge(f["k_mm"].sem, f["k_mm"](b + 1))
            s.activation(ksq, A[:, 0:NKL], ACT.Square)
            s.activation(knT, A[:, 0:NKL], ACT.Copy).then_inc(f["k_sq"].sem, 1)

        def inverse_rms(b):
            e.wait_ge(f["k_max"].sem, f["k_max"](b + 1))
            g.link["act"](s.activation(ksq, kinv, ACT.Ln))
            s.activation(kinv, ksq, ACT.Exp, scale=-0.5).then_inc(f["k_inv"].sem, 1)

        def values(b):
            e.wait_ge(f["v_mm"].sem, f["v_mm"](b + 1))
            s.activation(V[:, 0:FULL, :], Bk[:, 0:FULL * P].rearrange("p (c n) -> p c n", n=P), ACT.Copy)
            s.activation(V[0:LASTK, FULL, :], Bk[0:LASTK, FULL * P:FULL * P + P], ACT.Copy)
            s.activation(V[0:S, NCH, :], Bk[0:S, NCH * P:NCH * P + P], ACT.Copy).then_inc(f["v_ready"].sem, 1)

        def probs(b):
            e.wait_ge(f["l0_max"].sem, f["l0_max"](b + 1))
            s.activation(prob, Bk[:, 0:NKL], ACT.Exp, bias=nmx[:, b:b + 1], accum_out=z[:, b:b + 1]).then_inc(f["l0_p"].sem, 1)

        def probs_T(b):
            e.wait_ge(f["l0_pt"].sem, f["l0_pt"](b + 1))
            s.activation(PT[:, 0:HALF, :], Bk[:, 0:HALF * P].rearrange("p (c n) -> p c n", n=P), ACT.Copy).then_inc(f["l0_pt_a"].sem, 1)

        row_std(0)
        context_T(0)
        gains(0)
        squares(0)
        inverse_rms(0)
        values(0)
        row_std(1)
        for b in range(B):
            more = b + 1 < B
            if more:
                context_T(b + 1)
                gains(b + 1)
            probs(b)
            if more:
                squares(b + 1)
            probs_T(b)
            if more:
                inverse_rms(b + 1)
                values(b + 1)
            if b + 2 < B:
                row_std(b + 2)

    def pe(e):
        t = nc.tensor
        e.wait_ge(g.flag["consts"].sem, 1)
        e.wait_ge(f["l0_w_in"].sem, f["l0_w_in"](96))
        for i, m in enumerate((wq, wo, wlk, wlv)):
            t.transpose(A[:, P * i:P * i + P], m, g.ident)
        t.transpose(A[0:DC, 4 * P:5 * P], wk, g.ident)
        t.transpose(A[0:DC, 5 * P:6 * P], wv, g.ident).then_inc(f["l0_wT"].sem, 1)
        g.pe_vectors(e)
        ln1["pe"](e)
        ln2["pe"](e)
        e.wait_ge(f["l0_w_ready"].sem, f["l0_w_ready"](1))
        e.wait_ge(ln2["ready"].sem, ln2["ready"](1))
        t.matmul(A[:, 0:TOK], wqT, lT, start=True, stop=True).then_inc(f["q_mm"].sem, 1)
        e.wait_ge(f["q_sq"].sem, f["q_sq"](1))
        t.matmul(Bk[:, 0:TOK], g.blk, qsq, start=True, stop=True).then_inc(f["q_ss"].sem, 1)
        e.wait_ge(f["q_ready"].sem, f["q_ready"](1))

        def transposed(b, done):
            for c in range(NCH):
                n = P if c < FULL else LASTK
                i = t.transpose(A[0:DC, P * c:P * c + n], raw[b % 2][0:n, c, :], g.ident[0:n, 0:n])
            i.then_inc(done.sem, 1)

        def context_T(b):
            e.wait_ge(raw_in[b % 2].sem, raw_in[b % 2](32 * (b // 2 + 1)))
            if b:
                e.wait_ge(f["k_max"].sem, f["k_max"](b))
            transposed(b, f["cT_mm"])

        def rows_T(b):
            e.wait_ge(f["c_rows"].sem, f["c_rows"](b + 1))
            transposed(b, f["xh_T"])

        def keys(b):
            e.wait_ge(f["xn_ready"].sem, f["xn_ready"](b + 1))
            for a, n in KSPAN:
                t.matmul(A[:, a:a + n], wkT, xnT[0:DC, a:a + n], start=True, stop=True)
            t.matmul(A[:, NK:NKL], wlkT, lT[:, S * b:S * b + S], start=True, stop=True).then_inc(f["k_mm"].sem, 1)

        def square_sums(b):
            e.wait_ge(f["k_sq"].sem, f["k_sq"](b + 1))
            for a in RS:
                n = min(BANK, NKL - a)
                i = t.matmul(A[:, a:a + n], g.blk, ksq[:, a:a + n], start=True, stop=True)
            i.then_inc(f["k_ss"].sem, 1)

        def values(b):
            if b:
                e.wait_ge(f["l0_o_sb"].sem, f["l0_o_sb"](b))
            for c in range(NCH):
                n = P if c < FULL else LASTK
                t.matmul(Bk[0:n, P * c:P * c + P], xnT[0:DC, P * c:P * c + n], wvT, start=True, stop=True)
            t.matmul(Bk[0:S, P * NCH:P * NCH + P], lT[:, S * b:S * b + S], wlvT, start=True, stop=True).then_inc(f["v_mm"].sem, 1)

        def scores(b):
            if b == 0:
                e.wait_ge(g.flag["masks"].sem, 1)
            e.wait_ge(f["k_ready"].sem, f["k_ready"](b + 1))
            e.wait_ge(f["v_ready"].sem, f["v_ready"](b + 1))
            for a, n in KSPAN:
                t.matmul(Bk[:, a:a + n], Qbd[:, b, :], knT[:, a:a + n], start=True, stop=False)
                t.matmul(Bk[:, a:a + n], g.sel[:, b, :], g.kmask[0:8, 0, a:a + n], start=False, stop=True)
            t.matmul(Bk[:, NK:NKL], Qbd[:, b, :], knT[:, NK:NKL], start=True, stop=True).then_inc(f["l0_s"].sem, 1)

        def probs_T(b):
            e.wait_ge(f["l0_diag"].sem, f["l0_diag"](b + 1))
            for c in range(NCH + 1):
                n = P if c < FULL else LASTK if c == FULL else S
                a = P * c if c <= FULL else NK
                i = t.matmul(Bk[0:n, P * c:P * c + P], prob[:, a:a + n], diag, start=True, stop=True)
            i.then_inc(f["l0_pt"].sem, 1)

        def out_heads(b):
            e.wait_ge(f["l0_pt_a"].sem, f["l0_pt_a"](b + 1))
            e.wait_ge(f["l0_pt_d"].sem, f["l0_pt_d"](b + 1))
            for c in range(NCH + 1):
                n = P if c < FULL else LASTK if c == FULL else S
                i = t.matmul(Bk[:, 0:P], V[0:n, c, :], PT[0:n, c, :], start=c == 0, stop=c == NCH)
            i.then_inc(f["l0_o"].sem, 1)

        context_T(0)
        rows_T(0)
        keys(0)
        square_sums(0)
        values(0)
        for b in range(B):
            more = b + 1 < B
            if more:
                context_T(b + 1)
            scores(b)
            if more:
                rows_T(b + 1)
                keys(b + 1)
            probs_T(b)
            if more:
                square_sums(b + 1)
            out_heads(b)
            if more:
                values(b + 1)
        e.wait_ge(f["l0_o_sb"].sem, f["l0_o_sb"](B))
        t.matmul(Bk[:, 0:TOK], woT, oT, start=True, stop=True).then_inc(f["l0_y"].sem, 1)
        back["pe"](e)

    def pool(e):
        pass

    return dict(early=early, load=load, sp=sp, dve=dve, act=act, pe=pe, pool=pool)


def wait_slot(g, e, layer):
    if layer >= 2:
        e.wait_ge(g.flag["x_done"].sem, layer - 1)


def layer_l0_cosine(g):
    nc = g.nc
    tmp = g.temps()
    NI = 4
    w = g.slot[1]
    kw = w[:, 0:NI * D].rearrange("p (c d) -> p c d", d=D)
    qw = w[:, NI * D:2 * NI * D].rearrange("p (c d) -> p c d", d=D)
    rows = tmp.take(NT * D).rearrange("p (t d) -> p t d", d=D)
    sq = tmp.take(NT * D).rearrange("p (t d) -> p t d", d=D)
    kn = tmp.take(NT * D).rearrange("p (t d) -> p t d", d=D)
    ss, sd, inv = (tmp.take(NT) for _ in range(3))
    kss, ksd, kin = (tmp.take(NT) for _ in range(3))
    QT, KT = tmp.take(TOK), tmp.take(TOK)
    c = tmp.take(NI * TOK)
    a = tmp.take(NI * TOK)
    t = tmp.take(NI * TOK)
    A = g.ps[:, 0:4, :].rearrange("p a n -> p (a n)")
    ln1 = layernorm(g, g.x, g.xn)
    ln2 = layernorm(g, g.xn, g.xn, eps=1e-12)
    f = steps(g, flags(g, a0_w_in=32, x_done=1), sums_ready="a0_kss a0_ss a0_xss", stds_ready="a0_kstd a0_std a0_xstd",
              rows_ready="a0_krows a0_rows", rows_T="a0_KT a0_QT", T_ready="a0_KT_sb a0_QT_sb", products="a0_s a0_X",
              act_step="a0_den a0_angle a0_p8", dve_step="a0_clip a0_ratio a0_B")

    def load(e):
        for dst, name in ((kw, "L0_attn_k_weight"), (qw, "L0_attn_q_weight")):
            e.dma_start(dst, g.a[name].rearrange("(c p) d -> p c d", p=P)).then_inc(f["a0_w_in"].sem, 16)

    def l2rows(e, src, ss, sq, flag):
        ln, v = g.link["dve"], nc.vector
        ln(v.tensor_tensor(sq, src, src, ALU.mult))
        ln(v.tensor_reduce(ss, sq, AX.X, ALU.add))
        v.tensor_scalar(ss, ss, 1e-24, None, ALU.max).then_inc(flag.sem, 1)

    def dve(e):
        g.wait_rest(e)
        nc.vector.tensor_copy(g.tmask, g.tmask8)
        ln, v = g.link["dve"], nc.vector
        e.wait_ge(f["a0_w_in"].sem, f["a0_w_in"](32))
        l2rows(e, kw, kss, sq, f["a0_kss"])
        e.wait_ge(f["a0_kstd"].sem, f["a0_kstd"](1))
        ln(v.reciprocal(kin, ksd))
        for j in range(NT):
            i = v.tensor_scalar(kn[:, j, :], kw[:, j, :], kin[:, j:j + 1], None, ALU.mult)
        i.then_inc(f["a0_krows"].sem, 1)
        e.wait_ge(f["a0_KT"].sem, f["a0_KT"](1))
        v.tensor_copy(KT, g.ps[:, 4, :]).then_inc(f["a0_KT_sb"].sem, 1)
        ln1["dve"](e)
        ln2["dve"](e)
        for j in range(NT):
            i = v.tensor_tensor(rows[:, j, :], g.xn[:, j, :], g.bcv["l0a_w"], ALU.mult)
        ln(i)
        for j in range(NT):
            i = v.tensor_tensor(rows[:, j, :], rows[:, j, :], g.bcv["l0a_b"], ALU.add)
        ln(i)
        l2rows(e, rows, ss, sq, f["a0_ss"])
        e.wait_ge(f["a0_std"].sem, f["a0_std"](1))
        ln(v.reciprocal(inv, sd))
        for j in range(NT):
            i = v.tensor_scalar(rows[:, j, :], rows[:, j, :], inv[:, j:j + 1], None, ALU.mult)
        i.then_inc(f["a0_rows"].sem, 1)
        e.wait_ge(f["a0_QT"].sem, f["a0_QT"](1))
        v.tensor_copy(QT, g.ps[:, 5, :]).then_inc(f["a0_QT_sb"].sem, 1)
        e.wait_ge(f["a0_s"].sem, f["a0_s"](1))
        v.tensor_scalar(c, A, -1.0 + 1e-6, 1.0 - 1e-6, ALU.max, ALU.min).then_inc(f["a0_clip"].sem, 1)
        e.wait_ge(f["a0_den"].sem, f["a0_den"](1))
        ln(v.tensor_scalar(t, t, 1.0, None, ALU.add))
        ln(v.tensor_tensor(t, t, a, ALU.mult))
        ln(v.tensor_scalar(t, t, -1.0, 2.0, ALU.mult, ALU.add))
        ln(v.tensor_tensor(a, a, t, ALU.mult))
        v.tensor_tensor(c, c, a, ALU.mult).then_inc(f["a0_ratio"].sem, 1)
        e.wait_ge(f["a0_angle"].sem, f["a0_angle"](1))
        ln(v.tensor_scalar(t, a, 2.0 / PI, 0.5, ALU.mult, ALU.add))
        e.wait_ge(f["a0_p8"].sem, f["a0_p8"](1))
        v.tensor_tensor(t, t, c, ALU.mult).then_inc(f["a0_B"].sem, 1)
        e.wait_ge(f["a0_X"].sem, f["a0_X"](1))
        ln(v.tensor_copy(rows, g.ps[:, 6, :].rearrange("p (t d) -> p t d", d=D)))
        l2rows(e, rows, ss, sq, f["a0_xss"])
        e.wait_ge(f["a0_xstd"].sem, f["a0_xstd"](1))
        ln(v.reciprocal(inv, sd))
        for j in range(NT):
            i = v.scalar_tensor_tensor(out=rows[:, j, :], in0=rows[:, j, :], scalar=inv[:, j:j + 1], in1=g.bcv["l0a_bias"],
                                       op0=ALU.mult, op1=ALU.add)
        ln(i)
        v.tensor_tensor(g.x[:, :, :], g.x[:, :, :], rows, ALU.add).then_inc(f["x_done"].sem, 1)
        e.wait_ge(f["x_done"].sem, f["x_done"](1))

    def act(e):
        g.wait_rest(e)
        s, ln = nc.scalar, g.link["act"]
        e.wait_ge(f["a0_kss"].sem, f["a0_kss"](1))
        s.activation(ksd, kss, ACT.Sqrt).then_inc(f["a0_kstd"].sem, 1)
        ln1["act"](e)
        ln2["act"](e)
        e.wait_ge(f["a0_ss"].sem, f["a0_ss"](1))
        s.activation(sd, ss, ACT.Sqrt).then_inc(f["a0_std"].sem, 1)
        e.wait_ge(f["a0_clip"].sem, f["a0_clip"](1))
        ln(s.activation(a, c, ACT.Square))
        ln(s.activation(t, a, ACT.Ln, scale=-1.0, bias=1.0))
        ln(s.activation(t, t, ACT.Exp, scale=0.5))
        ln(s.activation(a, t, ACT.Ln, bias=1.0))
        s.activation(a, a, ACT.Exp, scale=-1.0).then_inc(f["a0_den"].sem, 1)
        e.wait_ge(f["a0_ratio"].sem, f["a0_ratio"](1))
        s.activation(a, c, ACT.Arctan).then_inc(f["a0_angle"].sem, 1)
        e.wait_ge(f["a0_angle"].sem, f["a0_angle"](1))
        ln(s.activation(c, a, ACT.Square, scale=2.0 / PI, bias=g.half))
        ln(s.activation(c, c, ACT.Square))
        s.activation(c, c, ACT.Square).then_inc(f["a0_p8"].sem, 1)
        e.wait_ge(f["a0_xss"].sem, f["a0_xss"](1))
        s.activation(sd, ss, ACT.Sqrt).then_inc(f["a0_xstd"].sem, 1)

    def pe(e):
        g.wait_rest(e)
        m = nc.tensor
        e.wait_ge(f["a0_krows"].sem, f["a0_krows"](1))
        for j in range(NT):
            i = m.transpose(g.ps[:, 4, P * j:P * j + P], kn[:, j, :], g.ident)
        i.then_inc(f["a0_KT"].sem, 1)
        ln1["pe"](e)
        ln2["pe"](e)
        e.wait_ge(f["a0_rows"].sem, f["a0_rows"](1))
        for j in range(NT):
            i = m.transpose(g.ps[:, 5, P * j:P * j + P], rows[:, j, :], g.ident)
        i.then_inc(f["a0_QT"].sem, 1)
        e.wait_ge(f["a0_QT_sb"].sem, f["a0_QT_sb"](1))
        e.wait_ge(f["a0_KT_sb"].sem, f["a0_KT_sb"](1))
        for j in range(NI):
            i = m.matmul(g.ps[:, j, :], KT[:, P * j:P * j + P], QT, start=True, stop=True)
        i.then_inc(f["a0_s"].sem, 1)
        e.wait_ge(f["a0_B"].sem, f["a0_B"](1))
        for j in range(NT):
            for c_ in range(NI):
                i = m.matmul(g.ps[:, 6, P * j:P * j + P], t[:, TOK * c_ + P * j:TOK * c_ + P * j + P], qw[:, c_, :],
                             start=c_ == 0, stop=c_ == NI - 1)
        i.then_inc(f["a0_X"].sem, 1)

    return dict(load=load, sp=nothing, dve=dve, act=act, pe=pe, pool=nothing)


def nothing(e):
    pass


def global_max(g, src, n, dst, bank):
    f = flags(g, max_in=1, max_T=1, max_row=1, max_all=1)
    fin, fT, frow, fall = f["max_in"], f["max_T"], f["max_row"], f["max_all"]

    def pe(e):
        e.wait_ge(fin.sem, fin(1))
        g.nc.tensor.transpose(g.ps[0:1, bank, 0:n], src[0:n, :], g.ident[0:n, 0:n]).then_inc(fT.sem, 1)
        e.wait_ge(frow.sem, frow(1))
        g.nc.tensor.matmul(g.ps[:, bank, 128:129], g.ones[0:1, :], g.one_max, start=True, stop=True).then_inc(fall.sem, 1)

    def dve(e):
        e.wait_ge(fT.sem, fT(1))
        g.nc.vector.tensor_reduce(g.one_max, g.ps[0:1, bank, 0:n], AX.X, ALU.max).then_inc(frow.sem, 1)
        e.wait_ge(fall.sem, fall(1))
        g.link["dve"](g.nc.vector.tensor_copy(dst, g.ps[:, bank, 128:129]))
    return dict(pe=pe, dve=dve, ready=fin)


def layer_l0_quant_ffn(g):
    nc = g.nc
    tmp = g.temps()
    IC, NI = 88, 4
    w = g.slot[0]
    wg, wu = (w[0:IC, NI * D * i:NI * D * (i + 1)].rearrange("p (c d) -> p c d", d=D) for i in range(2))
    wd = w[:, 2 * NI * D:2 * NI * D + IC * NI]
    wgT, wuT = tmp.take(IC * NI, BF16), tmp.take(IC * NI, BF16)
    wdT = tmp.take(NI * D, BF16)
    swg, swu, iwg, iwu, sgx, sux = (tmp.take(NI)[0:IC, :] for _ in range(6))
    swd, iwd, sx, isx, sh, ish, gm, sig, amax, sdn = (tmp.take(1) for _ in range(10))
    sg2 = tmp.take(2)
    g.one_max = tmp.take(1)[0:1, :]
    xiT = tmp.take(TOK, BF16)
    sg = tmp.take(NI * TOK)[0:IC, :].rearrange("p (c n) -> p c n", c=NI)
    h = tmp.take(NI * TOK)[0:IC, :]
    hi = tmp.take(NI * TOK, BF16)[0:IC, :]
    yT = tmp.take(TOK)
    ln1 = layernorm(g, g.x, g.xn)
    f = steps(g, flags(g, f0_w_in=48), rows_ready="f0_wq f0_xi", rows_T="f0_wT f0_xiT", T_ready="f0_xiT_sb",
              products="f0_gu f0_y", act_step="f0_sig_e f0_silu", dve_step="f0_scale f0_hi f0_yT")
    gmx = global_max(g, amax, P, gm, 5)
    gmh = global_max(g, amax, IC, gm, 5)
    back = add_back(g, yT, f["f0_yT"])
    xrows = g.xn2d

    def load(e):
        wait_slot(g, e, 2)
        for dst, name in ((wg, "L0_ffn_w_gate"), (wu, "L0_ffn_w_up")):
            e.dma_start(dst, g.a[name].rearrange("(c p) d -> p c d", p=IC)).then_inc(f["f0_w_in"].sem, 16)
        e.dma_start(wd, g.a["L0_ffn_w_down"]).then_inc(f["f0_w_in"].sem, 16)

    def round_(v, ap, out, inv=None):
        ln = g.link["dve"]
        if inv is not None:
            ln(v.tensor_scalar(ap, ap, inv, -128.0, ALU.mult, ALU.max))
        else:
            ln(v.tensor_scalar(ap, ap, -128.0, None, ALU.max))
        ln(v.tensor_scalar(ap, ap, 127.0, HALF_ULP, ALU.min, ALU.add))
        return v.tensor_scalar(out, ap, HALF_ULP, None, ALU.subtract)

    def dve(e):
        ln, v = g.link["dve"], nc.vector
        e.wait_ge(f["f0_w_in"].sem, f["f0_w_in"](48))
        for wt, sw, iw in ((wg, swg, iwg), (wu, swu, iwu)):
            ln(v.tensor_reduce(iw, wt, AX.X, ALU.max, apply_absolute_value=True))
            ln(v.tensor_scalar(sw, iw, 1.0 / 127.0, None, ALU.mult))
            ln(v.reciprocal(iw, sw))
            for c in range(NI):
                i = v.tensor_scalar(wt[:, c, :], wt[:, c, :], iw[:, c:c + 1], None, ALU.mult)
            ln(i)
            ln(round_(v, wt, wt))
        ln(v.tensor_reduce(iwd, wd, AX.X, ALU.max, apply_absolute_value=True))
        ln(v.tensor_scalar(swd, iwd, 1.0 / 127.0, None, ALU.mult))
        ln(v.reciprocal(iwd, swd))
        round_(v, wd, wd, iwd).then_inc(f["f0_wq"].sem, 1)
        e.wait_ge(f["f0_wT"].sem, f["f0_wT"](1))
        v.tensor_copy(wgT, g.ps[:, 0, 0:IC * NI])
        v.tensor_copy(wuT, g.ps[:, 1, 0:IC * NI])
        ln(v.tensor_copy(wdT[0:IC, :], g.ps[0:IC, 2, :]))
        e.wait_ge(f["f0_sig_e"].sem, f["f0_sig_e"](1))
        ln(v.tensor_scalar(sg2, sg2, 1.0, None, ALU.add))
        ln(v.reciprocal(sg2, sg2))
        ln(v.tensor_scalar(sg2, sg2, 1.0 / 127.0, None, ALU.mult))
        ln1["dve"](e)
        v.tensor_reduce(amax, xrows, AX.X, ALU.max, apply_absolute_value=True).then_inc(gmx["ready"].sem, 1)
        gmx["dve"](e)
        ln(v.tensor_scalar(sx, gm, sg2[:, 0:1], None, ALU.mult))
        ln(v.reciprocal(isx, sx))
        round_(v, xrows, xrows, isx).then_inc(f["f0_xi"].sem, 1)
        e.wait_ge(f["f0_xiT"].sem, f["f0_xiT"](1))
        v.tensor_copy(xiT, g.ps[:, 6, :]).then_inc(f["f0_xiT_sb"].sem, 1)
        v.tensor_scalar(sgx, swg, sx[0:IC, :], None, ALU.mult)
        v.tensor_scalar(sux, swu, sx[0:IC, :], None, ALU.mult).then_inc(f["f0_scale"].sem, 1)
        e.wait_ge(f["f0_scale"].sem, f["f0_scale"](1))
        e.wait_ge(f["f0_silu"].sem, f["f0_silu"](1))
        for c in range(NI):
            i = v.scalar_tensor_tensor(out=h[:, TOK * c:TOK * c + TOK], in0=g.ps[0:IC, 4 + c, :], scalar=sux[:, c:c + 1],
                                       in1=sg[:, c, :], op0=ALU.mult, op1=ALU.mult)
        ln(i)
        v.tensor_reduce(amax[0:IC, :], h, AX.X, ALU.max, apply_absolute_value=True).then_inc(gmh["ready"].sem, 1)
        gmh["dve"](e)
        ln(v.tensor_scalar(sh, gm, sg2[:, 1:2], None, ALU.mult))
        ln(v.reciprocal(ish, sh))
        ln(v.tensor_scalar(sdn, swd, sh, None, ALU.mult))
        round_(v, h, hi, ish[0:IC, :]).then_inc(f["f0_hi"].sem, 1)
        e.wait_ge(f["f0_y"].sem, f["f0_y"](1))
        v.tensor_scalar(yT, g.ps[:, 0, :], sdn, None, ALU.mult).then_inc(f["f0_yT"].sem, 1)
        back["dve"](e)

    def act(e):
        s = nc.scalar
        e.wait_ge(g.flag["x_done"].sem, 2)
        s.activation(sg2, g.scal[:, 0:16:8], ACT.Exp, scale=-1.0).then_inc(f["f0_sig_e"].sem, 1)
        ln1["act"](e)
        e.wait_ge(f["f0_gu"].sem, f["f0_gu"](1))
        e.wait_ge(f["f0_scale"].sem, f["f0_scale"](1))
        for c in range(NI):
            i = s.activation(sg[:, c, :], g.ps[0:IC, c, :], ACT.Silu, scale=sgx[:, c:c + 1])
        i.then_inc(f["f0_silu"].sem, 1)

    def pe(e):
        m = nc.tensor
        e.wait_ge(f["f0_wq"].sem, f["f0_wq"](1))
        for c in range(NI):
            m.transpose(g.ps[:, 0, IC * c:IC * c + IC], wg[:, c, :], g.ident[0:IC, 0:IC])
            m.transpose(g.ps[:, 1, IC * c:IC * c + IC], wu[:, c, :], g.ident[0:IC, 0:IC])
            i = m.transpose(g.ps[0:IC, 2, D * c:D * c + D], wd[:, IC * c:IC * c + IC], g.ident)
        i.then_inc(f["f0_wT"].sem, 1)
        ln1["pe"](e)
        gmx["pe"](e)
        e.wait_ge(f["f0_xi"].sem, f["f0_xi"](1))
        for t in range(NT):
            i = m.transpose(g.ps[:, 6, P * t:P * t + P], g.xn[:, t, :], g.ident)
        i.then_inc(f["f0_xiT"].sem, 1)
        e.wait_ge(f["f0_xiT_sb"].sem, f["f0_xiT_sb"](1))
        for c in range(NI):
            m.matmul(g.ps[0:IC, c, :], wgT[:, IC * c:IC * c + IC], xiT, start=True, stop=True)
        for c in range(NI):
            i = m.matmul(g.ps[0:IC, 4 + c, :], wuT[:, IC * c:IC * c + IC], xiT, start=True, stop=True)
        i.then_inc(f["f0_gu"].sem, 1)
        gmh["pe"](e)
        e.wait_ge(f["f0_hi"].sem, f["f0_hi"](1))
        for c in range(NI):
            i = m.matmul(g.ps[:, 0, :], wdT[0:IC, D * c:D * c + D], hi[:, TOK * c:TOK * c + TOK], start=c == 0, stop=c == NI - 1)
        i.then_inc(f["f0_y"].sem, 1)
        back["pe"](e)

    return dict(load=load, sp=nothing, dve=dve, act=act, pe=pe, pool=nothing)


def start_layer(g, e, layer):
    e.wait_ge(g.flag["x_done"].sem, layer)


def cross_attention(g, layer, slot, names):
    nc = g.nc
    tmp = g.temps()
    H, DH = 16, 64
    PAIRS = H // 2
    R = H * S
    NR = R // P
    HB = R // BANK
    SCALE = DH ** -0.5
    w = g.slot[slot]
    wq, wk, wv = w[:, 0:R], w[0:DC, R:2 * R], w[0:DC, 2 * R:3 * R]
    wo = w[:, 3 * R:4 * R].rearrange("p (j n) -> p j n", j=PAIRS)
    pre = Arena(g.pre, 4096)
    Gh, Gl = (pre.take(H * DC, BF16) for _ in range(2))
    Nh, Nl = (pre.take(H * P, BF16)[0:DC, :] for _ in range(2))
    xh, xl = g.xn2d[:, 0:TOK // 2].bitcast(BF16), g.xn2d[:, TOK // 2:TOK].bitcast(BF16)
    qh = [tmp.take(R, BF16) for _ in range(2)]
    ql = [tmp.take(R, BF16) for _ in range(2)]
    pf = [tmp.take(R) for _ in range(2)]
    ph = [tmp.take(R, BF16) for _ in range(3)]
    pl = [tmp.take(R, BF16) for _ in range(3)]
    pm = tmp.take(4 * NR).rearrange("p (j s) -> p j s", s=4)
    m = tmp.take(NR)
    mrow = tmp.take(P, BF16)[0:NR, :]
    pc = tmp.take(R)
    pcn = tmp.take(R)
    rz = pcn[96:97, :]
    wT = [pcn[:, (P + 2 * DC) * i:(P + 2 * DC) * (i + 1)] for i in range(2)]
    pcnh, pcnl = (tmp.take(R, BF16) for _ in range(2))
    yT = tmp.take(TOK)
    ln1 = layernorm(g, g.x, g.xn, out_T=g.xnT)
    f = flags(g, x_w_in=64, x_wT=PAIRS, x_wT_sb=PAIRS, x_GN=PAIRS, x_GN_sb=PAIRS, x_zero=1, x_xh=1, x_xl=1, x_qk=B, x_qh=B, x_ql=B, x_unit=4 * NR * B,
              x_red=4 * NR * B, x_m=B, x_mT=B, x_mrow=B, x_m_in=16 * B, x_s=NCH * B, x_ph=NCH * B, x_pf=NCH * B, x_pl=NCH * B,
              x_pv=NCH * B, x_pc=B, x_rz=B, x_bc=B, x_pcn=B, x_y=B, x_y_sb=B)
    all_y = Flag(f["x_y_sb"].sem)
    all_y.base = f["x_y_sb"](B - 1)
    back = add_back(g, yT, all_y)
    S_ = [g.ps[:, 2 * i:2 * i + 2, :].rearrange("p a n -> p (a n)") for i in range(2)]
    ACC = g.ps[:, 4:6, :].rearrange("p a n -> p (a n)")
    MX = g.ps[:, 6:8, :].rearrange("p a n -> p (a n)")
    UNITS = {3: 5, 4: 5, 5: 5, 6: 5, 7: 4, 8: 4, 9: 4}
    assert sum(UNITS.values()) == 4 * NR

    def load(e):
        wait_slot(g, e, layer)
        e.dma_start(wq, g.a[names[0]]).then_inc(f["x_w_in"].sem, 16)
        e.dma_start(wk, g.a[names[1]]).then_inc(f["x_w_in"].sem, 16)
        e.dma_start(wv, g.a[names[2]]).then_inc(f["x_w_in"].sem, 16)
        e.dma_start(wo, g.a[names[3]].rearrange("(j p) n -> p j n", p=P)).then_inc(f["x_w_in"].sem, 16)

    def sp(e):
        for b in range(B):
            e.wait_ge(f["x_mrow"].sem, f["x_mrow"](b + 1))
            if b >= 2:
                e.wait_ge(f["x_s"].sem, f["x_s"](NCH * (b - 1)))
            e.dma_start(qh[b % 2][96:97, :], mrow).then_inc(f["x_m_in"].sem, 16)

    def pool(e):
        ln = g.link["pool"]
        start_layer(g, e, layer)
        ln(nc.gpsimd.memset(ql[0][96:97, :], 0.0))
        nc.gpsimd.memset(ql[1][96:97, :], 0.0).then_inc(f["x_zero"].sem, 1)
        for b in range(B):
            for c in range(NCH):
                k = NCH * b + c
                n = P if c < FULL else LASTK
                e.wait_ge(f["x_ph"].sem, f["x_ph"](k + 1))
                e.wait_ge(f["x_pf"].sem, f["x_pf"](k + 1))
                if k >= 3:
                    e.wait_ge(f["x_pv"].sem, f["x_pv"](k - 2))
                nc.gpsimd.tensor_tensor(pl[k % 3][0:n, :], pf[k % 2][0:n, :], ph[k % 3][0:n, :], ALU.subtract).then_inc(f["x_pl"].sem, 1)

    def act(e):
        s, ln = nc.scalar, g.link["act"]
        start_layer(g, e, layer)
        ln1["act"](e)
        for j in range(PAIRS):
            e.wait_ge(f["x_wT"].sem, f["x_wT"](j + 1))
            if j >= 2:
                e.wait_ge(f["x_GN"].sem, f["x_GN"](j - 1))
            s.activation(wT[j % 2], g.ps[:, j % 2, 0:P + 2 * DC], ACT.Copy).then_inc(f["x_wT_sb"].sem, 1)

        def q_high(b):
            e.wait_ge(f["x_qk"].sem, f["x_qk"](b + 1))
            if b >= 2:
                e.wait_ge(f["x_s"].sem, f["x_s"](NCH * (b - 1)))
            s.activation(qh[b % 2][0:DC, :], MX[0:DC, :], ACT.Copy).then_inc(f["x_qh"].sem, 1)

        def sums(b):
            e.wait_ge(f["x_pc"].sem, f["x_pc"](b + 1))
            if b >= 1:
                e.wait_ge(f["x_bc"].sem, f["x_bc"](b))
            ln(s.activation(rz, pc[96:97, :], ACT.Ln))
            s.activation(rz, rz, ACT.Exp, scale=-1.0).then_inc(f["x_rz"].sem, 1)

        q_high(0)
        for b in range(B):
            for c in range(NCH):
                k = NCH * b + c
                n = P if c < FULL else LASTK
                if c == 2 and b + 1 < B:
                    q_high(b + 1)
                if c == 4 and b >= 1:
                    sums(b - 1)
                e.wait_ge(f["x_s"].sem, f["x_s"](k + 1))
                if k >= 3:
                    e.wait_ge(f["x_pv"].sem, f["x_pv"](k - 2))
                if k >= 2:
                    e.wait_ge(f["x_pl"].sem, f["x_pl"](k - 1))
                s.activation(ph[k % 3][0:n, :], S_[k % 2][0:n, :], ACT.Exp).then_inc(f["x_ph"].sem, 1)
                s.activation(pf[k % 2][0:n, :], S_[k % 2][0:n, :], ACT.Exp).then_inc(f["x_pf"].sem, 1)
        sums(B - 1)

    def dve(e):
        v, ln = nc.vector, g.link["dve"]
        ln1["dve"](e)
        v.tensor_copy(xh, g.xnT).then_inc(f["x_xh"].sem, 1)
        e.wait_ge(f["x_xh"].sem, f["x_xh"](1))
        v.tensor_tensor(xl, g.xnT, xh, ALU.subtract).then_inc(f["x_xl"].sem, 1)
        for j in range(PAIRS):
            e.wait_ge(f["x_GN"].sem, f["x_GN"](j + 1))
            pair = g.ps[:, 2 + 2 * (j % 2):4 + 2 * (j % 2), :]
            Gp, Np = pair[:, :, 0:DC], pair[0:DC, :, P:2 * P]
            gh, gl = (a[:, 2 * DC * j:2 * DC * (j + 1)].rearrange("p (o n) -> p o n", o=2) for a in (Gh, Gl))
            nh, nl = (a[:, 2 * P * j:2 * P * (j + 1)].rearrange("p (o n) -> p o n", o=2) for a in (Nh, Nl))
            v.tensor_scalar(gh, Gp, SCALE, None, ALU.mult)
            ln(v.tensor_copy(nh, Np))
            v.scalar_tensor_tensor(out=gl, in0=Gp, scalar=SCALE, in1=gh, op0=ALU.mult, op1=ALU.subtract)
            v.tensor_tensor(nl, Np, nh, ALU.subtract).then_inc(f["x_GN_sb"].sem, 1)

        def q_low(b):
            e.wait_ge(f["x_qh"].sem, f["x_qh"](b + 1))
            v.tensor_tensor(ql[b % 2][0:DC, :], MX[0:DC, :], qh[b % 2][0:DC, :], ALU.subtract).then_inc(f["x_ql"].sem, 1)

        def units(b, first, count):
            for u in range(first, first + count):
                k = 4 * NR * b + u
                n = KSPAN[u % 4][1]
                e.wait_ge(f["x_unit"].sem, f["x_unit"](k + 1))
                v.tensor_reduce(pm[:, u // 4, u % 4:u % 4 + 1], MX[:, BANK * (u % 2):BANK * (u % 2) + n], AX.X, ALU.max).then_inc(f["x_red"].sem, 1)

        def row_max(b):
            e.wait_ge(f["x_red"].sem, f["x_red"](4 * NR * (b + 1)))
            v.tensor_reduce(m, pm, AX.X, ALU.max).then_inc(f["x_m"].sem, 1)
            e.wait_ge(f["x_mT"].sem, f["x_mT"](b + 1))
            if b >= 1:
                e.wait_ge(f["x_m_in"].sem, f["x_m_in"](16 * b))
            v.tensor_scalar(mrow, MX[0:NR, 0:P], -1.0, None, ALU.mult).then_inc(f["x_mrow"].sem, 1)

        def acc_out(b):
            e.wait_ge(f["x_pv"].sem, f["x_pv"](NCH * (b + 1)))
            v.tensor_copy(pc[0:DC + 1, :], ACC[0:DC + 1, :]).then_inc(f["x_pc"].sem, 1)

        def norm(b):
            e.wait_ge(f["x_bc"].sem, f["x_bc"](b + 1))
            ln(v.tensor_tensor(pcn[0:DC, :], pc[0:DC, :], MX[0:DC, :], ALU.mult))
            ln(v.tensor_copy(pcnh[0:DC, :], pcn[0:DC, :]))
            v.tensor_tensor(pcnl[0:DC, :], pcn[0:DC, :], pcnh[0:DC, :], ALU.subtract).then_inc(f["x_pcn"].sem, 1)

        def y_out(b):
            e.wait_ge(f["x_y"].sem, f["x_y"](b + 1))
            v.tensor_scalar(yT[:, S * b:S * b + S], MX[:, 0:S], g.col(names[4]), None, ALU.add).then_inc(f["x_y_sb"].sem, 1)

        q_low(0)
        units(0, 0, 4 * NR)
        row_max(0)
        for b in range(B):
            done = 0
            for c in range(NCH):
                if c == 1 and b >= 1:
                    acc_out(b - 1)
                if b + 1 < B:
                    if c == 2:
                        q_low(b + 1)
                    if c in UNITS:
                        units(b + 1, done, UNITS[c])
                        done += UNITS[c]
                    if c == 10:
                        row_max(b + 1)
                if c == 11 and b >= 1:
                    norm(b - 1)
                if c == 12 and b >= 1:
                    y_out(b - 1)
        acc_out(B - 1)
        norm(B - 1)
        y_out(B - 1)
        back["dve"](e)

    def pe(e):
        t = nc.tensor
        start_layer(g, e, layer)
        e.wait_ge(f["x_w_in"].sem, f["x_w_in"](64))

        def transposes(j):
            if j >= 2:
                e.wait_ge(f["x_wT_sb"].sem, f["x_wT_sb"](j - 1))
            t.transpose(g.ps[:, j % 2, 0:P], wq[:, P * j:P * j + P], g.ident)
            t.transpose(g.ps[:, j % 2, P:P + DC], wk[:, P * j:P * j + P], g.ident[0:DC, 0:DC])
            t.transpose(g.ps[:, j % 2, P + DC:P + 2 * DC], wv[:, P * j:P * j + P], g.ident[0:DC, 0:DC]).then_inc(f["x_wT"].sem, 1)

        transposes(0)
        for j in range(PAIRS):
            if j + 1 < PAIRS:
                transposes(j + 1)
            e.wait_ge(f["x_wT_sb"].sem, f["x_wT_sb"](j + 1))
            if j >= 2:
                e.wait_ge(f["x_GN_sb"].sem, f["x_GN_sb"](j - 1))
            for o in range(2):
                r = slice(DH * o, DH * o + DH)
                bank = g.ps[:, 2 + 2 * (j % 2) + o, :]
                t.matmul(bank[:, 0:DC], wT[j % 2][r, 0:P], wT[j % 2][r, P:P + DC], start=True, stop=True)
                i = t.matmul(bank[0:DC, P:2 * P], wT[j % 2][r, P + DC:P + 2 * DC], wo[r, j, :], start=True, stop=True)
            i.then_inc(f["x_GN"].sem, 1)
            if j == 1:
                ln1["pe"](e)
        e.wait_ge(f["x_xl"].sem, f["x_xl"](1))
        e.wait_ge(f["x_GN_sb"].sem, f["x_GN_sb"](PAIRS))
        e.wait_ge(f["x_zero"].sem, f["x_zero"](1))

        def qk(b):
            if b >= 3:
                e.wait_ge(f["x_y_sb"].sem, f["x_y_sb"](b - 2))
            for h in range(H):
                for j, (G_, x_) in enumerate(((Gh, xh), (Gh, xl), (Gl, xh))):
                    i = t.matmul(MX[0:DC, S * h:S * h + S], G_[:, DC * h:DC * h + DC], x_[:, S * b:S * b + S], start=j == 0, stop=j == 2)
            i.then_inc(f["x_qk"].sem, 1)

        def units(b, first, count):
            for u in range(first, first + count):
                k = 4 * NR * b + u
                a, n = KSPAN[u % 4]
                if u < 2:
                    e.wait_ge(f["x_ql"].sem, f["x_ql"](b + 1))
                else:
                    e.wait_ge(f["x_red"].sem, f["x_red"](k - 1))
                t.matmul(MX[:, BANK * (u % 2):BANK * (u % 2) + n], qh[b % 2][0:DC, P * (u // 4):P * (u // 4) + P],
                         g.cT_hi[0:DC, b, a:a + n], start=True, stop=True).then_inc(f["x_unit"].sem, 1)

        def max_T(b):
            e.wait_ge(f["x_m"].sem, f["x_m"](b + 1))
            t.transpose(MX[0:NR, 0:P], m, g.ident).then_inc(f["x_mT"].sem, 1)

        def bcast(b):
            e.wait_ge(f["x_rz"].sem, f["x_rz"](b + 1))
            e.wait_ge(f["x_mrow"].sem, f["x_mrow"](min(b + 3, B)))
            for q in range(HB):
                i = t.matmul(MX[0:DC, BANK * q:BANK * q + BANK], g.ones[96:97, 0:DC], rz[:, BANK * q:BANK * q + BANK], start=True, stop=True)
            i.then_inc(f["x_bc"].sem, 1)

        def y(b):
            e.wait_ge(f["x_pcn"].sem, f["x_pcn"](b + 1))
            for h in range(H):
                for j, (N_, c_) in enumerate(((Nh, pcnh), (Nh, pcnl), (Nl, pcnh))):
                    i = t.matmul(MX[:, 0:S], N_[:, P * h:P * h + P], c_[0:DC, S * h:S * h + S], start=h == 0 and j == 0,
                                 stop=h == H - 1 and j == 2)
            i.then_inc(f["x_y"].sem, 1)

        def weighted(k, between):
            b, c = divmod(k, NCH)
            n = P if c < FULL else LASTK
            e.wait_ge(f["x_ph"].sem, f["x_ph"](k + 1))
            if c == 0 and b >= 1:
                e.wait_ge(f["x_pc"].sem, f["x_pc"](b))
            hi, lo = g.cr_hi[0:n, b, c, :], g.cr_lo[0:n, b, c, :]
            for j, (lhs, p) in enumerate(((hi, ph), (lo, ph), (hi, pl))):
                if j == 2:
                    e.wait_ge(f["x_pl"].sem, f["x_pl"](k + 1))
                for q in range(HB):
                    i = t.matmul(ACC[0:DC + 1, BANK * q:BANK * q + BANK], lhs, p[k % 3][0:n, BANK * q:BANK * q + BANK],
                                 start=c == 0 and j == 0, stop=c == NCH - 1 and j == 2)
                if j < 2:
                    between()
            i.then_inc(f["x_pv"].sem, 1)
            between()

        def nothing_between():
            pass

        qk(0)
        units(0, 0, 4 * NR)
        max_T(0)
        for b in range(B):
            e.wait_ge(f["x_m_in"].sem, f["x_m_in"](16 * (b + 1)))
            for c in range(NCH):
                k = NCH * b + c
                n = P if c < FULL else LASTK
                if k >= 2:
                    e.wait_ge(f["x_pf"].sem, f["x_pf"](k - 1))
                first = sum(UNITS.get(i, 0) for i in range(c))
                left = [(b + 1, first + i) for i in range(UNITS.get(c, 0) if b + 1 < B else 0)]

                def between():
                    if left:
                        units(*left.pop(0), 1)

                hi, lo = g.cT_hi[0:DC + 1, b, P * c:P * c + n], g.cT_lo[0:DC + 1, b, P * c:P * c + n]
                for j, (lhs, q_) in enumerate(((hi, qh), (lo, qh), (hi, ql))):
                    for q in range(HB):
                        i = t.matmul(S_[k % 2][0:n, BANK * q:BANK * q + BANK], lhs, q_[b % 2][0:DC + 1, BANK * q:BANK * q + BANK],
                                     start=j == 0, stop=j == 2)
                    if j < 2:
                        between()
                i.then_inc(f["x_s"].sem, 1)
                between()
                if b + 1 < B:
                    if c == 1:
                        qk(b + 1)
                    if c == 10:
                        max_T(b + 1)
                if b >= 1 and c == 11:
                    bcast(b - 1)
                if b >= 1 and c == 12:
                    y(b - 1)
                if k >= 2:
                    weighted(k - 2, between)
                assert not left
        weighted(NCH * B - 2, nothing_between)
        weighted(NCH * B - 1, nothing_between)
        bcast(B - 1)
        y(B - 1)
        back["pe"](e)

    return dict(load=load, sp=sp, dve=dve, act=act, pe=pe, pool=pool)


def layer_l1_cross(g):
    return cross_attention(g, 3, 1, ("L1_xattn_Wq", "L1_xattn_Wk", "L1_xattn_Wv", "L1_xattn_Wo", "l1x_bo"))


HG = 4
NG = 16 // HG


def self_attention(g, tmp, scores_of, value_of, out_of, soft, ready_pe=None, prep_pe=None, prep_act=None, prep_dve=None, itau=None, nthr=None):
    nc = g.nc
    GC = HG * P
    KG = NT * NG
    sm = [tmp.take(GC).rearrange("p (h k) -> p h k", h=HG) for _ in range(2)]
    pr = [tmp.take(GC).rearrange("p (h k) -> p h k", h=HG) for _ in range(3)]
    pT = [tmp.take(GC).rearrange("p (h k) -> p h k", h=HG) for _ in range(2)]
    mx = [tmp.take(HG) for _ in range(2)]
    nm = [tmp.take(HG) for _ in range(2)]
    z = [tmp.take(HG) for _ in range(2)]
    zi = [tmp.take(HG) for _ in range(2)]
    f = flags(g, s_scores=KG, s_masked=KG, s_prob=KG, s_zinv=KG, s_norm=KG, s_T=KG, s_T_sb=KG, s_out=KG)

    def bank(i):
        return g.ps[:, i, :].rearrange("p (h k) -> p h k", h=HG)

    def wide(m):
        return m[:, None, :].to_broadcast([P, HG, P])

    def pe(e):
        t = nc.tensor
        if prep_pe:
            prep_pe(e, 0)
        for k in range(KG + 3):
            if 0 <= k - 2 < KG:
                q = k - 2
                e.wait_ge(f["s_norm"].sem, f["s_norm"](q + 1))
                if q >= 2:
                    e.wait_ge(f["s_T_sb"].sem, f["s_T_sb"](q - 1))
                for h in range(HG):
                    i = t.transpose(bank(2 + q % 2)[:, h, :], pr[q % 3][:, h, :], g.ident)
                i.then_inc(f["s_T"].sem, 1)
            if k < KG:
                if ready_pe:
                    ready_pe(e, k)
                if k >= 2:
                    e.wait_ge(f["s_masked"].sem, f["s_masked"](k - 1))
                for h in range(HG):
                    lhs, rhs = scores_of(k, h)
                    i = t.matmul(bank(k % 2)[:, h, :], lhs, rhs, start=True, stop=True)
                i.then_inc(f["s_scores"].sem, 1)
                if prep_pe and k + 1 < KG:
                    prep_pe(e, k + 1)
            if 0 <= k - 3 < KG:
                q = k - 3
                e.wait_ge(f["s_T_sb"].sem, f["s_T_sb"](q + 1))
                for h in range(HG):
                    dst, start, stop = out_of(q, h)
                    i = t.matmul(dst, pT[q % 2][:, h, :], value_of(q, h), start=start, stop=stop)
                i.then_inc(f["s_out"].sem, 1)

    def dve(e):
        v, ln = nc.vector, g.link["dve"]

        def sums(q):
            e.wait_ge(f["s_prob"].sem, f["s_prob"](q + 1))
            if soft is None:
                if q >= 3:
                    e.wait_ge(f["s_T"].sem, f["s_T"](q - 2))
                ln(v.scalar_tensor_tensor(out=pr[q % 3], in0=pr[q % 3], scalar=1.0, in1=wide(g.neg_blk), op0=ALU.subtract, op1=ALU.mult))
                ln(v.tensor_reduce(z[q % 2], pr[q % 3], AX.X, ALU.add))
                ln(v.tensor_scalar(z[q % 2], z[q % 2], 1e-6, None, ALU.add))
            if q >= 2:
                e.wait_ge(f["s_norm"].sem, f["s_norm"](q - 1))
            v.reciprocal(zi[q % 2], z[q % 2]).then_inc(f["s_zinv"].sem, 1)

        if prep_dve:
            prep_dve(e, 0)
        for k in range(KG):
            if k >= 1:
                sums(k - 1)
            e.wait_ge(f["s_scores"].sem, f["s_scores"](k + 1))
            if k >= 2:
                e.wait_ge(f["s_prob"].sem, f["s_prob"](k - 1))
            if soft is not None:
                ln(v.tensor_tensor(sm[k % 2], bank(k % 2), wide(soft), ALU.add))
                ln(v.tensor_reduce(mx[k % 2], sm[k % 2], AX.X, ALU.max))
                v.tensor_scalar(nm[k % 2], mx[k % 2], -1.0, None, ALU.mult).then_inc(f["s_masked"].sem, 1)
            else:
                ln(v.tensor_tensor(sm[k % 2], bank(k % 2), wide(g.tri_mul), ALU.mult))
                v.tensor_tensor(sm[k % 2], sm[k % 2], wide(g.tri_add), ALU.add).then_inc(f["s_masked"].sem, 1)
            if prep_dve and k + 1 < KG:
                prep_dve(e, k + 1)
        sums(KG - 1)

    def act(e):
        s, ln = nc.scalar, g.link["act"]
        if prep_act:
            prep_act(e, 0)
        for k in range(KG + 2):
            if 0 <= k - 2 < KG:
                q = k - 2
                e.wait_ge(f["s_T"].sem, f["s_T"](q + 1))
                if q >= 2:
                    e.wait_ge(f["s_out"].sem, f["s_out"](q - 1))
                s.activation(pT[q % 2], bank(2 + q % 2), ACT.Copy).then_inc(f["s_T_sb"].sem, 1)
            if k < KG:
                if prep_act and k + 1 < KG:
                    prep_act(e, k + 1)
                e.wait_ge(f["s_masked"].sem, f["s_masked"](k + 1))
                if k >= 3:
                    e.wait_ge(f["s_T"].sem, f["s_T"](k - 2))
                if k >= 2:
                    e.wait_ge(f["s_zinv"].sem, f["s_zinv"](k - 1))
                for h in range(HG):
                    if soft is not None:
                        i = s.activation(pr[k % 3][:, h, :], sm[k % 2][:, h, :], ACT.Exp, bias=nm[k % 2][:, h:h + 1],
                                         accum_out=z[k % 2][:, h:h + 1])
                    else:
                        hh = HG * (k % NG) + h
                        i = s.activation(pr[k % 3][:, h, :], sm[k % 2][:, h, :], ACT.Tanh, bias=nthr[:, hh:hh + 1],
                                         scale=itau[:, hh:hh + 1])
                if soft is None:
                    ln(i)
                    i = s.activation(pr[k % 3], pr[k % 3], ACT.Square)
                i.then_inc(f["s_prob"].sem, 1)

    def pool(e):
        for k in range(KG):
            e.wait_ge(f["s_zinv"].sem, f["s_zinv"](k + 1))
            nc.gpsimd.tensor_tensor(pr[k % 3], pr[k % 3], zi[k % 2][:, :, None].to_broadcast([P, HG, P]), ALU.mult).then_inc(f["s_norm"].sem, 1)
    return dict(pe=pe, dve=dve, act=act, pool=pool, out=f["s_out"], f=f, KG=KG)


def layer_l1_self(g):
    nc = g.nc
    tmp = g.temps()
    H, DH = 16, 64
    PAIRS = H // 2
    w = g.slot[0]
    wq, wk, wv = (w[:, PAIRS * D * i:PAIRS * D * (i + 1)].rearrange("p (j d) -> p j d", d=D) for i in range(3))
    wo = w[:, 3 * PAIRS * D:4 * PAIRS * D]
    M_ = g.pre[:, 0:H * D]
    N_ = g.pre[:, H * D:2 * H * D]
    woT = [tmp.take(P) for _ in range(2)]
    tT = [tmp.take(HG * P) for _ in range(2)]
    vN = [tmp.take(HG * P) for _ in range(6)]
    ln1 = layernorm(g, g.x, g.xn, out_T=g.xnT)
    KG = NT * NG
    f = flags(g, l1_w_in=64, x_wT=PAIRS, x_wT_sb=PAIRS, x_GN=PAIRS, x_GN_sb=PAIRS, p_t=KG, p_t_sb=KG, p_v=KG, p_v_sb=KG)

    def tile(k):
        return slice(P * (k // NG), P * (k // NG) + P)

    def prep_pe(e, k):
        t = nc.tensor
        hs = HG * (k % NG)
        if k >= 1:
            e.wait_ge(f["p_t_sb"].sem, f["p_t_sb"](k))
            e.wait_ge(f["p_v_sb"].sem, f["p_v_sb"](k))
        for h in range(HG):
            i = t.matmul(g.ps[:, 5, P * h:P * h + P], M_[:, D * (hs + h):D * (hs + h) + D], g.xnT[:, tile(k)], start=True, stop=True)
        i.then_inc(f["p_t"].sem, 1)
        t.matmul(g.ps[:, 6, :], g.xnT[:, tile(k)], N_[:, D * hs:D * (hs + HG)], start=True, stop=True).then_inc(f["p_v"].sem, 1)

    def ready_pe(e, k):
        e.wait_ge(f["p_t_sb"].sem, f["p_t_sb"](k + 1))

    def prep_act(e, k):
        e.wait_ge(f["p_t"].sem, f["p_t"](k + 1))
        if k >= 2:
            e.wait_ge(core["f"]["s_scores"].sem, core["f"]["s_scores"](k - 1))
        nc.scalar.activation(tT[k % 2], g.ps[:, 5, :], ACT.Copy).then_inc(f["p_t_sb"].sem, 1)

    def prep_dve(e, k):
        e.wait_ge(f["p_v"].sem, f["p_v"](k + 1))
        if k >= 6:
            e.wait_ge(core["f"]["s_out"].sem, core["f"]["s_out"](k - 5))
        nc.vector.tensor_copy(vN[k % 6], g.ps[:, 6, :]).then_inc(f["p_v_sb"].sem, 1)

    core = self_attention(
        g, tmp, lambda k, h: (tT[k % 2][:, P * h:P * h + P], g.xnT[:, tile(k)]),
        lambda k, h: vN[k % 6][:, P * h:P * h + P],
        lambda k, h: (g.ps[:, 4, tile(k)], k % NG == 0 and h == 0, k % NG == NG - 1 and h == HG - 1),
        soft=g.mask_ca, ready_pe=ready_pe, prep_pe=prep_pe, prep_act=prep_act, prep_dve=prep_dve)
    last = Flag(core["out"].sem)
    last.base = core["out"](KG - 1)
    add = add_rows(g, 4, last)

    def load(e):
        wait_slot(g, e, 4)
        for dst, name in ((wq, "L1_attn_w_q"), (wk, "L1_attn_w_k"), (wv, "L1_attn_w_v")):
            e.dma_start(dst, g.a[name].rearrange("h q d -> (h q) d").rearrange("(j p) d -> p j d", p=P)).then_inc(f["l1_w_in"].sem, 16)
        e.dma_start(wo, g.a["L1_attn_w_o"]).then_inc(f["l1_w_in"].sem, 16)

    def pe(e):
        t = nc.tensor
        start_layer(g, e, 4)
        e.wait_ge(f["l1_w_in"].sem, f["l1_w_in"](64))

        def transpose(j):
            if j >= 2:
                e.wait_ge(f["x_wT_sb"].sem, f["x_wT_sb"](j - 1))
            t.transpose(g.ps[:, j % 2, 0:P], wo[:, P * j:P * j + P], g.ident).then_inc(f["x_wT"].sem, 1)

        transpose(0)
        for j in range(PAIRS):
            if j + 1 < PAIRS:
                transpose(j + 1)
            e.wait_ge(f["x_wT_sb"].sem, f["x_wT_sb"](j + 1))
            if j >= 2:
                e.wait_ge(f["x_GN_sb"].sem, f["x_GN_sb"](j - 1))
            for o in range(2):
                r = slice(DH * o, DH * o + DH)
                bank = g.ps[:, 2 + 2 * (j % 2) + o, :]
                t.matmul(bank[:, 0:P], wq[r, j, :], wk[r, j, :], start=True, stop=True)
                i = t.matmul(bank[:, P:2 * P], wv[r, j, :], woT[j % 2][r, :], start=True, stop=True)
            i.then_inc(f["x_GN"].sem, 1)
            if j == 1:
                ln1["pe"](e)
        e.wait_ge(ln1["ready"].sem, ln1["ready"](1))
        e.wait_ge(f["x_GN_sb"].sem, f["x_GN_sb"](PAIRS))
        core["pe"](e)

    def act(e):
        start_layer(g, e, 4)
        ln1["act"](e)
        for j in range(PAIRS):
            e.wait_ge(f["x_wT"].sem, f["x_wT"](j + 1))
            if j >= 2:
                e.wait_ge(f["x_GN"].sem, f["x_GN"](j - 1))
            nc.scalar.activation(woT[j % 2], g.ps[:, j % 2, 0:P], ACT.Copy).then_inc(f["x_wT_sb"].sem, 1)
        core["act"](e)

    def dve(e):
        ln1["dve"](e)
        for j in range(PAIRS):
            e.wait_ge(f["x_GN"].sem, f["x_GN"](j + 1))
            for o in range(2):
                h = 2 * j + o
                bank = g.ps[:, 2 + 2 * (j % 2) + o, :]
                nc.vector.tensor_scalar(M_[:, D * h:D * h + D], bank[:, 0:P], DH ** -0.5, None, ALU.mult)
                i = nc.vector.tensor_copy(N_[:, D * h:D * h + D], bank[:, P:2 * P])
            i.then_inc(f["x_GN_sb"].sem, 1)
        core["dve"](e)
        add["dve"](e)

    def pool(e):
        start_layer(g, e, 4)
        core["pool"](e)
    return dict(load=load, sp=nothing, dve=dve, act=act, pe=pe, pool=pool)


def layer_l1_moe(g):
    nc = g.nc
    tmp = g.temps()
    E, FC = 8, 4
    K = E * FC
    EW = 3 * 512
    place = [g.slot[1], g.slot[0], g.pre, g.slot[1]]
    sg = [tmp.take(TOK) for _ in range(2)]
    hb = [tmp.take(TOK) for _ in range(3)]
    yT = g.pre[:, 2 * EW:2 * EW + TOK]
    ln1 = layernorm(g, g.x, g.xn, out_T=g.xnT)
    f = flags(g, m_w_in0=96, m_w_in1=96, m_w_in2=96, m_w_in3=96, m_gate=K, m_up=K, m_act=K, m_h=K, m_y=K)
    s4 = s4d_kernel(g, tmp)
    f = steps(g, f, dve_step="m_yT")
    arrived = [f["m_w_in0"], f["m_w_in1"], f["m_w_in2"], f["m_w_in3"]]
    back = add_back(g, yT, f["m_yT"])

    def views(x):
        w = place[x // 2][:, EW * (x % 2):EW * (x % 2) + EW]
        return w[:, 0:512], w[:, 512:1024], w[:, 1024:1536].rearrange("p (c d) -> p c d", d=D)

    def load_pair(e, p):
        for x in (2 * p, 2 * p + 1):
            wg, wu, wd = views(x)
            e.dma_start(wg, g.a["L1_ffn_Wg"][x]).then_inc(arrived[p].sem, 16)
            e.dma_start(wu, g.a["L1_ffn_Wu"][x]).then_inc(arrived[p].sem, 16)
            e.dma_start(wd, g.a["L1_ffn_Wd"][x].rearrange("(c p) d -> p c d", p=P)).then_inc(arrived[p].sem, 16)

    def load(e):
        wait_slot(g, e, 5)
        load_pair(e, 0)

    def sp(e):
        start_layer(g, e, 5)
        load_pair(e, 1)
        load_pair(e, 2)
        e.wait_ge(f["m_y"].sem, f["m_y"](2 * FC))
        load_pair(e, 3)
        e.wait_ge(f["m_y"].sem, f["m_y"](4 * FC))

    def pe(e):
        t = nc.tensor
        ln1["pe"](e)
        e.wait_ge(ln1["ready"].sem, ln1["ready"](1))
        for k in range(K + 2):
            if k < K:
                x, c = divmod(k, FC)
                wg, wu, _ = views(x)
                if x % 2 == 0 and c == 0:
                    e.wait_ge(arrived[x // 2].sem, arrived[x // 2](96))
                if k >= 2:
                    e.wait_ge(f["m_act"].sem, f["m_act"](k - 1))
                t.matmul(g.ps[:, k % 2, :], wg[:, P * c:P * c + P], g.xnT, start=True, stop=True).then_inc(f["m_gate"].sem, 1)
                if k >= 2:
                    e.wait_ge(f["m_h"].sem, f["m_h"](k - 1))
                t.matmul(g.ps[:, 2 + k % 2, :], wu[:, P * c:P * c + P], g.xnT, start=True, stop=True).then_inc(f["m_up"].sem, 1)
            if k >= 2:
                q = k - 2
                x, c = divmod(q, FC)
                e.wait_ge(f["m_h"].sem, f["m_h"](q + 1))
                t.matmul(g.ps[:, 4, :], views(x)[2][:, c, :], hb[q % 3], start=q == 0, stop=q == K - 1).then_inc(f["m_y"].sem, 1)
        back["pe"](e)

    def act(e):
        start_layer(g, e, 5)
        s4["act"](e)
        table(g)
        ln1["act"](e)
        for k in range(K):
            e.wait_ge(f["m_gate"].sem, f["m_gate"](k + 1))
            if k >= 2:
                e.wait_ge(f["m_h"].sem, f["m_h"](k - 1))
            nc.scalar.activation(sg[k % 2], g.ps[:, k % 2, :], ACT.Silu).then_inc(f["m_act"].sem, 1)

    def dve(e):
        s4["dve"](e)
        ln1["dve"](e)
        for k in range(K):
            e.wait_ge(f["m_act"].sem, f["m_act"](k + 1))
            e.wait_ge(f["m_up"].sem, f["m_up"](k + 1))
            if k >= 3:
                e.wait_ge(f["m_y"].sem, f["m_y"](k - 2))
            nc.vector.tensor_tensor(hb[k % 3], g.ps[:, 2 + k % 2, :], sg[k % 2], ALU.mult).then_inc(f["m_h"].sem, 1)
        s4["dve_end"](e)
        e.wait_ge(f["m_y"].sem, f["m_y"](K))
        nc.vector.tensor_copy(yT, g.ps[:, 4, :]).then_inc(f["m_yT"].sem, 1)
        back["dve"](e)

    def pool(e):
        start_layer(g, e, 5)
        s4["pool"](e)
    return dict(own_loads_first=True, load=load, sp=sp, dve=dve, act=act, pe=pe, pool=pool)


def s4d_kernel(g, tmp):
    nc = g.nc
    N = 64
    HL = S // 2
    ar, ai, cr, ci = (g.s4in[:, N * i:N * i + N] for i in range(4))
    Vr = tmp.take(HL * N).rearrange("p (l n) -> p l n", n=N)
    Vi = tmp.take(HL * N).rearrange("p (l n) -> p l n", n=N)
    T1 = tmp.take(HL * N).rearrange("p (l n) -> p l n", n=N)
    T2 = tmp.take(HL * N).rearrange("p (l n) -> p l n", n=N)
    small = T2.rearrange("p l n -> p (l n)")
    names = "re er th r1 r2 sn cs wr wi nr ni pr pi den t1 t2 w2r w2i".split()
    q = {n: small[:, N * i:N * i + N] for i, n in enumerate(names)}
    W = [T1.rearrange("p l n -> p (l n)")[:, 1024 + N * i:1024 + N * i + N] for i in range(2)]
    keep = g.pre[:, 4096 - 2 * N:4096]
    wr, wi = keep[:, 0:N], keep[:, N:2 * N]
    f = flags(g, s4_pool=1)
    f = steps(g, f, dve_step="s4_arg s4_start", act_step="s4_dt s4_trig")

    def act(e):
        s, ln = nc.scalar, g.link["act"]
        s.activation(g.s4dt, g.col("l3x_dt"), ACT.Exp).then_inc(f["s4_dt"].sem, 1)
        e.wait_ge(f["s4_arg"].sem, f["s4_arg"](1))
        s.activation(q["er"], q["re"], ACT.Exp)
        s.activation(q["sn"], q["r1"], ACT.Sin)
        s.activation(q["cs"], q["r2"], ACT.Sin).then_inc(f["s4_trig"].sem, 1)

    def reduce_angle(v, ln, out, src, shift):
        ln(v.tensor_scalar(q["t1"], src, 1.0 / (2.0 * PI), shift / (2.0 * PI), ALU.mult, ALU.add))
        ln(v.tensor_scalar(q["t1"], q["t1"], HALF_ULP, HALF_ULP, ALU.add, ALU.subtract))
        ln(v.scalar_tensor_tensor(out=q["t2"], in0=q["t1"], scalar=-6.28125, in1=src, op0=ALU.mult, op1=ALU.add))
        ln(v.scalar_tensor_tensor(out=q["t2"], in0=q["t1"], scalar=-(2.0 * PI - 6.28125), in1=q["t2"], op0=ALU.mult, op1=ALU.add))
        ln(v.tensor_scalar(out, q["t2"], shift, -3.1415925, ALU.add, ALU.max))
        return v.tensor_scalar(out, out, 3.1415925, None, ALU.min)

    def dve(e):
        v, ln = nc.vector, g.link["dve"]
        e.wait_ge(g.s4_sem, 64)
        e.wait_ge(f["s4_dt"].sem, f["s4_dt"](1))
        v.tensor_scalar(q["re"], ar, g.s4dt, None, ALU.mult)
        ln(v.tensor_scalar(q["th"], ai, g.s4dt, None, ALU.mult))
        ln(reduce_angle(v, ln, q["r1"], q["th"], 0.0))
        reduce_angle(v, ln, q["r2"], q["th"], PI / 2.0).then_inc(f["s4_arg"].sem, 1)
        e.wait_ge(f["s4_trig"].sem, f["s4_trig"](1))
        v.tensor_tensor(wr, q["er"], q["cs"], ALU.mult)
        ln(v.tensor_tensor(wi, q["er"], q["sn"], ALU.mult))
        ln(v.tensor_scalar(q["nr"], wr, -1.0, None, ALU.add))
        v.tensor_tensor(q["pr"], cr, q["nr"], ALU.mult)
        v.tensor_tensor(q["t1"], ci, wi, ALU.mult)
        v.tensor_tensor(q["pi"], cr, wi, ALU.mult)
        ln(v.tensor_tensor(q["t2"], ci, q["nr"], ALU.mult))
        v.tensor_tensor(q["pr"], q["pr"], q["t1"], ALU.subtract)
        ln(v.tensor_tensor(q["pi"], q["pi"], q["t2"], ALU.add))
        v.tensor_tensor(q["t1"], ar, ar, ALU.mult)
        ln(v.tensor_tensor(q["t2"], ai, ai, ALU.mult))
        ln(v.tensor_tensor(q["den"], q["t1"], q["t2"], ALU.add))
        ln(v.reciprocal(q["den"], q["den"]))
        v.tensor_tensor(q["t1"], q["pr"], ar, ALU.mult)
        ln(v.tensor_tensor(q["t2"], q["pi"], ai, ALU.mult))
        ln(v.tensor_tensor(q["t1"], q["t1"], q["t2"], ALU.add))
        ln(v.tensor_tensor(Vr[:, 0, :], q["t1"], q["den"], ALU.mult))
        v.tensor_tensor(q["t1"], q["pi"], ar, ALU.mult)
        ln(v.tensor_tensor(q["t2"], q["pr"], ai, ALU.mult))
        ln(v.tensor_tensor(q["t1"], q["t1"], q["t2"], ALU.subtract))
        v.tensor_tensor(Vi[:, 0, :], q["t1"], q["den"], ALU.mult).then_inc(f["s4_start"].sem, 1)
        e.wait_ge(f["s4_start"].sem, f["s4_start"](1))

    def pool(e):
        p, ln = nc.gpsimd, g.link["pool"]
        e.wait_ge(f["s4_start"].sem, f["s4_start"](1))
        m = 1
        while m <= HL:
            br = wr[:, None, :].to_broadcast([P, m, N])
            bi = wi[:, None, :].to_broadcast([P, m, N])
            src_r, src_i = Vr[:, 0:m, :], Vi[:, 0:m, :]
            if m == HL:
                ln(p.tensor_tensor(T1, src_r, br, ALU.mult))
                ln(p.tensor_tensor(T2, src_i, bi, ALU.mult))
                p.tensor_tensor(T1, T1, T2, ALU.subtract).then_inc(f["s4_pool"].sem, 1)
                break
            dr, di, t = Vr[:, m:2 * m, :], Vi[:, m:2 * m, :], T2[:, 0:m, :]
            ln(p.tensor_tensor(dr, src_r, br, ALU.mult))
            ln(p.tensor_tensor(t, src_i, bi, ALU.mult))
            ln(p.tensor_tensor(dr, dr, t, ALU.subtract))
            ln(p.tensor_tensor(di, src_r, bi, ALU.mult))
            ln(p.tensor_tensor(t, src_i, br, ALU.mult))
            ln(p.tensor_tensor(di, di, t, ALU.add))
            ln(p.tensor_tensor(W[0], wr, wr, ALU.mult))
            ln(p.tensor_tensor(W[1], wi, wi, ALU.mult))
            ln(p.tensor_tensor(W[0], W[0], W[1], ALU.subtract))
            ln(p.tensor_tensor(W[1], wr, wi, ALU.mult))
            ln(p.tensor_tensor(wi, W[1], W[1], ALU.add))
            ln(p.tensor_copy(wr, W[0]))
            m *= 2

    def dve_end(e):
        v, ln = nc.vector, g.link["dve"]
        e.wait_ge(f["s4_pool"].sem, f["s4_pool"](1))
        v.tensor_reduce(g.s4k[:, 0:HL], Vr, AX.X, ALU.add)
        ln(v.tensor_reduce(g.s4k[:, HL:S], T1, AX.X, ALU.add))
        ln(v.tensor_scalar(g.s4k, g.s4k, 2.0, None, ALU.mult))
        ln(v.tensor_tensor(g.s4k[:, 0:1], g.s4k[:, 0:1], g.col("l3x_skip"), ALU.add))
    return dict(act=act, dve=dve, pool=pool, dve_end=dve_end)


def layer_l2_cross(g):
    return cross_attention(g, 6, 0, ("L2_xattn_w_q", "L2_xattn_w_k", "L2_xattn_w_v", "L2_xattn_w_out", "l2x_bo"))


def narrow_self(g, layer, slot, load_weights, w_count, soft, bias):
    nc = g.nc
    tmp = g.temps()
    HD = 8
    w = g.slot[slot]
    wT = tmp.take(4 * P)
    qT, kT = tmp.take(TOK), tmp.take(TOK)
    V = tmp.take(NT * P).rearrange("p (t d) -> p t d", d=D)
    qm = [tmp.take(HG * P).rearrange("p (h q) -> p h q", h=HG) for _ in range(2)]
    orow = tmp.take(NT * P)
    oT, yT = tmp.take(TOK), tmp.take(TOK)
    itau, nthr, sp1, sp2 = (tmp.take(16) for _ in range(4))
    ln1 = layernorm(g, g.x, g.xn, out_T=g.xnT)
    KG = NT * NG
    f = flags(g, **{"n_w_in%d" % slot: 16 * w_count}, p_v_sb=KG)
    w_in = f["n_w_in%d" % slot]
    f = steps(g, f, rows_T="n_wT n_oT", T_ready="n_wT_sb n_oT_sb", products="n_q n_k n_v n_y",
          dve_step=("" if soft is not None else "n_tau0 ") + "n_q_sb n_k_sb n_v_sb n_rows n_yT", act_step="" if soft is not None else "n_tau1")
    back = add_back(g, yT, f["n_yT"])

    def tile(k):
        return slice(P * (k // NG), P * (k // NG) + P)

    def prep_dve(e, k):
        hs = HG * (k % NG)
        if k >= 2:
            e.wait_ge(core["f"]["s_scores"].sem, core["f"]["s_scores"](k - 1))
        nc.vector.tensor_tensor(qm[k % 2], qT[:, None, tile(k)].to_broadcast([P, HG, P]),
                                g.head_of[:, hs:hs + HG, None].to_broadcast([P, HG, P]), ALU.mult).then_inc(f["p_v_sb"].sem, 1)

    def ready_pe(e, k):
        e.wait_ge(f["p_v_sb"].sem, f["p_v_sb"](k + 1))

    core = self_attention(
        g, tmp, lambda k, h: (qm[k % 2][:, h, :], kT[:, tile(k)]),
        lambda k, h: V[:, k // NG, HD * (HG * (k % NG) + h):HD * (HG * (k % NG) + h) + HD],
        lambda k, h: (g.ps[:, 4, P * (k // NG) + HD * (HG * (k % NG) + h):P * (k // NG) + HD * (HG * (k % NG) + h) + HD], True, True),
        soft=soft, ready_pe=ready_pe, prep_dve=prep_dve, itau=itau, nthr=nthr)

    def load(e):
        wait_slot(g, e, layer)
        load_weights(e, w, w_in)

    def pe(e):
        t = nc.tensor
        start_layer(g, e, layer)
        e.wait_ge(w_in.sem, w_in(16 * w_count))
        for i in range(4):
            m = t.transpose(g.ps[:, 0, P * i:P * i + P], w[:, P * i:P * i + P], g.ident)
        m.then_inc(f["n_wT"].sem, 1)
        ln1["pe"](e)
        e.wait_ge(ln1["ready"].sem, ln1["ready"](1))
        e.wait_ge(f["n_wT_sb"].sem, f["n_wT_sb"](1))
        t.matmul(g.ps[:, 1, :], wT[:, 0:P], g.xnT, start=True, stop=True).then_inc(f["n_q"].sem, 1)
        t.matmul(g.ps[:, 2, :], wT[:, P:2 * P], g.xnT, start=True, stop=True).then_inc(f["n_k"].sem, 1)
        for j in range(NT):
            m = t.matmul(g.ps[:, 3, P * j:P * j + P], g.xnT[:, P * j:P * j + P], wT[:, 2 * P:3 * P], start=True, stop=True)
        m.then_inc(f["n_v"].sem, 1)
        e.wait_ge(f["n_v_sb"].sem, f["n_v_sb"](1))
        core["pe"](e)
        e.wait_ge(f["n_rows"].sem, f["n_rows"](1))
        for j in range(NT):
            m = t.transpose(g.ps[:, 5, P * j:P * j + P], orow[:, P * j:P * j + P], g.ident)
        m.then_inc(f["n_oT"].sem, 1)
        e.wait_ge(f["n_oT_sb"].sem, f["n_oT_sb"](1))
        t.matmul(g.ps[:, 6, :], wT[:, 3 * P:4 * P], oT, start=True, stop=True).then_inc(f["n_y"].sem, 1)
        back["pe"](e)

    def act(e):
        s, ln = nc.scalar, g.link["act"]
        start_layer(g, e, layer)
        if soft is None:
            e.wait_ge(f["n_tau0"].sem, f["n_tau0"](1))
            ln(s.activation(sp2, sp1, ACT.Exp, scale=-1.0))
            s.activation(sp2, sp2, ACT.Ln, bias=1.0).then_inc(f["n_tau1"].sem, 1)
        ln1["act"](e)
        core["act"](e)

    def dve(e):
        v, ln = nc.vector, g.link["dve"]
        if soft is None:
            comp, thr = g.scal[:, 32:48], g.scal[:, 48:64]
            ln(v.tensor_scalar(sp2, comp, -1.0, None, ALU.mult))
            v.tensor_tensor(sp1, comp, sp2, ALU.max).then_inc(f["n_tau0"].sem, 1)
            e.wait_ge(f["n_tau1"].sem, f["n_tau1"](1))
            ln(v.tensor_scalar(itau, comp, 0.0, 1e-6, ALU.max, ALU.add))
            ln(v.tensor_tensor(itau, itau, sp2, ALU.add))
            ln(v.reciprocal(itau, itau))
            ln(v.scalar_tensor_tensor(out=nthr, in0=thr, scalar=-1.0, in1=itau, op0=ALU.mult, op1=ALU.mult))
        e.wait_ge(f["n_wT"].sem, f["n_wT"](1))
        v.tensor_copy(wT, g.ps[:, 0, :]).then_inc(f["n_wT_sb"].sem, 1)
        ln1["dve"](e)
        e.wait_ge(f["n_q"].sem, f["n_q"](1))
        if bias:
            v.tensor_scalar(qT, g.ps[:, 1, :], g.col(bias[0], 0), HD ** -0.5, ALU.add, ALU.mult).then_inc(f["n_q_sb"].sem, 1)
        else:
            v.tensor_copy(qT, g.ps[:, 1, :]).then_inc(f["n_q_sb"].sem, 1)
        e.wait_ge(f["n_k"].sem, f["n_k"](1))
        if bias:
            v.tensor_scalar(kT, g.ps[:, 2, :], g.col(bias[0], 1), None, ALU.add).then_inc(f["n_k_sb"].sem, 1)
        else:
            v.tensor_copy(kT, g.ps[:, 2, :]).then_inc(f["n_k_sb"].sem, 1)
        e.wait_ge(f["n_v"].sem, f["n_v"](1))
        v.tensor_copy(V, g.ps[:, 3, :].rearrange("p (t d) -> p t d", d=D)).then_inc(f["n_v_sb"].sem, 1)
        e.wait_ge(f["n_v_sb"].sem, f["n_v_sb"](1))
        core["dve"](e)
        e.wait_ge(core["out"].sem, core["out"](KG))
        v.tensor_copy(orow, g.ps[:, 4, :]).then_inc(f["n_rows"].sem, 1)
        e.wait_ge(f["n_oT"].sem, f["n_oT"](1))
        if bias:
            v.tensor_scalar(oT, g.ps[:, 5, :], g.col(bias[0], 2), None, ALU.add).then_inc(f["n_oT_sb"].sem, 1)
        else:
            v.tensor_copy(oT, g.ps[:, 5, :]).then_inc(f["n_oT_sb"].sem, 1)
        e.wait_ge(f["n_y"].sem, f["n_y"](1))
        if bias:
            v.tensor_scalar(yT, g.ps[:, 6, :], g.col(bias[1]), None, ALU.add).then_inc(f["n_yT"].sem, 1)
        else:
            v.tensor_copy(yT, g.ps[:, 6, :]).then_inc(f["n_yT"].sem, 1)
        back["dve"](e)

    def pool(e):
        start_layer(g, e, layer)
        core["pool"](e)
    return dict(load=load, sp=nothing, dve=dve, act=act, pe=pe, pool=pool)


def layer_l2_self(g):
    def load_weights(e, w, w_in):
        e.dma_start(w[:, 0:3 * P].rearrange("p (j d) -> p j d", d=D), g.a["L2_attn_qkv_w"].rearrange("(j p) d -> p j d", p=P)).then_inc(w_in.sem, 16)
        e.dma_start(w[:, 3 * P:4 * P], g.a["L2_attn_proj_w"]).then_inc(w_in.sem, 16)
    return narrow_self(g, 7, 1, load_weights, 2, g.mask_bd, ("l2a_qkvb", "l2a_pb"))


def layer_l2_quant(g):
    nc = g.nc
    tmp = g.temps()
    w = g.slot[0][:, 0:D]
    wqT = tmp.take(P, BF16)
    aqT = tmp.take(TOK, BF16)
    asum, ws, iws, sc = (tmp.take(1) for _ in range(4))
    am, ia, ys = (tmp.take(NT) for _ in range(3))
    ln1 = layernorm(g, g.x, g.xn)
    f = flags(g, l2f_w_in=16, x_done=1)
    f = steps(g, f, products="t_sum t_y", rows_ready="t_abs t_wq t_rows", rows_T="t_wqT t_aT", T_ready="t_T_sb")

    def load(e):
        wait_slot(g, e, 8)
        e.dma_start(w, g.a["L2_ffn_weight"]).then_inc(f["l2f_w_in"].sem, 16)

    def dve(e):
        v, ln = nc.vector, g.link["dve"]
        e.wait_ge(f["l2f_w_in"].sem, f["l2f_w_in"](16))
        v.tensor_reduce(asum, w, AX.X, ALU.add, apply_absolute_value=True).then_inc(f["t_abs"].sem, 1)
        e.wait_ge(f["t_sum"].sem, f["t_sum"](1))
        ln(v.tensor_scalar(ws, g.ps[:, 0, 0:1], 1.0 / (D * D), 1e-8, ALU.mult, ALU.add))
        ln(v.reciprocal(iws, ws))
        ln(v.tensor_scalar(w, w, iws, HALF_ULP, ALU.mult, ALU.add))
        ln(v.tensor_scalar(w, w, HALF_ULP, 1.0, ALU.subtract, ALU.min))
        v.tensor_scalar(w, w, -1.0, None, ALU.max).then_inc(f["t_wq"].sem, 1)
        ln1["dve"](e)
        ln(v.tensor_reduce(am, g.xn[:, :, :], AX.X, ALU.max, apply_absolute_value=True))
        ln(v.tensor_scalar(am, am, 1e-8, None, ALU.add))
        ln(v.reciprocal(ia, am))
        ln(v.tensor_scalar(ia, ia, 127.0, None, ALU.mult))
        for j in range(NT):
            i = v.tensor_scalar(g.xn[:, j, :], g.xn[:, j, :], ia[:, j:j + 1], -128.0, ALU.mult, ALU.max)
        ln(i)
        ln(v.tensor_scalar(g.xn2d, g.xn2d, 127.0, HALF_ULP, ALU.min, ALU.add))
        v.tensor_scalar(g.xn2d, g.xn2d, HALF_ULP, None, ALU.subtract).then_inc(f["t_rows"].sem, 1)
        ln(v.tensor_scalar(ys, am, ws, 1.0 / 127.0, ALU.mult, ALU.mult))
        e.wait_ge(f["t_wqT"].sem, f["t_wqT"](1))
        v.tensor_copy(wqT, g.ps[:, 1, 0:P])
        e.wait_ge(f["t_aT"].sem, f["t_aT"](1))
        v.tensor_copy(aqT, g.ps[:, 2, :]).then_inc(f["t_T_sb"].sem, 1)
        e.wait_ge(f["t_y"].sem, f["t_y"](1))
        for j in range(NT):
            i = v.scalar_tensor_tensor(out=g.x[:, j, :], in0=g.ps[:, 3, P * j:P * j + P], scalar=ys[:, j:j + 1], in1=g.x[:, j, :],
                                       op0=ALU.mult, op1=ALU.add)
        i.then_inc(f["x_done"].sem, 1)
        e.wait_ge(f["x_done"].sem, f["x_done"](1))

    def act(e):
        ln1["act"](e)

    def pe(e):
        t = nc.tensor
        e.wait_ge(f["t_abs"].sem, f["t_abs"](1))
        t.matmul(g.ps[:, 0, 0:1], g.ones, asum, start=True, stop=True).then_inc(f["t_sum"].sem, 1)
        e.wait_ge(f["t_wq"].sem, f["t_wq"](1))
        t.transpose(g.ps[:, 1, 0:P], w, g.ident).then_inc(f["t_wqT"].sem, 1)
        ln1["pe"](e)
        e.wait_ge(f["t_rows"].sem, f["t_rows"](1))
        for j in range(NT):
            i = t.transpose(g.ps[:, 2, P * j:P * j + P], g.xn[:, j, :], g.ident)
        i.then_inc(f["t_aT"].sem, 1)
        e.wait_ge(f["t_T_sb"].sem, f["t_T_sb"](1))
        for j in range(NT):
            i = t.matmul(g.ps[:, 3, P * j:P * j + P], aqT[:, P * j:P * j + P], wqT, start=True, stop=True)
        i.then_inc(f["t_y"].sem, 1)
    return dict(load=load, sp=nothing, dve=dve, act=act, pe=pe, pool=nothing)


def layer_l3_cross(g):
    nc = g.nc
    tmp = g.temps()
    H, DH, TOPK = 4, 32, 32
    REPL = -3.0e38
    NTL = 2 * B
    w = g.slot[1]
    wcols = dict(wq=(0, P, P), wk=(P, DC, P), wv=(2 * P, DC, P), wfi=(3 * P, P, 2 * P), wfo=(5 * P, P, 2 * P), w1=(7 * P, P, 512), w2=(7 * P + 512, P, 512))
    wq, wk, wv, wfi, wfo, w1, w2 = (w[0:r, a:a + n] for a, r, n in wcols.values())
    w2 = w2.rearrange("p (c d) -> p c d", d=D)
    pre = Arena(g.pre, 4096)
    Gm = pre.take(H * DC)
    qh = pre.take(B * H * S, BF16)[0:DC, :].rearrange("p (b h q) -> p b h q", b=B, h=H)
    ql = pre.take(B * H * S, BF16)[0:DC, :].rearrange("p (b h q) -> p b h q", b=B, h=H)
    aTh = pre.take(NCH * S, BF16)
    aTl = pre.take(NCH * S, BF16)
    xiT = pre.take(TOK)
    wT = pre.take(2 * P)
    sc = [tmp.take(NK) for _ in range(2)]
    work = [tmp.take(NK) for _ in range(2)]
    spare = Arena(g.slot[0][:, 4 * P:4096], 4096 - 4 * P)
    at = [tmp.take(NK), tmp.take(NK), spare.take(NK), spare.take(NK)]
    top = [tmp.take(TOPK) for _ in range(2)]
    ex = [tmp.take(TOPK) for _ in range(2)]
    nm, z, zi = ([tmp.take(1) for _ in range(2)] for _ in range(3))
    sel = [tmp.take(S) for _ in range(4)]
    c1, ctT = tmp.take(TOK), tmp.take(TOK)
    late = g.temps()
    m1, b1_, m2, b2_, y, xt, hT, yT = (late.take(TOK) for _ in range(8))
    rows = late.take(NT * P).rearrange("p (t d) -> p t d", d=D)
    h1 = late.take(4 * TOK)
    SB = g.ps[:, 0:4, :].rearrange("p a n -> p (a n)")
    AT = g.ps[:, 4:6, :].rearrange("p a n -> p (a n)")
    ln1 = layernorm(g, g.x, g.xn, out_T=g.xnT)
    xin = work[0][:, 0:TOK].rearrange("p (t d) -> p t d", d=D)
    ln2 = layernorm(g, g.xn, xin, out_T=xiT, gain=g.col("l3x_gi"), shift=g.col("l3x_bi"))
    ln3 = layernorm(g, rows, rows, out_T=hT, gain=g.col("l3x_gf"), shift=g.col("l3x_bf"))
    ln4 = layernorm(g, rows, rows)
    f = flags(g, n_w_in1=112, k_scores=NTL, k_copied=NTL, k_lo=1, k_max=NTL, k_top=NTL, k_exp=NTL, k_att=NTL, k_sel=NTL, k_aT=B, k_aT_hi=B,
              k_aT_lo=B, k_c1=B, x_done=1)
    f = steps(g, f, rows_T="k_wT k_xtT k_x2T", products="k_G k_qk k_ct k_film k_h0 k_h1 k_h2 k_h3 k_y", T_ready="k_wT_sb k_rows k_rows2",
          dve_step="k_G_sb k_qlo k_c1_sb k_ct_sb k_xt k_xt2", act_step="k_qhi k_gelu")
    w_in = f["n_w_in1"]

    def load(e):
        wait_slot(g, e, 9)
        for dst, name in ((wq, "Wq"), (wk, "Wk"), (wv, "Wv"), (wfi, "W_film_in"), (wfo, "W_film_out"), (w1, "W1")):
            e.dma_start(dst, g.a["L3_xattn_" + name]).then_inc(w_in.sem, 16)
        e.dma_start(w2, g.a["L3_xattn_W2"].rearrange("(c p) d -> p c d", p=P)).then_inc(w_in.sem, 16)

    def pe(e):
        t = nc.tensor
        start_layer(g, e, 9)
        e.wait_ge(w_in.sem, w_in(112))
        t.transpose(g.ps[:, 4, 0:P], wq, g.ident)
        t.transpose(g.ps[:, 4, P:P + DC], wk, g.ident[0:DC, 0:DC]).then_inc(f["k_wT"].sem, 1)
        e.wait_ge(f["k_wT_sb"].sem, f["k_wT_sb"](1))
        for h in range(H):
            r = slice(DH * h, DH * h + DH)
            i = t.matmul(g.ps[:, h, 0:DC], wT[r, 0:P], wT[r, P:P + DC], start=True, stop=True)
        i.then_inc(f["k_G"].sem, 1)
        ln1["pe"](e)
        ln2["pe"](e)
        e.wait_ge(ln1["ready"].sem, ln1["ready"](1))
        e.wait_ge(f["k_G_sb"].sem, f["k_G_sb"](1))
        for h in range(H):
            i = t.matmul(g.ps[0:DC, h, :], Gm[:, DC * h:DC * h + DC], g.xnT, start=True, stop=True)
        i.then_inc(f["k_qk"].sem, 1)
        e.wait_ge(f["k_qlo"].sem, f["k_qlo"](1))

        def attend_T(b):
            e.wait_ge(f["k_sel"].sem, f["k_sel"](2 * b + 2))
            e.wait_ge(f["k_att"].sem, f["k_att"](2 * b + 2))
            if b >= 1:
                e.wait_ge(f["k_aT_lo"].sem, f["k_aT_lo"](b))
            for c in range(NCH):
                n = P if c < FULL else LASTK
                for j in range(2):
                    q = (2 * b + j) % 4
                    i = t.matmul(AT[0:n, S * c:S * c + S], at[q][:, P * c:P * c + n], sel[q], start=j == 0, stop=j == 1)
            i.then_inc(f["k_aT"].sem, 1)

        def attend_V(b):
            e.wait_ge(f["k_aT_lo"].sem, f["k_aT_lo"](b + 1))
            for c in range(NCH):
                n = P if c < FULL else LASTK
                for j, (lhs, rhs) in enumerate(((g.cr_hi, aTh), (g.cr_lo, aTh), (g.cr_hi, aTl))):
                    i = t.matmul(g.ps[0:DC, 6, S * b:S * b + S], lhs[0:n, b, c, 0:DC], rhs[0:n, S * c:S * c + S],
                                 start=c == 0 and j == 0, stop=c == NCH - 1 and j == 2)
            i.then_inc(f["k_c1"].sem, 1)

        for k in range(NTL):
            b, j = divmod(k, 2)
            if k >= 1:
                e.wait_ge(f["k_copied"].sem, f["k_copied"](k))
            for a, n in KSPAN:
                q_hi = qh[:, b, 2 * j:2 * j + 2, :].rearrange("p h q -> p (h q)")
                q_lo = ql[:, b, 2 * j:2 * j + 2, :].rearrange("p h q -> p (h q)")
                t.matmul(SB[:, a:a + n], q_hi, g.cT_hi[0:DC, b, a:a + n], start=True, stop=False)
                t.matmul(SB[:, a:a + n], q_lo, g.cT_hi[0:DC, b, a:a + n], start=False, stop=False)
                t.matmul(SB[:, a:a + n], q_hi, g.cT_lo[0:DC, b, a:a + n], start=False, stop=False)
                i = t.matmul(SB[:, a:a + n], g.sel[:, b, :], g.kmask[0:8, 1, a:a + n], start=False, stop=True)
            i.then_inc(f["k_scores"].sem, 1)
            if j == 1 and b >= 1:
                attend_T(b - 1)
            if j == 0 and b >= 2:
                attend_V(b - 2)
        attend_V(B - 2)
        attend_T(B - 1)
        attend_V(B - 1)
        e.wait_ge(f["k_c1_sb"].sem, f["k_c1_sb"](1))
        t.matmul(g.ps[:, 7, :], wv, c1[0:DC, :], start=True, stop=True).then_inc(f["k_ct"].sem, 1)
        e.wait_ge(f["k_ct_sb"].sem, f["k_ct_sb"](1))
        for i_, (wf, half) in enumerate(((wfi, 0), (wfi, 1), (wfo, 0), (wfo, 1))):
            i = t.matmul(g.ps[:, i_, :], wf[:, P * half:P * half + P], ctT, start=True, stop=True)
        i.then_inc(f["k_film"].sem, 1)
        e.wait_ge(f["k_xt"].sem, f["k_xt"](1))
        for j in range(NT):
            i = t.transpose(g.ps[:, 4, P * j:P * j + P], xt[:, P * j:P * j + P], g.ident)
        i.then_inc(f["k_xtT"].sem, 1)
        ln3["pe"](e)
        e.wait_ge(ln3["ready"].sem, ln3["ready"](1))
        for c, flag in enumerate((f["k_h0"], f["k_h1"], f["k_h2"], f["k_h3"])):
            t.matmul(g.ps[:, c, :], w1[:, P * c:P * c + P], hT, start=True, stop=True).then_inc(flag.sem, 1)
        e.wait_ge(f["k_gelu"].sem, f["k_gelu"](1))
        for c in range(4):
            i = t.matmul(g.ps[:, 5, :], w2[:, c, :], h1[:, TOK * c:TOK * c + TOK], start=c == 0, stop=c == 3)
        i.then_inc(f["k_y"].sem, 1)
        e.wait_ge(f["k_xt2"].sem, f["k_xt2"](1))
        for j in range(NT):
            i = t.transpose(g.ps[:, 6, P * j:P * j + P], yT[:, P * j:P * j + P], g.ident)
        i.then_inc(f["k_x2T"].sem, 1)

    def act(e):
        s, ln = nc.scalar, g.link["act"]
        start_layer(g, e, 9)
        ln1["act"](e)
        ln2["act"](e)
        e.wait_ge(f["k_qk"].sem, f["k_qk"](1))
        for h in range(H):
            i = s.activation(qh[:, :, h, :], g.ps[0:DC, h, :].rearrange("p (b q) -> p b q", b=B), ACT.Copy)
        i.then_inc(f["k_qhi"].sem, 1)

        def copy(k):
            e.wait_ge(f["k_scores"].sem, f["k_scores"](k + 1))
            if k >= 2:
                e.wait_ge(f["k_exp"].sem, f["k_exp"](k - 1))
                e.wait_ge(f["k_max"].sem, f["k_max"](k - 1))
            s.activation(sc[k % 2], SB[:, 0:NK], ACT.Copy).then_inc(f["k_copied"].sem, 1)

        def aT_high(b):
            e.wait_ge(f["k_aT"].sem, f["k_aT"](b + 1))
            if b >= 1:
                e.wait_ge(f["k_c1"].sem, f["k_c1"](b))
            s.activation(aTh[:, 0:FULL * S], AT[:, 0:FULL * S], ACT.Copy)
            s.activation(aTh[0:LASTK, FULL * S:NCH * S], AT[0:LASTK, FULL * S:NCH * S], ACT.Copy).then_inc(f["k_aT_hi"].sem, 1)

        copy(0)
        for k in range(NTL):
            b, j = divmod(k, 2)
            if j == 1 and b >= 1:
                aT_high(b - 1)
            if k + 1 < NTL:
                copy(k + 1)
            e.wait_ge(f["k_top"].sem, f["k_top"](k + 1))
            if b >= 2:
                e.wait_ge(f["k_aT"].sem, f["k_aT"](b - 1))
            if k >= 2:
                e.wait_ge(f["k_exp"].sem, f["k_exp"](k - 1))
            s.activation(ex[k % 2], top[k % 2], ACT.Exp, bias=nm[k % 2], accum_out=z[k % 2])
            s.activation(at[k % 4], sc[k % 2], ACT.Exp, bias=nm[k % 2])
            s.activation(work[k % 2], work[k % 2], ACT.Exp, bias=nm[k % 2]).then_inc(f["k_exp"].sem, 1)
        aT_high(B - 1)
        ln3["act"](e)
        for c, flag in enumerate((f["k_h0"], f["k_h1"], f["k_h2"], f["k_h3"])):
            e.wait_ge(flag.sem, flag(1))
            i = s.activation(h1[:, TOK * c:TOK * c + TOK], g.ps[:, c, :], ACT.Gelu, bias=g.col("l3x_b1", c))
        i.then_inc(f["k_gelu"].sem, 1)
        table(g)
        ln4["act"](e)

    def dve(e):
        v, ln = nc.vector, g.link["dve"]
        e.wait_ge(f["k_wT"].sem, f["k_wT"](1))
        v.tensor_copy(wT[:, 0:P + DC], g.ps[:, 4, 0:P + DC]).then_inc(f["k_wT_sb"].sem, 1)
        e.wait_ge(f["k_G"].sem, f["k_G"](1))
        for h in range(H):
            i = v.tensor_scalar(Gm[:, DC * h:DC * h + DC], g.ps[:, h, 0:DC], DH ** -0.5, None, ALU.mult)
        i.then_inc(f["k_G_sb"].sem, 1)
        ln1["dve"](e)
        ln2["dve"](e)
        e.wait_ge(f["k_qhi"].sem, f["k_qhi"](1))
        for h in range(H):
            i = v.tensor_tensor(ql[:, :, h, :], g.ps[0:DC, h, :].rearrange("p (b q) -> p b q", b=B), qh[:, :, h, :], ALU.subtract)
        i.then_inc(f["k_qlo"].sem, 1)

        def lows(b):
            e.wait_ge(f["k_aT_hi"].sem, f["k_aT_hi"](b + 1))
            v.tensor_tensor(aTl[:, 0:FULL * S], AT[:, 0:FULL * S], aTh[:, 0:FULL * S], ALU.subtract)
            v.tensor_tensor(aTl[0:LASTK, FULL * S:NCH * S], AT[0:LASTK, FULL * S:NCH * S], aTh[0:LASTK, FULL * S:NCH * S],
                            ALU.subtract).then_inc(f["k_aT_lo"].sem, 1)

        def finish(k):
            e.wait_ge(f["k_exp"].sem, f["k_exp"](k + 1))
            ln(v.reciprocal(zi[k % 2], z[k % 2]))
            if k >= 4:
                e.wait_ge(f["k_aT"].sem, f["k_aT"](k // 2 - 1))
            v.tensor_scalar(sel[k % 4], g.fold, zi[k % 2], 1.0 / H, ALU.mult, ALU.mult).then_inc(f["k_sel"].sem, 1)

        for k in range(NTL):
            b, j = divmod(k, 2)
            left, tops = work[k % 2], top[k % 2]
            e.wait_ge(f["k_copied"].sem, f["k_copied"](k + 1))
            if k >= 2:
                e.wait_ge(f["k_att"].sem, f["k_att"](k - 1))
            for r in range(TOPK // 8):
                src = sc[k % 2] if r == 0 else left
                ln(v.max(out=tops[:, 8 * r:8 * r + 8], in_=src))
                i = v.match_replace(out=left, in_to_replace=tops[:, 8 * r:8 * r + 8], in_values=src, imm_value=REPL)
                if r == 0:
                    i.then_inc(f["k_max"].sem, 1)
                    e.wait_ge(f["k_max"].sem, f["k_max"](k + 1))
                else:
                    ln(i)
            v.tensor_scalar(nm[k % 2], tops[:, 0:1], -1.0, None, ALU.mult).then_inc(f["k_top"].sem, 1)
            if k >= 1:
                finish(k - 1)
            if j == 1 and b >= 1:
                lows(b - 1)
        finish(NTL - 1)
        lows(B - 1)
        e.wait_ge(f["k_c1"].sem, f["k_c1"](B))
        v.tensor_copy(c1[0:DC, :], g.ps[0:DC, 6, :]).then_inc(f["k_c1_sb"].sem, 1)
        e.wait_ge(f["k_ct"].sem, f["k_ct"](1))
        v.tensor_tensor(ctT, g.ps[:, 7, :], g.tmask, ALU.mult).then_inc(f["k_ct_sb"].sem, 1)
        e.wait_ge(f["k_film"].sem, f["k_film"](1))
        gate = g.scal[:, 24:25]
        for i_, (dst, name, half) in enumerate(((m1, "l3x_bfi", 0), (b1_, "l3x_bfi", 1), (m2, "l3x_bfo", 0), (b2_, "l3x_bfo", 1))):
            i = v.tensor_scalar(dst, g.ps[:, i_, :], g.col(name, half), gate, ALU.add, ALU.mult)
        ln(i)
        v.tensor_scalar(m1, m1, 1.0, None, ALU.add)
        ln(v.tensor_scalar(m2, m2, 1.0, None, ALU.add))
        ln(v.tensor_tensor(xiT, xiT, m1, ALU.mult))
        ln(v.tensor_tensor(xiT, xiT, b1_, ALU.add))
        ln(v.tensor_scalar(y, xiT, g.s4k[:, 0:1], None, ALU.mult))
        xv, yv = (a.rearrange("p (b s) -> p b s", b=B) for a in (xiT, y))
        for j in range(1, S):
            ln(v.scalar_tensor_tensor(out=yv[:, :, j:S], in0=xv[:, :, 0:S - j], scalar=g.s4k[:, j:j + 1], in1=yv[:, :, j:S],
                                      op0=ALU.mult, op1=ALU.add))
        ln(v.tensor_tensor(y, y, m2, ALU.mult))
        ln(v.tensor_tensor(y, y, b2_, ALU.add))
        v.tensor_tensor(xt, y, g.xnT, ALU.add).then_inc(f["k_xt"].sem, 1)
        e.wait_ge(f["k_xtT"].sem, f["k_xtT"](1))
        v.tensor_copy(rows, g.ps[:, 4, :].rearrange("p (t d) -> p t d", d=D)).then_inc(f["k_rows"].sem, 1)
        e.wait_ge(f["k_rows"].sem, f["k_rows"](1))
        ln3["dve"](e)
        e.wait_ge(f["k_y"].sem, f["k_y"](1))
        v.scalar_tensor_tensor(out=yT, in0=g.ps[:, 5, :], scalar=g.col("l3x_b2"), in1=xt, op0=ALU.add, op1=ALU.add).then_inc(f["k_xt2"].sem, 1)
        e.wait_ge(f["k_x2T"].sem, f["k_x2T"](1))
        v.tensor_copy(rows, g.ps[:, 6, :].rearrange("p (t d) -> p t d", d=D)).then_inc(f["k_rows2"].sem, 1)
        e.wait_ge(f["k_rows2"].sem, f["k_rows2"](1))
        ln4["dve"](e)
        for j in range(NT):
            i = v.tensor_tensor(rows[:, j, :], rows[:, j, :], g.bcv["l3x_go"], ALU.mult)
        ln(i)
        for j in range(NT):
            i = v.tensor_tensor(rows[:, j, :], rows[:, j, :], g.bcv["l3x_bo"], ALU.add)
        ln(i)
        v.tensor_tensor(g.x[:, :, :], g.x[:, :, :], rows, ALU.add).then_inc(f["x_done"].sem, 1)
        e.wait_ge(f["x_done"].sem, f["x_done"](1))

    def pool(e):
        start_layer(g, e, 9)
        for k in range(NTL):
            e.wait_ge(f["k_exp"].sem, f["k_exp"](k + 1))
            nc.gpsimd.tensor_tensor(at[k % 4], at[k % 4], work[k % 2], ALU.subtract).then_inc(f["k_att"].sem, 1)
    return dict(load=load, sp=nothing, dve=dve, act=act, pe=pe, pool=pool)


def layer_l3_self(g):
    def load_weights(e, w, w_in):
        for i, name in enumerate(("Wq", "Wk", "Wv", "Wo")):
            e.dma_start(w[:, P * i:P * i + P], g.a["L3_attn_" + name]).then_inc(w_in.sem, 16)
    return narrow_self(g, 10, 0, load_weights, 4, None, None)


def layer_l3_moe(g):
    nc = g.nc
    tmp = g.temps()
    E, FC = 8, 4
    K = E * FC
    EW = 2 * 512
    place = [g.slot[1], g.slot[0]]
    wr = tmp.take(E)
    hb = [tmp.take(TOK) for _ in range(8)]
    acc = tmp.take(NT * P).rearrange("p (t d) -> p t d", d=D)
    lg, ga, se, ew, wt = (tmp.take(NT * E).rearrange("p (t e) -> p t e", e=E) for _ in range(5))
    pair = tmp.take(NT * E * E).rearrange("p (t a b) -> p t a b", t=NT, a=E)
    eq = tmp.take(NT * E * E).rearrange("p (t a b) -> p t a b", t=NT, a=E)
    mx, zs, zi = (tmp.take(NT) for _ in range(3))
    wTt = tmp.take(TOK)
    ln1 = layernorm(g, g.x, g.xn, out_T=g.xnT)
    f = flags(g, e_w_in0=144, e_w_in1=128, m_gate=K, m_act=K, m_y=E, m_acc=E, x_done=1)
    f = steps(g, f, products="r_logits r_b2", dve_step="r_shift r_weights r_wT_sb", rows_T="r_wT", act_step="r_exp")
    arrived, total = [f["e_w_in0"], f["e_w_in1"]], [144, 128]

    def views(x):
        w = place[x // 4][:, EW * (x % 4):EW * (x % 4) + EW]
        return w[:, 0:512], w[:, 512:1024].rearrange("p (c d) -> p c d", d=D)

    def load_four(e, p):
        for x in range(4 * p, 4 * p + 4):
            w1, w2 = views(x)
            e.dma_start(w1, g.a["L3_ffn_W1"][x]).then_inc(arrived[p].sem, 16)
            e.dma_start(w2, g.a["L3_ffn_W2"][x].rearrange("(c p) d -> p c d", p=P)).then_inc(arrived[p].sem, 16)

    def load(e):
        wait_slot(g, e, 11)
        load_four(e, 0)

    def sp(e):
        start_layer(g, e, 11)
        e.dma_start(wr, g.a["L3_ffn_W_router"]).then_inc(f["e_w_in0"].sem, 16)
        load_four(e, 1)

    def pe(e):
        t = nc.tensor
        ln1["pe"](e)
        e.wait_ge(ln1["ready"].sem, ln1["ready"](1))
        e.wait_ge(f["e_w_in0"].sem, f["e_w_in0"](144))
        for j in range(NT):
            i = t.matmul(g.ps[:, 4, E * j:E * j + E], g.xnT[:, P * j:P * j + P], wr, start=True, stop=True)
        i.then_inc(f["r_logits"].sem, 1)

        def up(k):
            x, c = divmod(k, FC)
            if k == K // 2:
                e.wait_ge(f["e_w_in1"].sem, f["e_w_in1"](128))
            if k >= 2:
                e.wait_ge(f["m_act"].sem, f["m_act"](k - 1))
            t.matmul(g.ps[:, k % 2, :], views(x)[0][:, P * c:P * c + P], g.xnT, start=True, stop=True).then_inc(f["m_gate"].sem, 1)

        for c in range(FC):
            up(c)
        e.wait_ge(f["r_weights"].sem, f["r_weights"](1))
        for j in range(NT):
            i = t.transpose(g.ps[0:E, 5, P * j:P * j + P], wt[:, j, :], g.ident)
        i.then_inc(f["r_wT"].sem, 1)
        e.wait_ge(f["r_wT_sb"].sem, f["r_wT_sb"](1))
        for j in range(NT):
            i = t.matmul(g.ps[:, 6, P * j:P * j + P], wTt[0:E, P * j:P * j + P], g.b2moe[0:E, :], start=True, stop=True)
        i.then_inc(f["r_b2"].sem, 1)
        for x in range(E):
            if x + 1 < E:
                for c in range(FC):
                    up(FC * (x + 1) + c)
            e.wait_ge(f["m_act"].sem, f["m_act"](FC * (x + 1)))
            if x >= 2:
                e.wait_ge(f["m_acc"].sem, f["m_acc"](x - 1))
            for j in range(NT):
                for c in range(FC):
                    i = t.matmul(g.ps[:, 2 + x % 2, P * j:P * j + P], hb[(FC * x + c) % 8][:, P * j:P * j + P], views(x)[1][:, c, :],
                                 start=c == 0, stop=c == FC - 1)
            i.then_inc(f["m_y"].sem, 1)

    def act(e):
        s = nc.scalar
        start_layer(g, e, 11)
        ln1["act"](e)

        def relu(k):
            x, c = divmod(k, FC)
            e.wait_ge(f["m_gate"].sem, f["m_gate"](k + 1))
            if x >= 2:
                e.wait_ge(f["m_y"].sem, f["m_y"](x - 1))
            s.activation(hb[k % 8], g.ps[:, k % 2, :], ACT.Relu, bias=g.moe_b1(x, c)).then_inc(f["m_act"].sem, 1)
        e.wait_ge(f["r_shift"].sem, f["r_shift"](1))
        s.activation(ew, ga, ACT.Exp).then_inc(f["r_exp"].sem, 1)
        for k in range(K):
            relu(k)

    def dve(e):
        v, ln = nc.vector, g.link["dve"]
        ln1["dve"](e)
        e.wait_ge(f["r_logits"].sem, f["r_logits"](1))
        ln(v.tensor_tensor(lg, g.ps[:, 4, 0:NT * E].rearrange("p (t e) -> p t e", e=E),
                           g.scal[:, None, 16:24].to_broadcast([P, NT, E]), ALU.add))
        ln(v.tensor_reduce(mx, lg, AX.X, ALU.max))
        v.tensor_tensor(ga, lg, mx[:, :, None].to_broadcast([P, NT, E]), ALU.subtract).then_inc(f["r_shift"].sem, 1)
        A4 = [P, NT, E, E]
        va, vb = lg[:, :, :, None].to_broadcast(A4), lg[:, :, None, :].to_broadcast(A4)
        v.tensor_tensor(pair, vb, va, ALU.is_gt)
        ln(v.tensor_tensor(eq, vb, va, ALU.is_equal))
        ln(v.tensor_tensor(eq, eq, g.before[:, None, :, :].to_broadcast(A4), ALU.mult))
        ln(v.tensor_tensor(pair, pair, eq, ALU.add))
        ln(v.tensor_reduce(se, pair, AX.X, ALU.add))
        ln(v.tensor_scalar(se, se, 2.0, None, ALU.is_lt))
        e.wait_ge(f["r_exp"].sem, f["r_exp"](1))
        ln(v.tensor_tensor(ew, ew, se, ALU.mult))
        ln(v.tensor_reduce(zs, ew, AX.X, ALU.add))
        ln(v.reciprocal(zi, zs))
        v.tensor_tensor(wt, ew, zi[:, :, None].to_broadcast([P, NT, E]), ALU.mult).then_inc(f["r_weights"].sem, 1)
        e.wait_ge(f["r_wT"].sem, f["r_wT"](1))
        v.tensor_copy(wTt[0:E, :], g.ps[0:E, 5, :]).then_inc(f["r_wT_sb"].sem, 1)
        e.wait_ge(f["r_b2"].sem, f["r_b2"](1))
        ln(v.tensor_tensor(acc, g.x[:, :, :], g.ps[:, 6, :].rearrange("p (t d) -> p t d", d=D), ALU.add))
        for x in range(E):
            e.wait_ge(f["m_y"].sem, f["m_y"](x + 1))
            for j in range(NT):
                i = v.scalar_tensor_tensor(out=acc[:, j, :], in0=g.ps[:, 2 + x % 2, P * j:P * j + P], scalar=wt[:, j, x:x + 1],
                                           in1=acc[:, j, :], op0=ALU.mult, op1=ALU.add)
            i.then_inc(f["m_acc"].sem, 1)
            e.wait_ge(f["m_acc"].sem, f["m_acc"](x + 1))
        v.tensor_copy(g.x[:, :, :], acc).then_inc(f["x_done"].sem, 1)
    return dict(own_loads_first=True, load=load, sp=sp, dve=dve, act=act, pe=pe, pool=nothing)


LAYERS = [layer_l0_cross,layer_l0_cosine,layer_l0_quant_ffn,layer_l1_cross,layer_l1_self,layer_l1_moe,layer_l2_cross,layer_l2_self,layer_l2_quant,layer_l3_cross,layer_l3_self,layer_l3_moe]
ROOM = 11300


def build(nc, args, out, layers=12):
    g = G()
    g.nc, g.a = nc, args
    with ExitStack() as ctx:
        def sb(name, shape, dt=F32):
            return ctx.enter_context(nc.sbuf_tensor(name, shape, dt))

        g.new_sem = lambda name: ctx.enter_context(nc.semaphore(name))
        g.flag = {}
        g.x = sb("x_rows", [P, NT, D])
        g.x2d = g.x[:, :, :].rearrange("p t d -> p (t d)")
        g.cT_hi = sb("ctxT_hi", [P, B, NK], BF16)
        g.cT_lo = sb("ctxT_lo", [P, B, NK], BF16)
        g.cr_hi = sb("ctx_hi", [P, B, NCH, DC + 1], BF16)
        g.cr_lo = sb("ctx_lo", [P, B, NCH, DC + 1], BF16)
        slots = sb("weight_slots", [P, 2, 4096])
        g.slot = [slots[:, i, :] for i in range(2)]
        g.vrows = sb("vector_rows", [P, P])[:, :]
        g.vcols = sb("vector_cols", [P, P])[:, :]
        g.bc = sb("row_vectors", [P, len(BCAST), D])
        g.bcv = {name: g.bc[:, i, :] for i, (name, _) in enumerate(BCAST)}
        g.scal = sb("scalars", [P, 64])[:, :]
        g.tmask8 = sb("token_mask_bytes", [P, TOK], U8)[:, :]
        g.tmask = sb("token_mask", [P, TOK], BF16)[:, :]
        g.kmask = sb("key_mask_terms", [8, 2, NK], BF16)
        g.b2moe = sb("moe_b2", [8, D])
        g.ident = sb("ident", [P, P])[:, :]
        g.ones = sb("ones", [P, P])[:, :]
        g.blk = sb("blk", [P, P])[:, :]
        g.mask_bd = sb("mask_bd", [P, P])[:, :]
        g.mask_ca = sb("mask_ca", [P, P])[:, :]
        g.tri_mul = sb("tri_mul", [P, P])[:, :]
        g.tri_add = sb("tri_add", [P, P])[:, :]
        g.neg_blk = sb("neg_blk", [P, P])[:, :]
        g.head_of = sb("head_of", [P, 16])[:, :]
        g.fold = sb("fold", [P, 64])[:, :]
        g.st = sb("st", [P, 6 * NT])[:, :]
        g.mv = sb("mv", [P, 2 * NT])[:, :]
        g.ve = sb("ve", [P, NT])[:, :]
        g.sd = sb("sd", [P, NT])[:, :]
        g.rstd = sb("rstd", [P, NT])[:, :]
        g.xnT = sb("xnT", [P, TOK])[:, :]
        g.sel = sb("sel", [8, B, P], BF16)[:, :, :]
        g.before = sb("before", [P, 8, 8])[:, :, :]
        g.xn = sb("x_normed", [P, NT, D])
        g.xn2d = g.xn[:, :, :].rearrange("p t d -> p (t d)")
        g.s4in = sb("s4d_in", [P, 4 * S])[:, :]
        g.s4k = sb("s4d_kernel", [P, S])[:, :]
        g.s4dt = sb("s4d_dt", [P, 1])[:, :]
        g.s4_sem = g.new_sem("s4d_in_loaded")
        g.half = sb("half", [P, 1])[:, :]
        g.pre = sb("folded_weights", [P, 4096])[:, :]
        g.ps = ctx.enter_context(nc.psum_tensor("banks", [P, 8, BANK], F32))
        room = sb("temporaries", [P, ROOM])
        early = Arena(g.slot[0][:, 8 * P:4096], 4096 - 8 * P)
        g.m8 = early.take((2 * NK + 3) // 4).bitcast(U8)[0:8, 0:2 * NK].rearrange("p (m k) -> p m k", m=2)
        g.mtmp = early.take(2 * NK, BF16)[0:8, :].rearrange("p (m k) -> p m k", m=2)
        g.temps = lambda: Arena(room, ROOM)
        chain = {n: g.new_sem(n + "_order") for n in ("dve", "act", "pool")}
        g.link = {}
        out_done = g.new_sem("out_done")

        stages = [stage_setup(g)] + [LAYERS[i](g) for i in range(layers)]

        with nc.Block() as block:
            @block.sync
            def _(sp):
                stages[0]["first"](sp)
                stages[1]["load"](sp)
                stages[1]["early"](sp)
                stages[0]["sp"](sp)
                for i in range(1, len(stages)):
                    if "own_loads_first" in stages[i]:
                        stages[i]["sp"](sp)
                    if i + 1 < len(stages):
                        stages[i + 1]["load"](sp)
                    if "own_loads_first" not in stages[i]:
                        stages[i]["sp"](sp)
                sp.wait_ge(g.flag["x_done"].sem, layers)
                sp.dma_start(out.rearrange("b s d -> (b s) d").rearrange("(t p) d -> p t d", p=P), g.x[:, :, :]).then_inc(out_done, 16)
                sp.wait_ge(out_done, 16)

            @block.tensor
            def _(pe):
                for s in stages:
                    s["pe"](pe)

            @block.scalar
            def _(act):
                g.link["act"] = Link(act, chain["act"])
                for i, s in enumerate(stages):
                    if i > 3:
                        table(g)
                    s["act"](act)

            @block.vector
            def _(dve):
                g.link["dve"] = Link(dve, chain["dve"])
                for s in stages:
                    s["dve"](dve)

            @block.gpsimd
            def _(pool):
                g.link["pool"] = Link(pool, chain["pool"])
                for s in stages:
                    s["pool"](pool)


def kernel(**inputs):
    import numpy as _np
    import concourse.bacc as _bacc
    from concourse import mybir as _mybir
    from concourse.bass_utils import run_bass_kernel_spmd as _run

    nc = _bacc.Bacc("TRN2", target_bir_lowering=False, num_devices=1)
    arrays, args = {}, {}
    for name in inputs:
        a = _np.ascontiguousarray(inputs[name])
        a = a.reshape(inputs[name].shape or (1,))
        if a.dtype == _np.bool_:
            words = a.reshape(-1).view(_np.int32)
            ap = nc.dram_tensor(f"in_{name}", words.shape, _mybir.dt.from_np(words.dtype), kind="ExternalInput").ap()
            arrays[f"in_{name}"] = words
            args[name] = ap.bitcast(U8).rearrange("(b s) -> b s", b=B)
        else:
            arrays[f"in_{name}"] = a
            args[name] = nc.dram_tensor(f"in_{name}", a.shape, _mybir.dt.from_np(a.dtype), kind="ExternalInput").ap()
    out = nc.dram_tensor("out", (B, S, D), F32, kind="ExternalOutput").ap()
    build(nc, args, out)
    r = _run(nc, [arrays], core_ids=[0])
    return r.results[0]["out"]
```
